# Optimizing a Trainium2 kernel written in Bass

```python
import numpy as np
import jax
import jax.numpy as jnp

def _softmax(x, axis=-1):
    return jax.nn.softmax(x, axis=axis)

def _gelu(x):
    return jax.nn.gelu(x, approximate=True)

def _silu(x):
    return jax.nn.silu(x)

def _sigmoid(x):
    return jax.nn.sigmoid(x)

def _layernorm(x, axis=-1, eps=1e-05):
    m = jnp.mean(x, axis=axis, keepdims=True)
    v = jnp.var(x, axis=axis, keepdims=True)
    return (x - m) / jnp.sqrt(v + eps)

def _scatter_add(tgt, idx, src, axis=0):
    return tgt.at[idx].add(src)

def _segment_sum(src, seg, n):
    return jax.ops.segment_sum(src, seg, n)
kernel_name = 'mk_gnn_preln_d4_gnn_r8_89e4c9'

def setup_inputs(seed: int=0):
    np.random.seed(seed)
    _w = jnp.asarray

    def _rec_inputs():
        import jax
        import jax.numpy as jnp
        _gk = jax.random.key(seed)
        x = -0.0005207 + 1.001 * jax.random.normal(jax.random.fold_in(_gk, 1), (512, 512), jnp.float32)
        _s = jax.random.randint(jax.random.fold_in(_gk, 2), (4096,), 0, 512, jnp.int32)
        _d = jax.random.randint(jax.random.fold_in(_gk, 3), (4096,), 0, 512, jnp.int32)
        _loop = jnp.arange(512, dtype=jnp.int32)
        src = jnp.concatenate([_s, _d, _loop])
        dst = jnp.concatenate([_d, _s, _loop])
        _o = jnp.argsort(dst, stable=True)
        src = src[_o]
        dst = dst[_o]
        edge_attr_64 = 0.000279952 + 1.00013 * jax.random.normal(jax.random.fold_in(_gk, 11), (8704, 64), jnp.float32)
        return (x, src, dst, edge_attr_64)
    x, src, dst, edge_attr_64 = _rec_inputs()

    def _L0_gnn_setup():
        import jax, jax.numpy as jnp
        import numpy as np
        N, E = (512, 16384)
        D_IN, D_OUT, H = (512, 512, 8)
        HEAD = D_OUT // H
        EPS = 1e-05

        def _layer_norm(x, g, b):
            m = jnp.mean(x, axis=-1, keepdims=True)
            v = jnp.mean(jnp.square(x - m), axis=-1, keepdims=True)
            return (x - m) * jax.lax.rsqrt(v + EPS) * g + b
        key = jax.random.key(seed)
        ks = jax.random.split(key, 16)
        s = 1.0 / np.sqrt(D_OUT)
        inp = {'x': jax.random.normal(ks[0], (N, D_IN), dtype=jnp.float32), 'edge_index': jax.random.randint(ks[1], (2, E), 0, N, dtype=jnp.int64), 'Wq': jax.random.normal(ks[2], (D_OUT, D_OUT), jnp.float32) * s, 'bq': jnp.zeros((D_OUT,), jnp.float32), 'Wk': jax.random.normal(ks[3], (D_OUT, D_OUT), jnp.float32) * s, 'bk': jnp.zeros((D_OUT,), jnp.float32), 'Wv': jax.random.normal(ks[4], (D_OUT, D_OUT), jnp.float32) * s, 'bv': jnp.zeros((D_OUT,), jnp.float32), 'Wo': jax.random.normal(ks[5], (D_OUT, D_OUT), jnp.float32) * s, 'bo': jnp.zeros((D_OUT,), jnp.float32), 'W1': jax.random.normal(ks[6], (D_OUT, 2 * D_OUT), jnp.float32) * s, 'b1': jnp.zeros((2 * D_OUT,), jnp.float32), 'W2': jax.random.normal(ks[7], (2 * D_OUT, D_OUT), jnp.float32) * (1.0 / np.sqrt(2 * D_OUT)), 'b2': jnp.zeros((D_OUT,), jnp.float32), 'g1': jnp.ones((D_OUT,), jnp.float32), 'be1': jnp.zeros((D_OUT,), jnp.float32), 'g2': jnp.ones((D_OUT,), jnp.float32), 'be2': jnp.zeros((D_OUT,), jnp.float32)}
        return inp
    _L0_gnn_all = _L0_gnn_setup()
    _L0_gnn_in = {k: v for k, v in _L0_gnn_all.items() if k in ('Wq', 'bq', 'Wk', 'bk', 'Wv', 'bv', 'Wo', 'bo', 'W1', 'b1', 'W2', 'b2', 'g1', 'be1', 'g2', 'be2')}
    del _L0_gnn_all

    def _L1_gnn_setup():
        import jax, jax.numpy as jnp
        import numpy as np
        N_NODES = 2500
        N_EDGES = 40000
        HIDDEN = 512
        EDGE_DIM = 64
        LN_EPS = 1e-05

        def mish(x):
            return x * jnp.tanh(jax.nn.softplus(x))
        key = jax.random.key(seed)
        ks = jax.random.split(key, 8)
        s = lambda fan_in: 1.0 / np.sqrt(fan_in)
        return {'x': jax.random.normal(ks[0], (N_NODES, HIDDEN), dtype=jnp.float32), 'edge_index': jax.random.randint(ks[1], (2, N_EDGES), 0, N_NODES, dtype=jnp.int64), 'edge_attr': jax.random.normal(ks[2], (N_EDGES, EDGE_DIM), dtype=jnp.float32), 'W1': jax.random.normal(ks[3], (2 * HIDDEN + EDGE_DIM, HIDDEN), dtype=jnp.float32) * s(2 * HIDDEN + EDGE_DIM), 'b1': jnp.zeros((HIDDEN,), dtype=jnp.float32), 'W2': jax.random.normal(ks[4], (HIDDEN, HIDDEN), dtype=jnp.float32) * s(HIDDEN), 'b2': jnp.zeros((HIDDEN,), dtype=jnp.float32), 'W3': jax.random.normal(ks[5], (2 * HIDDEN, HIDDEN), dtype=jnp.float32) * s(2 * HIDDEN), 'b3': jnp.zeros((HIDDEN,), dtype=jnp.float32), 'W4': jax.random.normal(ks[6], (HIDDEN, HIDDEN), dtype=jnp.float32) * s(HIDDEN), 'b4': jnp.zeros((HIDDEN,), dtype=jnp.float32), 'gamma': jnp.ones((HIDDEN,), dtype=jnp.float32), 'beta': jnp.zeros((HIDDEN,), dtype=jnp.float32)}
    _L1_gnn_all = _L1_gnn_setup()
    _L1_gnn_in = {k: v for k, v in _L1_gnn_all.items() if k in ('W1', 'b1', 'W2', 'b2', 'W3', 'b3', 'W4', 'b4', 'gamma', 'beta')}
    del _L1_gnn_all

    def _L2_gnn_setup():
        import jax, jax.numpy as jnp
        import numpy as np
        N_NODES = 6250
        N_EDGES = 100000
        D_IN = 512
        D_HID = 16

        def _gcn_conv(x, src, dst, W, b):
            n = x.shape[0]
            ones = jnp.ones(src.shape, dtype=x.dtype)
            deg = jax.ops.segment_sum(ones, dst, num_segments=n)
            dinv = jnp.where(deg > 0, jax.lax.rsqrt(deg), 0.0)
            norm = dinv[src] * dinv[dst]
            h = x @ W
            msg = h[src] * norm[:, None]
            return jax.ops.segment_sum(msg, dst, num_segments=n) + b
        key = jax.random.key(seed)
        k1, k2, k3, k4, k5 = jax.random.split(key, 5)
        x = jax.random.normal(k1, (N_NODES, D_IN), dtype=jnp.float32)
        src = jax.random.randint(k2, (N_EDGES,), 0, N_NODES, dtype=jnp.int64)
        dst = jax.random.randint(k3, (N_EDGES,), 0, N_NODES, dtype=jnp.int64)
        edge_index = jnp.stack([src, dst], axis=0)
        W1 = jax.random.normal(k4, (D_IN, D_HID), dtype=jnp.float32) * (1.0 / np.sqrt(D_IN))
        b1 = jnp.zeros((D_HID,), dtype=jnp.float32)
        W2 = jax.random.normal(k5, (D_HID, D_IN), dtype=jnp.float32) * (1.0 / np.sqrt(D_HID))
        b2 = jnpep = jnp.zeros((D_IN,), dtype=jnp.float32)
        return {'x': x, 'edge_index': edge_index, 'W1': W1, 'b1': b1, 'W2': W2, 'b2': b2}
    _L2_gnn_all = _L2_gnn_setup()
    _L2_gnn_in = {k: v for k, v in _L2_gnn_all.items() if k in ('W1', 'b1', 'W2', 'b2')}
    del _L2_gnn_all

    def _L3_gnn_setup():
        import jax, jax.numpy as jnp
        import numpy as np
        N_NODES = 6250
        N_EDGES = 20000
        NODE_DIM = 512
        EDGE_DIM = 64
        NUM_LAYERS = 3
        LN_EPS = 1e-05

        def _layer_norm(x, gamma, beta):
            mu = jnp.mean(x, axis=-1, keepdims=True)
            var = jnp.mean((x - mu) ** 2, axis=-1, keepdims=True)
            return (x - mu) * jax.lax.rsqrt(var + LN_EPS) * gamma + beta
        key = jax.random.key(seed)
        k1, k2, k3, k4 = jax.random.split(key, 4)
        node_features = jax.random.normal(k1, (N_NODES, NODE_DIM), dtype=jnp.float32)
        edge_index = jax.random.randint(k2, (2, N_EDGES), 0, N_NODES, dtype=jnp.int32)
        edge_features = jax.random.normal(k3, (N_EDGES, EDGE_DIM), dtype=jnp.float32)
        Ws = jax.random.normal(k4, (NUM_LAYERS, NODE_DIM + EDGE_DIM, NODE_DIM), dtype=jnp.float32) * (1.0 / np.sqrt(NODE_DIM + EDGE_DIM))
        bs = jnp.zeros((NUM_LAYERS, NODE_DIM), dtype=jnp.float32)
        gammas = jnp.ones((NUM_LAYERS, NODE_DIM), dtype=jnp.float32)
        betas = jnp.zeros((NUM_LAYERS, NODE_DIM), dtype=jnp.float32)
        return {'node_features': node_features, 'edge_index': edge_index, 'edge_features': edge_features, 'Ws': Ws, 'bs': bs, 'gammas': gammas, 'betas': betas}
    _L3_gnn_all = _L3_gnn_setup()
    _L3_gnn_in = {k: v for k, v in _L3_gnn_all.items() if k in ('Ws', 'bs', 'gammas', 'betas')}
    del _L3_gnn_all
    return {'x': x, 'src': src, 'dst': dst, 'edge_attr_64': edge_attr_64, 'L0_gnn_Wq': _L0_gnn_in['Wq'], 'L0_gnn_bq': _L0_gnn_in['bq'], 'L0_gnn_Wk': _L0_gnn_in['Wk'], 'L0_gnn_bk': _L0_gnn_in['bk'], 'L0_gnn_Wv': _L0_gnn_in['Wv'], 'L0_gnn_bv': _L0_gnn_in['bv'], 'L0_gnn_Wo': _L0_gnn_in['Wo'], 'L0_gnn_bo': _L0_gnn_in['bo'], 'L0_gnn_W1': _L0_gnn_in['W1'], 'L0_gnn_b1': _L0_gnn_in['b1'], 'L0_gnn_W2': _L0_gnn_in['W2'], 'L0_gnn_b2': _L0_gnn_in['b2'], 'L0_gnn_g1': _L0_gnn_in['g1'], 'L0_gnn_be1': _L0_gnn_in['be1'], 'L0_gnn_g2': _L0_gnn_in['g2'], 'L0_gnn_be2': _L0_gnn_in['be2'], 'L1_gnn_W1': _L1_gnn_in['W1'], 'L1_gnn_b1': _L1_gnn_in['b1'], 'L1_gnn_W2': _L1_gnn_in['W2'], 'L1_gnn_b2': _L1_gnn_in['b2'], 'L1_gnn_W3': _L1_gnn_in['W3'], 'L1_gnn_b3': _L1_gnn_in['b3'], 'L1_gnn_W4': _L1_gnn_in['W4'], 'L1_gnn_b4': _L1_gnn_in['b4'], 'L1_gnn_gamma': _L1_gnn_in['gamma'], 'L1_gnn_beta': _L1_gnn_in['beta'], 'L2_gnn_W1': _L2_gnn_in['W1'], 'L2_gnn_b1': _L2_gnn_in['b1'], 'L2_gnn_W2': _L2_gnn_in['W2'], 'L2_gnn_b2': _L2_gnn_in['b2'], 'L3_gnn_Ws': _L3_gnn_in['Ws'], 'L3_gnn_bs': _L3_gnn_in['bs'], 'L3_gnn_gammas': _L3_gnn_in['gammas'], 'L3_gnn_betas': _L3_gnn_in['betas']}

def reference(x, src, dst, edge_attr_64, L0_gnn_Wq, L0_gnn_bq, L0_gnn_Wk, L0_gnn_bk, L0_gnn_Wv, L0_gnn_bv, L0_gnn_Wo, L0_gnn_bo, L0_gnn_W1, L0_gnn_b1, L0_gnn_W2, L0_gnn_b2, L0_gnn_g1, L0_gnn_be1, L0_gnn_g2, L0_gnn_be2, L1_gnn_W1, L1_gnn_b1, L1_gnn_W2, L1_gnn_b2, L1_gnn_W3, L1_gnn_b3, L1_gnn_W4, L1_gnn_b4, L1_gnn_gamma, L1_gnn_beta, L2_gnn_W1, L2_gnn_b1, L2_gnn_W2, L2_gnn_b2, L3_gnn_Ws, L3_gnn_bs, L3_gnn_gammas, L3_gnn_betas):
    import jax
    import jax.numpy as jnp

    def _L0_gnn_ref(x, edge_index, Wq, bq, Wk, bk, Wv, bv, Wo, bo, W1, b1, W2, b2, g1, be1, g2, be2):
        import jax, jax.numpy as jnp
        import numpy as np
        N, E = (512, 16384)
        D_IN, D_OUT, H = (512, 512, 8)
        HEAD = D_OUT // H
        EPS = 1e-05

        def _layer_norm(x, g, b):
            m = jnp.mean(x, axis=-1, keepdims=True)
            v = jnp.mean(jnp.square(x - m), axis=-1, keepdims=True)
            return (x - m) * jax.lax.rsqrt(v + EPS) * g + b
        q = (x @ Wq + bq).reshape(N, H, HEAD)
        k = (x @ Wk + bk).reshape(N, H, HEAD)
        v = (x @ Wv + bv).reshape(N, H, HEAD)
        scores = jnp.einsum('nhd,mhd->nhm', q, k) / np.sqrt(HEAD)
        adj = jnp.zeros((N, N), jnp.float32).at[edge_index[0], edge_index[1]].set(1.0)
        scores = jnp.where(adj[:, None, :] == 0, -1000000000.0, scores)
        attn = jax.nn.softmax(scores, axis=1)
        attn_out = jnp.einsum('nhm,mhd->nhd', attn, v).reshape(N, D_OUT)
        attn_out = attn_out @ Wo + bo
        h1 = _layer_norm(x + attn_out, g1, be1)
        ff = jax.nn.relu(h1 @ W1 + b1) @ W2 + b2
        return _layer_norm(h1 + ff, g2, be2)

    def _L1_gnn_ref(x, edge_index, edge_attr, W1, b1, W2, b2, W3, b3, W4, b4, gamma, beta):
        import jax, jax.numpy as jnp
        import numpy as np
        N_NODES = 2500
        N_EDGES = 40000
        HIDDEN = 512
        EDGE_DIM = 64
        LN_EPS = 1e-05

        def mish(x):
            return x * jnp.tanh(jax.nn.softplus(x))
        src, dst = (edge_index[0], edge_index[1])
        edge_feat = jnp.concatenate([x[src], x[dst], edge_attr], axis=-1)
        h = mish(edge_feat @ W1 + b1)
        messages = mish(h @ W2 + b2)
        agg = jax.ops.segment_sum(messages, dst, num_segments=x.shape[0])
        u = mish(jnp.concatenate([x, agg], axis=-1) @ W3 + b3)
        out = u @ W4 + b4
        y = x + out
        mu = jnp.mean(y, axis=-1, keepdims=True)
        var = jnp.mean(jnp.square(y - mu), axis=-1, keepdims=True)
        return (y - mu) * jax.lax.rsqrt(var + LN_EPS) * gamma + beta

    def _L2_gnn_ref(x, edge_index, W1, b1, W2, b2):
        import jax, jax.numpy as jnp
        import numpy as np
        N_NODES = 6250
        N_EDGES = 100000
        D_IN = 512
        D_HID = 16

        def _gcn_conv(x, src, dst, W, b):
            n = x.shape[0]
            ones = jnp.ones(src.shape, dtype=x.dtype)
            deg = jax.ops.segment_sum(ones, dst, num_segments=n)
            dinv = jnp.where(deg > 0, jax.lax.rsqrt(deg), 0.0)
            norm = dinv[src] * dinv[dst]
            h = x @ W
            msg = h[src] * norm[:, None]
            return jax.ops.segment_sum(msg, dst, num_segments=n) + b
        n = x.shape[0]
        loop = jnp.arange(n, dtype=edge_index.dtype)
        src = jnp.concatenate([edge_index[0], loop])
        dst = jnp.concatenate([edge_index[1], loop])
        h = _gcn_conv(x, src, dst, W1, b1)
        h = jax.nn.relu(h)
        out = _gcn_conv(h, src, dst, W2, b2)
        return out

    def _L3_gnn_ref(node_features, edge_index, edge_features, Ws, bs, gammas, betas):
        import jax, jax.numpy as jnp
        import numpy as np
        N_NODES = 6250
        N_EDGES = 20000
        NODE_DIM = 512
        EDGE_DIM = 64
        NUM_LAYERS = 3
        LN_EPS = 1e-05

        def _layer_norm(x, gamma, beta):
            mu = jnp.mean(x, axis=-1, keepdims=True)
            var = jnp.mean((x - mu) ** 2, axis=-1, keepdims=True)
            return (x - mu) * jax.lax.rsqrt(var + LN_EPS) * gamma + beta
        src, tgt = (edge_index[0], edge_index[1])
        x = node_features
        n = x.shape[0]
        for i in range(NUM_LAYERS):
            msg = jnp.concatenate([x[src], edge_features], axis=-1)
            msg = msg @ Ws[i] + bs[i]
            agg = jax.ops.segment_sum(msg, tgt, num_segments=n)
            x = x + agg
            x = _layer_norm(x, gammas[i], betas[i])
            x = jax.nn.relu(x)
        return x
    edge_index = jnp.stack([src, dst])
    h = jnp.maximum(_layernorm(x, axis=-1), 0.0)
    x = x + _L0_gnn_ref(h, edge_index, L0_gnn_Wq, L0_gnn_bq, L0_gnn_Wk, L0_gnn_bk, L0_gnn_Wv, L0_gnn_bv, L0_gnn_Wo, L0_gnn_bo, L0_gnn_W1, L0_gnn_b1, L0_gnn_W2, L0_gnn_b2, L0_gnn_g1, L0_gnn_be1, L0_gnn_g2, L0_gnn_be2)
    h = jnp.maximum(_layernorm(x, axis=-1), 0.0)
    x = x + _L1_gnn_ref(h, edge_index, edge_attr_64, L1_gnn_W1, L1_gnn_b1, L1_gnn_W2, L1_gnn_b2, L1_gnn_W3, L1_gnn_b3, L1_gnn_W4, L1_gnn_b4, L1_gnn_gamma, L1_gnn_beta)
    h = jnp.maximum(_layernorm(x, axis=-1), 0.0)
    x = x + _L2_gnn_ref(h, edge_index, L2_gnn_W1, L2_gnn_b1, L2_gnn_W2, L2_gnn_b2)
    h = jnp.maximum(_layernorm(x, axis=-1), 0.0)
    x = x + _L3_gnn_ref(h, edge_index, edge_attr_64, L3_gnn_Ws, L3_gnn_bs, L3_gnn_gammas, L3_gnn_betas)
    return x

_drawn_inputs = setup_inputs


def setup_inputs(seed=0):
    import zlib

    import numpy as np

    out = dict(_drawn_inputs(seed))
    spreads = {'L0_gnn_bq': (0.0, 2.0),
     'L0_gnn_bk': (0.0, 2.0),
     'L0_gnn_bv': (0.0, 0.1),
     'L0_gnn_bo': (0.0, 2.0),
     'L0_gnn_b1': (0.0, 0.1),
     'L0_gnn_b2': (0.0, 0.1),
     'L0_gnn_g1': (1.0, 0.2),
     'L0_gnn_be1': (0.0, 0.1),
     'L0_gnn_g2': (1.0, 0.2),
     'L0_gnn_be2': (0.0, 0.1),
     'L1_gnn_b1': (0.0, 0.1),
     'L1_gnn_b2': (0.0, 0.1),
     'L1_gnn_b3': (0.0, 0.473),
     'L1_gnn_b4': (0.0, 0.338),
     'L1_gnn_gamma': (1.0, 0.2),
     'L1_gnn_beta': (0.0, 0.1),
     'L2_gnn_b1': (0.0, 0.294),
     'L2_gnn_b2': (0.0, 0.1),
     'L3_gnn_bs': (0.0, 0.1),
     'L3_gnn_gammas': (1.0, 0.2),
     'L3_gnn_betas': (0.0, 0.1)}
    factors = {'L0_gnn_Wq': 7.701, 'L0_gnn_Wk': 8.0}
    for name, (base, spread) in spreads.items():
        noise = np.random.default_rng([zlib.crc32(name.encode()), seed]).standard_normal(out[name].shape)
        drawn = base * np.exp(spread * noise) if base else spread * noise
        out[name] = jnp.asarray(drawn.astype(out[name].dtype))
    for name, factor in factors.items():
        out[name] = (out[name] * factor).astype(out[name].dtype)
    return out
```

```python
from contextlib import ExitStack

import concourse.bass as bass
from concourse import mybir


def gnn_stack_kernel(nc, ins, out):
    f32, f32r, bf16, i32 = mybir.dt.float32, mybir.dt.float32r, mybir.dt.bfloat16, mybir.dt.int32
    ALU, ACT, AX = mybir.AluOpType, mybir.ActivationFunctionType, mybir.AxisListType

    N, D = ins["x"].shape
    E, DE = ins["edge_attr_64"].shape
    P = 128
    NT = N // P
    T = E // P
    HEADS = 8
    HD = D // HEADS
    FT = ins["L0_gnn_W1"].shape[1] // P
    DH = ins["L2_gnn_W1"].shape[1]
    LAYERS = ins["L3_gnn_Ws"].shape[0]
    EPS = 1e-5
    SHIFT = 6
    WIN = 1 << SHIFT
    HALF = N // 2
    TOP = 1e8
    QUADS = T // 4
    assert N == D == 512 and T % 4 == 0 and 2 * DE == P and FT == 2 * NT

    ctx = ExitStack()
    with ctx:
        def sb(name, shape, dt=f32, to=ctx):
            return to.enter_context(nc.sbuf_tensor(name, shape, dt))

        src_table = nc.dram_tensor("src_table", (N, D), f32, kind="Internal").ap()
        dst_table = nc.dram_tensor("dst_table", (N, D), f32, kind="Internal").ap()
        eaT_dram = nc.dram_tensor("eaT_dram", (P, E), f32, kind="Internal").ap()

        ident = sb("ident", [P, P])
        iota_n = sb("iota_n", [P, N])
        ones = sb("ones", [P, 1])
        zrow = sb("zrow", [1, N], bf16)
        eps_c = sb("eps_c", [P, 1])
        dst_f = sb("dst_f", [P, T])
        src_f = sb("src_f", [P, T])
        dst_i = sb("dst_i", [P, T], i32)
        src_i = sb("src_i", [P, T], i32)
        idx_now = sb("idx_now", [P, 2, 4], i32)
        win_f = sb("win_f", [T, 2])
        win_v = sb("win_v", [T, 2], i32)
        win_i = sb("win_i", [T, 2], i32)
        win = sb("win", [1, 2 * T], i32)
        xres = sb("xres", [P, NT, D])
        h = sb("h", [P, NT, D])
        hT = sb("hT", [P, NT, N])
        CT = sb("CT", [P, NT, N])
        EAT = sb("EAT", [DE + 1, N])
        deg = sb("deg", [P, NT])
        dlog = sb("dlog", [P, NT])
        dinv = sb("dinv", [P, NT])
        bcol = sb("bcol", [P, 20])
        bn_st = sb("bn_st", [P, 8, NT, 6])
        bn_mv = sb("bn_mv", [P, 8, NT, 2])
        lnv = sb("lnv", [P, 8, NT])
        rstd = sb("rstd", [P, 8, NT])
        nbias = sb("nbias", [P, 8, NT])
        WA = sb("WA", [P, 8, NT * D])
        brow = sb("brow", [P, 7, D])
        w1c_hi = sb("w1c_hi", [P, D], f32r)
        w1c_lo = sb("w1c_lo", [DE, D], f32r)
        b2_rows = sb("b2_rows", [P, D], f32r)
        ones_r = sb("ones_r", [P, P], f32r)
        w2_hi = sb("w2_hi", [P, NT, D], f32r)
        w2_lo = sb("w2_lo", [P, NT, D], f32r)
        l2w1 = sb("l2w1", [P, NT, DH])
        l2w2 = sb("l2w2", [DH, D])
        l2b1 = sb("l2b1", [P, DH])
        t1 = sb("t1", [P, NT, DH])
        t2 = sb("t2", [P, NT, DH])
        a2 = sb("a2", [DH, N])

        wx_flat = WA[:, 5:8, :].rearrange("p l w -> p (l w)")
        we_flat = WA[0:DE + 1, 3, :]

        def slot(k):
            return WA[:, k, :].rearrange("p (t d) -> p t d", d=D)

        with ExitStack() as a:
            y = sb("y", [P, NT, D], to=a)
            mask = sb("mask", [P, NT, N], to=a)
            qT = sb("qT", [P, NT, N], to=a)
            kT = sb("kT", [P, NT, N], to=a)
            v = sb("v", [P, NT, D], to=a)
            S = sb("S", [P, 2, HEADS, HALF], to=a)
            smx = sb("smx", [P, HALF], to=a)
            ssm = sb("ssm", [P, 2, HALF], to=a)
        w1c_raw = mask[:, 0, :]
        b2_raw = mask[0:33, 1, :]
        with ExitStack() as a:
            sb("unused_by_counting", [P, 5, NT * D], to=a)
            idx_i = sb("idx_i", [T, 2, P], i32, to=a)
            idx_f = sb("idx_f", [T, 2, P], to=a)
            e_raw = sb("e_raw", [P, 4, DE + 1], to=a)
            e_split = sb("e_split", [P, 4, P], f32r, to=a)
            oh_src = sb("oh_src", [P, 2, N], to=a)
            oh_cnt = sb("oh_cnt", [P, 2, N], to=a)
            eaT_out = sb("eaT_out", [P, 4 * P], to=a)
        with ExitStack() as a:
            G = sb("G", [P, 4, D], to=a)
            h_hi = sb("h_hi", [P, 2, NT, 2 * P], f32r, to=a)
            h_lo = sb("h_lo", [P, 2, NT, 2 * P], f32r, to=a)
            eaT = sb("eaT", [P, 2, 2 * P], f32r, to=a)
            eA = sb("eA", [P, 2, D], to=a)
            uA = sb("uA", [P, 2, D], to=a)
            mA = sb("mA", [P, 2, D], to=a)
            eB = sb("eB", [P, 2, D], to=a)
            uB = sb("uB", [P, 2, D], to=a)
            mB = sb("mB", [P, 2, D], to=a)
            oh = sb("oh", [P, 2, N], to=a)

        bank = [ctx.enter_context(nc.psum_tensor(f"bank{i}", [P, 512], f32)) for i in range(8)]

        s = {name: ctx.enter_context(nc.semaphore(name)) for name in """
            consts ident_done idx_in idx_float idx_T idx_taken win_range win_value win_shift win_row
            x_in wq_in wk_in wv_in wo_in f1_in f2_in bcol_in
            rows_in
            w1a_in w1b_in w2_in w3_in w4_in wx_in affine_in we_in l2_in b2_in w1c_in
            rows1_in
            ea_in0 ea_in1 ea_hi ea_lo src_hot dst_hot counted ea_evac ea_out
            counts ct_taken cT_ready mask_ready deg_ready deg_taken dlog_done dinv_ready
            ln_stats ln_mv ln_log ln_rstd ln_nb h_ready hT_ready hT_taken
            qkv_ready qkv_taken w2hi_done w2lo_done w1chi_done w1clo_done b2_done
            s_ready s_masked s_max s_sub s_exp s_sum s_log s_rec att_ready av_done av_taken
            hb_done wo_ready y1_ready y_norm y_scaled hb2_done ff1_ready ff1_taken ff2_ready y2_ready
            y_shifted x1_ready
            tab_ready ptab_taken qtab_taken src_stored dst_stored idx_now_set gath0 gath1 eaT0 eaT1
            preA expA topA sqA logA recA mishA hiA loA
            preB expB topB sqB logB recB mishB hotB scattered
            agg_ready agg_taken hb4_done u_ready u_x u_exp u_top u_sq u_log u_rec u_mish
            w4_ready y4_ready x2_ready
            t1_ready t1_taken a1_ready a1_sum a1_dinv a1_bias a1_relu t2_done a2_ready a2_taken xb2_done
            o2_ready x3_ready
            m_agg m_taken m_msg m_y m_norm m_scaled m_shifted m_h result stored
            """.split()}

        block = ctx.enter_context(nc.Block())

        def need(eng, semaphore, value):
            if not isinstance(value, int) or value > 0:
                eng.wait_ge(semaphore, value)

        def rows(ap):
            return ap.rearrange("(t p) d -> p t d", p=P)

        def spread(name):
            return ins[name].rearrange("(a d) -> a d", a=1).to_broadcast([P, D])

        def ws(w):
            return bass.ds(w * WIN, WIN)

        BV, BO, G1, BE1, B2, G2, BE2 = range(7)
        B1, B4, GAMMA, BETA, L2B2 = range(5)
        LN_IN0, LN_A, LN_B, LN_IN1, LN_C, LN_IN2, LN_IN3, LN_L3 = range(8)

        @block.sync
        def _(eng):
            eng.dma_start(idx_i[:, 0, :], ins["dst"].rearrange("(t p) -> t p", p=P)).then_inc(s["idx_in"], 16)
            eng.dma_start(idx_i[:, 1, :], ins["src"].rearrange("(t p) -> t p", p=P)).then_inc(s["idx_in"], 16)
            eng.dma_start(xres[:, :, :], rows(ins["x"])).then_inc(s["x_in"], 16)

            pairs = ins["edge_attr_64"].rearrange("(g j p) d -> g p j d", j=2, p=P)

            def load_pair(pair, k, loaded):
                eng.dma_start(e_raw[:, 2 * k:2 * k + 2, 0:DE], pairs[bass.ds(pair, 1), :, :, :]
                              .rearrange("g p j d -> (g p) j d")).then_inc(loaded, 16)

            def store_quad(i):
                eng.wait_ge(s["ea_evac"], i + 1)
                eng.dma_start(eaT_dram[:, bass.ds(i * (4 * P), 4 * P)], eaT_out[:, :]).then_inc(s["ea_out"], 16)

            eng.wait_ge(s["consts"], 8)
            load_pair(0, 0, s["ea_in0"])
            load_pair(1, 1, s["ea_in1"])
            eng.wait_ge(s["win_shift"], 1)
            eng.dma_start(win[0:1, :], win_i[:, :]).then_inc(s["win_row"], 16)
            with eng.Fori(0, QUADS - 1) as i:
                eng.wait_ge(s["counted"], 4 * i + 2)
                load_pair(2 * i + 2, 0, s["ea_in0"])
                eng.wait_ge(s["counted"], 4 * i + 4)
                load_pair(2 * i + 3, 1, s["ea_in1"])
                store_quad(i)
            store_quad(QUADS - 1)

            w1 = ins["L1_gnn_W1"]
            eng.wait_ge(s["qkv_ready"], NT)
            eng.dma_start(slot(0), rows(w1[0:D, :])).then_inc(s["w1a_in"], 16)
            eng.wait_ge(s["qkv_ready"], 2 * NT)
            eng.dma_start(slot(1), rows(w1[D:2 * D, :])).then_inc(s["w1b_in"], 16)
            eng.wait_ge(s["qkv_ready"], 3 * NT)
            eng.dma_start(slot(2), rows(ins["L1_gnn_W2"])).then_inc(s["w2_in"], 16)
            eng.wait_ge(s["qkv_taken"], 3 * NT)
            eng.dma_start(brow[:, B1, :], spread("L1_gnn_b1")).then_inc(s["rows1_in"], 16)
            eng.wait_ge(s["hb_done"], NT)
            eng.dma_start(brow[:, B4, :], spread("L1_gnn_b4")).then_inc(s["rows1_in"], 16)
            eng.wait_ge(s["h_ready"], 2 * NT)
            eng.dma_start(brow[:, GAMMA, :], spread("L1_gnn_gamma")).then_inc(s["rows1_in"], 16)
            eng.dma_start(brow[:, BETA, :], spread("L1_gnn_beta")).then_inc(s["rows1_in"], 16)
            eng.wait_ge(s["ff1_ready"], FT)
            for c in range(2):
                eng.dma_start(slot(3 + c), rows(ins["L1_gnn_W3"][c * D:(c + 1) * D, :])).then_inc(s["w3_in"], 16)
            eng.wait_ge(s["hb2_done"], NT)
            eng.dma_start(brow[:, L2B2, :], spread("L2_gnn_b2")).then_inc(s["rows1_in"], 16)
            eng.wait_ge(s["w2lo_done"], NT)
            eng.dma_start(slot(2), rows(ins["L1_gnn_W4"])).then_inc(s["w4_in"], 16)
            eng.wait_ge(s["ff2_ready"], NT)
            for l in range(LAYERS):
                eng.dma_start(slot(5 + l), rows(ins["L3_gnn_Ws"][l, 0:D, :])).then_inc(s["wx_in"], 16)

            for t in range(NT):
                eng.wait_ge(s["ptab_taken"], t + 1)
                eng.dma_start(src_table[t * P:(t + 1) * P, :], y[:, t, :]).then_inc(s["src_stored"], 16)
            for t in range(NT):
                eng.wait_ge(s["qtab_taken"], t + 1)
                eng.dma_start(dst_table[t * P:(t + 1) * P, :], v[:, t, :]).then_inc(s["dst_stored"], 16)
            for l in range(LAYERS):
                eng.dma_start(WA[:, 0, l * D:(l + 1) * D], ins["L3_gnn_gammas"][l:l + 1, :].to_broadcast([P, D])).then_inc(s["affine_in"], 16)
                eng.dma_start(WA[:, 1, l * D:(l + 1) * D], ins["L3_gnn_betas"][l:l + 1, :].to_broadcast([P, D])).then_inc(s["affine_in"], 16)

            def load_group(g, k, loaded):
                eng.dma_start(eaT[:, k, :].bitcast(f32), eaT_dram[:, bass.ds(g * (2 * P), 2 * P)]).then_inc(loaded, 16)

            eng.wait_ge(s["src_stored"], 16 * NT)
            eng.wait_ge(s["dst_stored"], 16 * NT)
            eng.wait_ge(s["ea_out"], 16 * QUADS)
            load_group(0, 0, s["eaT0"])
            load_group(1, 1, s["eaT1"])
            with eng.Fori(0, QUADS - 1) as i:
                eng.wait_ge(s["preA"], 4 * i + 2)
                load_group(2 * i + 2, 0, s["eaT0"])
                eng.wait_ge(s["preA"], 4 * i + 4)
                load_group(2 * i + 3, 1, s["eaT1"])

            eng.wait_ge(s["u_ready"], NT)
            for l in range(LAYERS):
                eng.dma_start(we_flat[0:DE, l * D:(l + 1) * D], ins["L3_gnn_Ws"][l, D:D + DE, :]).then_inc(s["we_in"], 16)
                eng.dma_start(we_flat[DE:DE + 1, l * D:(l + 1) * D], ins["L3_gnn_bs"][l:l + 1, :]).then_inc(s["we_in"], 16)
            for t in range(NT):
                eng.wait_ge(s["result"], t + 1)
                eng.dma_start(out[t * P:(t + 1) * P, :], y[:, t, :]).then_inc(s["stored"], 16)
            eng.wait_ge(s["stored"], 16 * NT)

        @block.gpsimd
        def _(eng):
            eng.memset(ident[:, :], 0.0).then_inc(s["consts"], 1)
            eng.iota(iota_n[:, :], pattern=[[1, N]], base=0, channel_multiplier=0,
                     allow_small_or_imprecise_dtypes=True).then_inc(s["consts"], 1)
            eng.memset(ones[:, :], 1.0).then_inc(s["consts"], 1)
            eng.memset(zrow[:, :], 0.0).then_inc(s["consts"], 1)
            eng.memset(eps_c[:, :], EPS).then_inc(s["consts"], 1)
            eng.memset(e_raw[:, :, :], 1.0).then_inc(s["consts"], 1)
            eng.memset(ones_r[:, :].bitcast(f32), 1.0).then_inc(s["consts"], 1)
            eng.memset(b2_rows[:, :].bitcast(f32), 0.0).then_inc(s["consts"], 1)
            eng.wait_ge(s["consts"], 8)
            eng.affine_select(out=ident[:, :], in_=ident[:, :], compare_op=ALU.not_equal, fill=1.0, base=0,
                              pattern=[[-1, P]], channel_multiplier=1).then_inc(s["ident_done"], 1)
            eng.wait_ge(s["counted"], 8)
            eng.dma_start(slot(3), rows(ins["L0_gnn_Wo"])).then_inc(s["wo_in"], 16)
            for c in range(2):
                eng.dma_start(slot(4 + c), rows(ins["L0_gnn_W1"][:, c * D:(c + 1) * D])).then_inc(s["f1_in"], 16)
            for c in range(2):
                eng.dma_start(slot(6 + c), rows(ins["L0_gnn_W2"][c * D:(c + 1) * D, :])).then_inc(s["f2_in"], 16)
            eng.dma_start(l2w1[:, :, :], rows(ins["L2_gnn_W1"])).then_inc(s["l2_in"], 16)
            eng.dma_start(l2w2[:, :], ins["L2_gnn_W2"]).then_inc(s["l2_in"], 16)
            eng.dma_start(l2b1[:, :], ins["L2_gnn_b1"].rearrange("(a d) -> a d", a=1).to_broadcast([P, DH])).then_inc(s["l2_in"], 16)

            eng.wait_ge(s["s_masked"], 2 * NT * 4)
            for half in range(2):
                eng.dma_start(w1c_raw[half * DE:(half + 1) * DE, :], ins["L1_gnn_W1"][2 * D:2 * D + DE, :]).then_inc(s["w1c_in"], 16)
                eng.dma_start(b2_raw[32 * half:32 * half + 1, :], ins["L1_gnn_b2"].rearrange("(a d) -> a d", a=1)).then_inc(s["b2_in"], 16)

            eng.wait_ge(s["src_stored"], 16 * NT)
            eng.wait_ge(s["dst_stored"], 16 * NT)
            eng.wait_ge(s["idx_taken"], 4)

            def gather(g, k, gathered, before):
                eng.tensor_copy(idx_now[:, k, 0:2], src_i[:, bass.ds(2 * g, 2)]).then_inc(s["idx_now_set"], 1)
                eng.tensor_copy(idx_now[:, k, 2:4], dst_i[:, bass.ds(2 * g, 2)]).then_inc(s["idx_now_set"], 1)
                eng.wait_ge(s["idx_now_set"], 2 * g + 2)
                eng.nop(nofuse=True)
                for j in range(2):
                    eng.indirect_dma_start(out=G[:, 2 * k + j, :], out_offset=None, in_=src_table,
                                           in_offset=bass.IndirectOffsetOnAxis(ap=idx_now[:, k, j:j + 1], axis=0)
                                           ).then_inc(gathered, 16)
                eng.wait_ge(gathered, 64 * before + 32)
                eng.nop(nofuse=True)
                for j in range(2):
                    eng.indirect_dma_start(out=G[:, 2 * k + j, :], out_offset=None, in_=dst_table,
                                           in_offset=bass.IndirectOffsetOnAxis(ap=idx_now[:, k, 2 + j:3 + j], axis=0),
                                           compute_op=ALU.add).then_inc(gathered, 16)

            gather(0, 0, s["gath0"], 0)
            gather(1, 1, s["gath1"], 0)
            with eng.Fori(0, QUADS - 1) as i:
                eng.wait_ge(s["preA"], 4 * i + 2)
                gather(2 * i + 2, 0, s["gath0"], i + 1)
                eng.wait_ge(s["preA"], 4 * i + 4)
                gather(2 * i + 3, 1, s["gath1"], i + 1)

        @block.scalar
        def _(eng):
            eng.preload_act_table_set("natural_log_exp_and_others")
            eng.dma_start(slot(0), rows(ins["L0_gnn_Wq"])).then_inc(s["wq_in"], 16)
            eng.dma_start(slot(1), rows(ins["L0_gnn_Wk"])).then_inc(s["wk_in"], 16)
            eng.dma_start(slot(2), rows(ins["L0_gnn_Wv"])).then_inc(s["wv_in"], 16)
            for name, lo, n in (("L0_gnn_bq", 0, 4), ("L0_gnn_bk", 4, 4), ("L0_gnn_b1", 8, 8), ("L1_gnn_b3", 16, 4)):
                eng.dma_start(bcol[:, lo:lo + n], ins[name].rearrange("(c p) -> p c", p=P),
                              allow_slow_non_contiguous=True).then_inc(s["bcol_in"], 16)
            for name, k in (("bv", BV), ("bo", BO), ("g1", G1), ("be1", BE1), ("b2", B2), ("g2", G2), ("be2", BE2)):
                eng.dma_start(brow[:, k, :], spread("L0_gnn_" + name)).then_inc(s["rows_in"], 16)
            eng.wait_ge(s["consts"], 8)

            def inverse_deviation(k, t, before):
                eng.wait_ge(s["ln_mv"], before + t + 1)
                eng.activation(lnv[:, k, t:t + 1], bn_mv[:, k, t, 1:2], ACT.Ln, bias=eps_c[:, 0:1]).then_inc(s["ln_log"], 1)
                eng.wait_ge(s["ln_log"], before + t + 1)
                eng.activation(rstd[:, k, t:t + 1], lnv[:, k, t:t + 1], ACT.Exp, scale=-0.5).then_inc(s["ln_rstd"], 1)

            def relu_norm(k, before, done):
                for t in range(NT):
                    inverse_deviation(k, t, NT * k)
                for t in range(NT):
                    eng.wait_ge(s["ln_nb"], NT * before + t + 1)
                    eng.activation(h[:, t, :], xres[:, t, :], ACT.Relu, bias=nbias[:, k, t:t + 1],
                                   scale=rstd[:, k, t:t + 1]).then_inc(done, 1)

            def take_hT(before, banks):
                for t in range(NT):
                    eng.wait_ge(s["hT_ready"], before + t + 1)
                    eng.activation(hT[:, :, t * P:(t + 1) * P], banks[t % 2][:, :].rearrange("p (c n) -> p c n", n=P),
                                   ACT.Copy).then_inc(s["hT_taken"], 1)

            relu_norm(LN_IN0, 0, s["h_ready"])

            def quad(i):
                for q in range(4):
                    if q % 2 == 0:
                        eng.wait_ge((s["ea_in0"], s["ea_in1"])[q // 2], 16 * i + 16)
                    need(eng, s["counted"], 4 * i + q - 3)
                    eng.activation(e_split[:, q, 0:DE], e_raw[:, q, 0:DE], ACT.Copy).then_inc(s["ea_hi"], 1)
                eng.wait_ge(s["counted"], 4 * i + 4)
                need(eng, s["ea_out"], 16 * i)
                eng.activation(eaT_out[:, :], bank[5][:, :], ACT.Copy).then_inc(s["ea_evac"], 1)

            quad(0)
            with eng.Fori(1, QUADS) as i:
                quad(i)

            take_hT(0, bank[6:8])
            eng.wait_ge(s["counts"], 1)
            for t in range(NT):
                eng.activation(CT[:, t, :], bank[t][:, :], ACT.Copy).then_inc(s["ct_taken"], 1)
            eng.activation(EAT[:, :], bank[4][0:DE + 1, :], ACT.Copy).then_inc(s["ct_taken"], 1)
            eng.wait_ge(s["deg_taken"], 1)
            eng.activation(dlog[:, :], deg[:, :], ACT.Ln).then_inc(s["dlog_done"], 1)
            eng.wait_ge(s["dlog_done"], 1)
            eng.activation(dinv[:, :], dlog[:, :], ACT.Exp, scale=-0.5).then_inc(s["dinv_ready"], 1)

            for u in range(2 * NT):
                k = u % 2
                eng.wait_ge(s["s_sub"], u + 1)
                eng.activation(S[:, k, :, :], S[:, k, :, :], ACT.Exp).then_inc(s["s_exp"], 1)
                eng.wait_ge(s["s_sum"], u + 1)
                eng.activation(ssm[:, k, :], ssm[:, k, :], ACT.Ln).then_inc(s["s_log"], 1)
                eng.wait_ge(s["s_log"], u + 1)
                eng.activation(ssm[:, k, :], ssm[:, k, :], ACT.Exp, scale=-1.0).then_inc(s["s_rec"], 1)
                if u == NT:
                    eng.wait_ge(s["w2_in"], 16)
                    for t in range(NT):
                        eng.activation(w2_hi[:, t, :], slot(2)[:, t, :], ACT.Copy).then_inc(s["w2hi_done"], 1)
            eng.wait_ge(s["av_done"], 2 * NT)
            for t in range(NT):
                eng.activation(hT[:, t, :], bank[4 + t][:, :], ACT.Copy).then_inc(s["av_taken"], 1)
            for t in range(NT):
                inverse_deviation(LN_A, t, NT * LN_A)
            eng.wait_ge(s["w1c_in"], 32)
            eng.activation(w1c_hi[:, :], w1c_raw[:, :], ACT.Copy).then_inc(s["w1chi_done"], 1)
            eng.wait_ge(s["wo_ready"], NT)
            take_hT(NT, bank[4:6])
            eng.wait_ge(s["bcol_in"], 64)
            for f in range(FT):
                eng.wait_ge(s["ff1_ready"], f + 1)
                eng.activation((qT, kT)[f // NT][:, f % NT, :], bank[f % 4][:, :], ACT.Relu,
                               bias=bcol[:, 8 + f:9 + f]).then_inc(s["ff1_taken"], 1)
            for t in range(NT):
                inverse_deviation(LN_B, t, NT * LN_B)
            relu_norm(LN_IN1, 1, s["h_ready"])
            take_hT(2 * NT, bank[4:6])
            for t in range(NT):
                eng.wait_ge(s["tab_ready"], NT + t + 1)
                eng.activation(v[:, t, :], bank[t % 4][:, :], ACT.Copy).then_inc(s["qtab_taken"], 1)

            def step(n, q, first=True, second=True, finish=True):
                p = q % 2
                if first:
                    eng.wait_ge(s["preA"], n + 1)
                    need(eng, s["sqA"], n - 1)
                    eng.activation(eA[:, p, :], bank[p][:, :], ACT.Exp).then_inc(s["expA"], 1)
                if finish:
                    eng.wait_ge(s["sqB"], n - 2)
                    eng.activation(uB[:, 1 - p, :], uB[:, 1 - p, :], ACT.Ln, bias=1.0, scale=0.5).then_inc(s["logB"], 1)
                    eng.wait_ge(s["logB"], n - 2)
                    eng.activation(uB[:, 1 - p, :], uB[:, 1 - p, :], ACT.Exp, scale=-1.0).then_inc(s["recB"], 1)
                if first:
                    eng.wait_ge(s["sqA"], n + 1)
                    eng.activation(uA[:, p, :], uA[:, p, :], ACT.Ln, bias=1.0, scale=0.5).then_inc(s["logA"], 1)
                    eng.wait_ge(s["logA"], n + 1)
                    eng.activation(uA[:, p, :], uA[:, p, :], ACT.Exp, scale=-1.0).then_inc(s["recA"], 1)
                if second:
                    eng.wait_ge(s["preB"], n - 1)
                    need(eng, s["sqB"], n - 3)
                    eng.activation(eB[:, p, :], bank[2 + p][:, :], ACT.Exp).then_inc(s["expB"], 1)
                if first:
                    eng.wait_ge(s["mishA"], n + 1)
                    need(eng, s["preB"], n - p - 2)
                    eng.activation(h_hi[:, q // 2, 2 * p:2 * p + 2, :], mA[:, p, :].rearrange("p (c e) -> p c e", c=2),
                                   ACT.Copy).then_inc(s["hiA"], 1)

            for n in range(4):
                step(n, n, second=n >= 2, finish=n >= 3)
            with eng.Fori(1, QUADS) as i:
                for q in range(4):
                    step(4 * i + q, q)
            for n in range(T, T + 3):
                step(n, n % 4, first=False, second=n < T + 2)

            eng.wait_ge(s["agg_ready"], 1)
            for t in range(NT):
                eng.activation(mask[:, t, :], bank[4 + t][:, :], ACT.Copy).then_inc(s["agg_taken"], 1)
            for f in range(NT):
                eng.wait_ge(s["u_ready"], f + 1)
                eng.activation(v[:, f, :], bank[f][:, :], ACT.Exp, bias=bcol[:, 16 + f:17 + f]).then_inc(s["u_exp"], 1)
                if f:
                    finish_u = f - 1
                    eng.wait_ge(s["u_sq"], finish_u + 1)
                    eng.activation(v[:, finish_u, :], v[:, finish_u, :], ACT.Ln, bias=1.0, scale=0.5).then_inc(s["u_log"], 1)
                    eng.wait_ge(s["u_log"], finish_u + 1)
                    eng.activation(v[:, finish_u, :], v[:, finish_u, :], ACT.Exp, scale=-1.0).then_inc(s["u_rec"], 1)
            eng.wait_ge(s["u_sq"], NT)
            eng.activation(v[:, NT - 1, :], v[:, NT - 1, :], ACT.Ln, bias=1.0, scale=0.5).then_inc(s["u_log"], 1)
            eng.wait_ge(s["u_log"], NT)
            eng.activation(v[:, NT - 1, :], v[:, NT - 1, :], ACT.Exp, scale=-1.0).then_inc(s["u_rec"], 1)
            for t in range(NT):
                inverse_deviation(LN_C, t, NT * LN_C)
            relu_norm(LN_IN2, 2, s["h_ready"])
            take_hT(3 * NT, bank[4:6])
            eng.wait_ge(s["a2_ready"], 1)
            eng.activation(a2[:, :], bank[3][0:DH, :], ACT.Copy).then_inc(s["a2_taken"], 1)
            relu_norm(LN_IN3, 3, s["m_h"])

            with eng.Fori(0, LAYERS) as l:
                for f in range(NT):
                    eng.wait_ge(s["m_agg"], NT * l + f + 1)
                    eng.activation(hT[:, f, :], bank[f][:, :], ACT.Copy).then_inc(s["m_taken"], 1)
                for t in range(NT):
                    inverse_deviation(LN_L3, t, NT * l + NT * LN_L3)
                for t in range(NT):
                    eng.wait_ge(s["m_shifted"], NT * l + t + 1)
                    eng.activation(h[:, t, :], y[:, t, :], ACT.Relu).then_inc(s["m_h"], 1)

        @block.tensor
        def _(eng):
            def transposes(src, t, to):
                for c in range(NT):
                    mm = eng.transpose(to[:, c * P:(c + 1) * P], src[:, t, c * P:(c + 1) * P], ident[:, :])
                return mm

            def product(to, lhs, rhs):
                for j, (a, b) in enumerate(zip(lhs, rhs)):
                    mm = eng.matmul(to, a, b, start=(j == 0), stop=(j == len(lhs) - 1))
                return mm

            def clear(to):
                eng.matmul(to, zrow[:, 0:to.shape[0]], zrow[:, :], start=True, stop=False, skip_group_check=True)

            def close(to):
                return eng.matmul(to, zrow[:, 0:to.shape[0]], zrow[:, :], start=False, stop=True, skip_group_check=True)

            eng.wait_ge(s["ident_done"], 1)
            eng.wait_ge(s["idx_float"], 1)
            eng.transpose(bank[6][:, 0:T], idx_f[:, 0, :], ident[0:T, 0:T])
            eng.transpose(bank[6][:, P:P + T], idx_f[:, 1, :], ident[0:T, 0:T]).then_inc(s["idx_T"], 1)

            for t in range(NT):
                clear(bank[t][:, :])
            clear(bank[4][0:DE + 1, :])
            eng.wait_ge(s["win_row"], 16)

            def count(n, q):
                eng.wait_ge(s["src_hot"], n + 1)
                eng.wait_ge(s["dst_hot"], n + 1)
                eng.wait_ge(s["ea_lo"], n + 1)

                def window(w):
                    for t in range(NT):
                        eng.matmul(bank[t][:, ws(w)], oh_src[:, q % 2, t * P:(t + 1) * P], oh_cnt[:, q % 2, ws(w)],
                                   start=False, stop=False, skip_group_check=True)
                    eng.matmul(bank[4][0:DE + 1, ws(w)], e_raw[:, q, :], oh_cnt[:, q % 2, ws(w)],
                               start=False, stop=False, skip_group_check=True)

                first = eng.value_load(win[0:1, bass.ds(2 * n, 1)], min_val=0, max_val=N // WIN - 1)
                last = eng.value_load(win[0:1, bass.ds(2 * n + 1, 1)], min_val=0, max_val=N // WIN - 1)
                with eng.If(first < last):
                    with eng.Fori(first, last) as w:
                        window(w)
                window(last)
                eng.transpose(bank[5][:, q * P:(q + 1) * P], e_split[:, q, :].bitcast(f32), ident[:, :]).then_inc(s["counted"], 1)

            for q in range(4):
                count(q, q)
            with eng.Fori(1, QUADS) as i:
                for q in range(4):
                    if q == 0:
                        eng.wait_ge(s["ea_evac"], i)
                    count(4 * i + q, q)
            for t in range(NT):
                close(bank[t][:, :])
            close(bank[4][0:DE + 1, :]).then_inc(s["counts"], 1)

            def transpose_h(before, banks):
                for t in range(NT):
                    eng.wait_ge(s["h_ready"], before + t + 1)
                    if t >= 2:
                        eng.wait_ge(s["hT_taken"], before + t - 1)
                    transposes(h, t, banks[t % 2]).then_inc(s["hT_ready"], 1)

            eng.wait_ge(s["idx_taken"], 4)
            transpose_h(0, bank[6:8])

            eng.wait_ge(s["hT_taken"], NT)
            for j, (k, loaded) in enumerate(((0, s["wq_in"]), (1, s["wk_in"]), (2, s["wv_in"]))):
                eng.wait_ge(loaded, 16)
                for t in range(NT):
                    n = NT * j + t
                    if n >= 2:
                        eng.wait_ge(s["qkv_taken"], n - 1)
                    weight = [slot(k)[:, c, t * P:(t + 1) * P] for c in range(NT)]
                    nodes = [hT[:, c, t * P:(t + 1) * P] for c in range(NT)]
                    if j < 2:
                        mm = product(bank[6 + n % 2][:, :], weight, [hT[:, c, :] for c in range(NT)])
                    else:
                        mm = product(bank[6 + n % 2][:, :], nodes, [slot(k)[:, c, :] for c in range(NT)])
                    mm.then_inc(s["qkv_ready"], 1)

            eng.wait_ge(s["ct_taken"], NT + 1)
            eng.wait_ge(s["ea_evac"], QUADS)
            for t in range(NT):
                for c in range(NT):
                    mm = eng.matmul(bank[5][:, t:t + 1], CT[:, c, t * P:(t + 1) * P], ones[:, 0:1],
                                    start=(c == 0), stop=(c == NT - 1))
            mm.then_inc(s["deg_ready"], 1)
            for t in range(NT):
                for c in range(NT):
                    mm = eng.transpose(bank[t][:, c * P:(c + 1) * P], CT[:, c, t * P:(t + 1) * P], ident[:, :])
                mm.then_inc(s["cT_ready"], 1)

            def scores(u):
                half, m = u // NT, u % NT
                for j in range(4):
                    n = 4 * u + j
                    if n >= 4:
                        eng.wait_ge(s["s_masked"], n - 3)
                    for i in range(2):
                        c, lo = 2 * (j // 2) + i, HD * (j % 2)
                        mm = eng.matmul(bank[j][:, i * HALF:(i + 1) * HALF],
                                        kT[lo:lo + HD, c, m * P:(m + 1) * P],
                                        qT[lo:lo + HD, c, half * HALF:(half + 1) * HALF], start=True, stop=True)
                    mm.then_inc(s["s_ready"], 1)

            def attend(u):
                half, m, k = u // NT, u % NT, u % 2
                eng.wait_ge(s["att_ready"], u + 1)
                for hd in range(HEADS):
                    lo = HD * (hd % 2)
                    mm = eng.matmul(bank[4 + hd // 2][lo:lo + HD, half * HALF:(half + 1) * HALF],
                                    v[:, m, hd * HD:(hd + 1) * HD], S[:, k, hd, :],
                                    start=(m == 0), stop=(m == NT - 1))
                mm.then_inc(s["av_done"], 1)

            eng.wait_ge(s["mask_ready"], NT)
            eng.wait_ge(s["qkv_taken"], 3 * NT)
            eng.wait_ge(s["deg_taken"], 1)
            for u in range(2 * NT + 2):
                if u < 2 * NT:
                    scores(u)
                if u >= 2:
                    attend(u - 2)

            eng.wait_ge(s["av_taken"], NT)
            eng.wait_ge(s["wo_in"], 16)
            for t in range(NT):
                product(bank[t][:, :], [hT[:, c, t * P:(t + 1) * P] for c in range(NT)],
                        [slot(3)[:, c, :] for c in range(NT)]).then_inc(s["wo_ready"], 1)

            transpose_h(NT, bank[4:6])
            eng.wait_ge(s["hT_taken"], 2 * NT)
            eng.wait_ge(s["y1_ready"], NT)
            eng.wait_ge(s["f1_in"], 32)
            for f in range(FT):
                if f >= 4:
                    eng.wait_ge(s["ff1_taken"], f - 3)
                product(bank[f % 4][:, :], [slot(4 + f // NT)[:, c, (f % NT) * P:(f % NT + 1) * P] for c in range(NT)],
                        [hT[:, c, :] for c in range(NT)]).then_inc(s["ff1_ready"], 1)
            eng.wait_ge(s["ff1_taken"], FT)
            eng.wait_ge(s["f2_in"], 32)
            for t in range(NT):
                product(bank[4 + t][:, :], [(qT, kT)[c // NT][:, c % NT, t * P:(t + 1) * P] for c in range(FT)],
                        [slot(6 + c // NT)[:, c % NT, :] for c in range(FT)]).then_inc(s["ff2_ready"], 1)

            eng.wait_ge(s["y2_ready"], NT)
            transpose_h(2 * NT, bank[4:6])
            eng.wait_ge(s["hT_taken"], 3 * NT)
            for j, (k, loaded) in enumerate(((0, s["w1a_in"]), (1, s["w1b_in"]))):
                eng.wait_ge(loaded, 16)
                for t in range(NT):
                    if j:
                        eng.wait_ge(s["ptab_taken"], t + 1)
                    product(bank[t][:, :], [hT[:, c, t * P:(t + 1) * P] for c in range(NT)],
                            [slot(k)[:, c, :] for c in range(NT)]).then_inc(s["tab_ready"], 1)

            def first_layer(n, q, k_use):
                p, k = q % 2, q // 2
                if p == 0:
                    eng.wait_ge((s["gath0"], s["gath1"])[k], 64 * k_use + 64)
                    eng.wait_ge((s["eaT0"], s["eaT1"])[k], 16 * k_use + 16)
                need(eng, s["mishA"], n - 1)
                for c in range(2):
                    f = slice((2 * p + c) * P, (2 * p + c + 1) * P)
                    for j in range(2):
                        eng.matmul(bank[p][:, (2 * c + j) * P:(2 * c + j + 1) * P], G[:, 2 * k + j, f], ident[:, :],
                                   is_transpose=True, start=(c == 0 and j == 0), stop=False, skip_group_check=True)
                for c in range(2):
                    f = slice((2 * p + c) * P, (2 * p + c + 1) * P)
                    to = bank[p][:, 2 * c * P:2 * (c + 1) * P]
                    eng.matmul(to, w1c_hi[:, f], eaT[:, k, :], start=False, stop=False, skip_group_check=True)
                    mm = eng.matmul(to, w1c_lo[:, f], eaT[0:DE, k, :], start=False, stop=True, skip_group_check=True)
                mm.then_inc(s["preA"], 1)

            def second_layer(n, q, units_before):
                p, k = q % 2, q // 2
                if p == 0:
                    eng.wait_ge(s["hiA"], units_before)
                    eng.wait_ge(s["loA"], units_before)
                need(eng, s["mishB"], n - 1)
                to = bank[2 + p][:, :]
                eng.matmul(to, ones_r[:, :], b2_rows[:, :], start=True, stop=False)
                for c in range(NT):
                    hi, lo = h_hi[:, k, c, p * P:(p + 1) * P], h_lo[:, k, c, p * P:(p + 1) * P]
                    eng.matmul(to, hi, w2_hi[:, c, :], start=False, stop=False)
                    eng.matmul(to, hi, w2_lo[:, c, :], start=False, stop=False)
                    mm = eng.matmul(to, lo, w2_hi[:, c, :], start=False, stop=(c == NT - 1))
                mm.then_inc(s["preB"], 1)

            def scatter(n, q):
                eng.wait_ge(s["mishB"], n + 1)
                eng.wait_ge(s["hotB"], n + 1)

                def window(w):
                    for t in range(NT):
                        mm = eng.matmul(bank[4 + t][:, ws(w)], mB[:, q % 2, t * P:(t + 1) * P], oh[:, q % 2, ws(w)],
                                        start=False, stop=False, skip_group_check=True)
                    return mm

                first = eng.value_load(win[0:1, bass.ds(2 * n, 1)], min_val=0, max_val=N // WIN - 1)
                last = eng.value_load(win[0:1, bass.ds(2 * n + 1, 1)], min_val=0, max_val=N // WIN - 1)
                with eng.If(first < last):
                    with eng.Fori(first, last) as w:
                        window(w)
                window(last).then_inc(s["scattered"], 1)

            eng.wait_ge(s["ptab_taken"], NT)
            eng.wait_ge(s["qtab_taken"], NT)
            eng.wait_ge(s["w1chi_done"], 1)
            eng.wait_ge(s["w1clo_done"], 1)
            eng.wait_ge(s["w2hi_done"], NT)
            eng.wait_ge(s["w2lo_done"], NT)
            eng.wait_ge(s["b2_done"], 3)
            for t in range(NT):
                clear(bank[4 + t][:, :])
            for n in range(4):
                first_layer(n, n, 0)
                if n >= 2:
                    second_layer(n - 2, n - 2, 2)
            with eng.Fori(1, QUADS) as i:
                for q in range(4):
                    n = 4 * i + q
                    first_layer(n, q, i)
                    scatter(n - 4, q)
                    second_layer(n - 2, (q + 2) % 4, 4 * i + (0, 2)[q // 2])
            for n in range(T, T + 4):
                scatter(n - 4, n % 4)
                if n < T + 2:
                    second_layer(n - 2, (n + 2) % 4, T)
            for t in range(NT):
                mm = close(bank[4 + t][:, :])
            mm.then_inc(s["agg_ready"], 1)

            eng.wait_ge(s["w3_in"], 32)
            eng.wait_ge(s["mishB"], T)
            eng.wait_ge(s["agg_taken"], NT)
            for f in range(NT):
                product(bank[f][:, :], [slot(3 + c // NT)[:, c % NT, f * P:(f + 1) * P] for c in range(2 * NT)],
                        [(hT, mask)[c // NT][:, c % NT, :] for c in range(2 * NT)]).then_inc(s["u_ready"], 1)
            eng.wait_ge(s["w4_in"], 16)
            eng.wait_ge(s["u_mish"], NT)
            for t in range(NT):
                product(bank[4 + t][:, :], [qT[:, c, t * P:(t + 1) * P] for c in range(NT)],
                        [slot(2)[:, c, :] for c in range(NT)]).then_inc(s["w4_ready"], 1)

            eng.wait_ge(s["y4_ready"], NT)
            transpose_h(3 * NT, bank[4:6])
            eng.wait_ge(s["hT_taken"], 4 * NT)
            eng.wait_ge(s["l2_in"], 48)
            for t in range(NT):
                mm = product(bank[6][:, t * DH:(t + 1) * DH], [hT[:, c, t * P:(t + 1) * P] for c in range(NT)],
                             [l2w1[:, c, :] for c in range(NT)])
            mm.then_inc(s["t1_ready"], 1)
            eng.wait_ge(s["t1_taken"], NT)
            for t in range(NT):
                mm = product(bank[7][:, t * DH:(t + 1) * DH], [CT[:, c, t * P:(t + 1) * P] for c in range(NT)],
                             [t1[:, c, :] for c in range(NT)])
            mm.then_inc(s["a1_ready"], 1)
            eng.wait_ge(s["t2_done"], NT)
            for c in range(NT):
                eng.matmul(bank[3][0:DH, c * P:(c + 1) * P], t2[:, c, :], ident[:, :],
                           start=(c == 0), stop=False, skip_group_check=True)
            for c in range(NT):
                mm = eng.matmul(bank[3][0:DH, :], t2[:, c, :], CT[:, c, :], start=False, stop=(c == NT - 1),
                                skip_group_check=True)
            mm.then_inc(s["a2_ready"], 1)
            eng.wait_ge(s["a2_taken"], 1)
            for t in range(NT):
                if t == 2:
                    eng.wait_ge(s["a1_sum"], NT)
                eng.matmul(bank[4 + t][:, :], a2[:, t * P:(t + 1) * P], l2w2[:, :], start=True, stop=True).then_inc(s["o2_ready"], 1)

            eng.wait_ge(s["wx_in"], 16 * LAYERS)
            eng.wait_ge(s["we_in"], 32 * LAYERS)
            eng.wait_ge(s["x3_ready"], NT)
            with eng.Fori(0, LAYERS) as l:
                eng.wait_ge(s["m_h"], NT * l + NT)
                for f in range(NT):
                    product(bank[f][:, :], [h[:, c, f * P:(f + 1) * P] for c in range(NT)],
                            [CT[:, c, :] for c in range(NT)]).then_inc(s["m_agg"], 1)
                eng.wait_ge(s["m_taken"], NT * l + NT)
                for t in range(NT):
                    product(bank[4 + t][:, :],
                            [hT[:, c, t * P:(t + 1) * P] for c in range(NT)] + [EAT[:, t * P:(t + 1) * P]],
                            [wx_flat[:, bass.ds(l * (NT * D) + c * D, D)] for c in range(NT)]
                            + [we_flat[:, bass.ds(l * D, D)]]).then_inc(s["m_msg"], 1)

        @block.vector
        def _(eng):
            eng.wait_ge(s["idx_in"], 32)
            eng.tensor_copy(idx_f[:, :, :], idx_i[:, :, :]).then_inc(s["idx_float"], 1)
            eng.wait_ge(s["idx_float"], 1)
            eng.tensor_reduce(win_f[:, 0:1], idx_f[:, 0, :], AX.X, ALU.min).then_inc(s["win_range"], 1)
            eng.tensor_reduce(win_f[:, 1:2], idx_f[:, 0, :], AX.X, ALU.max).then_inc(s["win_range"], 1)
            eng.wait_ge(s["win_range"], 2)
            eng.tensor_copy(win_v[:, :], win_f[:, :]).then_inc(s["win_value"], 1)
            eng.wait_ge(s["win_value"], 1)
            eng.tensor_scalar(win_i[:, :], win_v[:, :], SHIFT, None, ALU.arith_shift_right).then_inc(s["win_shift"], 1)

            def statistics(k, src, t, before):
                eng.bn_stats(bn_st[:, k, t, :], src[:, t, :]).then_inc(s["ln_stats"], 1)
                eng.wait_ge(s["ln_stats"], before + t + 1)
                eng.nop(nofuse=True)
                eng.bn_aggr(bn_mv[:, k, t, :], bn_st[:, k, t, :]).then_inc(s["ln_mv"], 1)

            def shifts(k, before):
                for t in range(NT):
                    eng.wait_ge(s["ln_rstd"], NT * k + t + 1)
                    eng.wait_ge(s["ln_mv"], NT * k + t + 1)
                    eng.scalar_tensor_tensor(nbias[:, k, t:t + 1], bn_mv[:, k, t, 0:1], -1.0, rstd[:, k, t:t + 1],
                                             ALU.mult, ALU.mult).then_inc(s["ln_nb"], 1)

            eng.wait_ge(s["x_in"], 16)
            for t in range(NT):
                statistics(LN_IN0, xres, t, 0)
            eng.wait_ge(s["idx_T"], 1)
            for to, lo in ((dst_f, 0), (src_f, P), (dst_i, 0), (src_i, P)):
                eng.tensor_copy(to[:, :], bank[6][:, lo:lo + T]).then_inc(s["idx_taken"], 1)
            shifts(LN_IN0, 0)

            eng.wait_ge(s["consts"], 8)
            eng.wait_ge(s["idx_taken"], 4)

            def count(n, q):
                need(eng, s["counted"], n - 1)
                eng.tensor_scalar(oh_src[:, q % 2, :], iota_n[:, :], src_f[:, bass.ds(n, 1)], None, ALU.is_equal
                                  ).then_inc(s["src_hot"], 1)
                eng.tensor_scalar(oh_cnt[:, q % 2, :], iota_n[:, :], dst_f[:, bass.ds(n, 1)], None, ALU.is_equal
                                  ).then_inc(s["dst_hot"], 1)
                eng.wait_ge(s["ea_hi"], n + 1)
                eng.tensor_tensor(e_split[:, q, DE:2 * DE], e_raw[:, q, 0:DE], e_split[:, q, 0:DE].bitcast(f32),
                                  ALU.subtract).then_inc(s["ea_lo"], 1)

            for q in range(4):
                count(q, q)
            with eng.Fori(1, QUADS) as i:
                for q in range(4):
                    count(4 * i + q, q)

            eng.wait_ge(s["bcol_in"], 64)
            eng.wait_ge(s["rows_in"], 16 * 7)
            for n in range(3 * NT):
                eng.wait_ge(s["qkv_ready"], n + 1)
                t, got = n % NT, bank[6 + n % 2][:, :]
                if n < NT:
                    eng.tensor_scalar(qT[:, t, :], got, bcol[:, t:t + 1], HD ** -0.5, ALU.add, ALU.mult).then_inc(s["qkv_taken"], 1)
                elif n < 2 * NT:
                    eng.tensor_scalar(kT[:, t, :], got, bcol[:, NT + t:NT + t + 1], None, ALU.add).then_inc(s["qkv_taken"], 1)
                else:
                    eng.tensor_tensor(v[:, t, :], got, brow[:, BV, :], ALU.add).then_inc(s["qkv_taken"], 1)
            eng.wait_ge(s["deg_ready"], 1)
            eng.tensor_scalar(deg[:, :], bank[5][:, 0:NT], 1.0, None, ALU.add).then_inc(s["deg_taken"], 1)
            for t in range(NT):
                eng.wait_ge(s["cT_ready"], t + 1)
                eng.tensor_scalar(mask[:, t, :], bank[t][:, :], 1.0, None, ALU.min).then_inc(s["mask_ready"], 1)

            def masked(u):
                half, m, k = u // NT, u % NT, u % 2
                need(eng, s["av_done"], u - 1)
                for j in range(4):
                    eng.wait_ge(s["s_ready"], 4 * u + j + 1)
                    hd = 4 * (j // 2) + j % 2
                    eng.tensor_tensor(S[:, k, hd:hd + 3:2, :], bank[j][:, :].rearrange("p (i n) -> p i n", i=2),
                                      mask[:, m, half * HALF:(half + 1) * HALF].unsqueeze(1).to_broadcast([P, 2, HALF]),
                                      ALU.mult).then_inc(s["s_masked"], 1)
                eng.wait_ge(s["s_masked"], 4 * u + 4)
                need(eng, s["s_sub"], u)
                eng.tensor_reduce(smx[:, :], S[:, k, :, :].rearrange("p h n -> p n h"), AX.X, ALU.max).then_inc(s["s_max"], 1)
                eng.wait_ge(s["s_max"], u + 1)
                eng.tensor_tensor(S[:, k, :, :], S[:, k, :, :], smx[:, :].unsqueeze(1).to_broadcast([P, HEADS, HALF]),
                                  ALU.subtract).then_inc(s["s_sub"], 1)

            def weights(u):
                k = u % 2
                eng.wait_ge(s["s_rec"], u + 1)
                eng.tensor_tensor(S[:, k, :, :], S[:, k, :, :], ssm[:, k, :].unsqueeze(1).to_broadcast([P, HEADS, HALF]),
                                  ALU.mult).then_inc(s["att_ready"], 1)

            eng.wait_ge(s["mask_ready"], NT)
            eng.wait_ge(s["ea_out"], 16 * QUADS)
            for u in range(2 * NT):
                k = u % 2
                masked(u)
                if u:
                    weights(u - 1)
                eng.wait_ge(s["s_exp"], u + 1)
                need(eng, s["att_ready"], u - 1)
                eng.tensor_reduce(ssm[:, k, :], S[:, k, :, :].rearrange("p h n -> p n h"), AX.X, ALU.add).then_inc(s["s_sum"], 1)
            weights(2 * NT - 1)

            def plus_row(k, done):
                for t in range(NT):
                    eng.tensor_tensor(h[:, t, :], h[:, t, :], brow[:, k, :], ALU.add).then_inc(done, 1)

            eng.wait_ge(s["hT_ready"], NT)
            plus_row(BO, s["hb_done"])
            eng.wait_ge(s["hb_done"], NT)
            for t in range(NT):
                eng.wait_ge(s["wo_ready"], t + 1)
                eng.tensor_tensor(y[:, t, :], bank[t][:, :], h[:, t, :], ALU.add).then_inc(s["y1_ready"], 1)
                eng.wait_ge(s["y1_ready"], t + 1)
                statistics(LN_A, y, t, NT * LN_A)

            def normalize(k, t, before, gain, shift_row, to, shifted):
                eng.wait_ge(s["ln_rstd"], NT * k + t + 1)
                eng.wait_ge(s["ln_mv"], NT * k + t + 1)
                eng.tensor_scalar(y[:, t, :], y[:, t, :], bn_mv[:, k, t, 0:1], rstd[:, k, t:t + 1],
                                  ALU.subtract, ALU.mult).then_inc(s["y_norm"], 1)
                eng.wait_ge(s["y_norm"], NT * before + t + 1)
                eng.tensor_tensor(y[:, t, :], y[:, t, :], brow[:, gain, :], ALU.mult).then_inc(s["y_scaled"], 1)
                eng.wait_ge(s["y_scaled"], NT * before + t + 1)
                eng.tensor_tensor(to[:, t, :], y[:, t, :], brow[:, shift_row, :], ALU.add).then_inc(shifted, 1)

            for t in range(NT):
                normalize(LN_A, t, 0, G1, BE1, h, s["h_ready"])
            eng.wait_ge(s["hT_ready"], 2 * NT)
            eng.wait_ge(s["h_ready"], 2 * NT)
            plus_row(B2, s["hb2_done"])

            eng.wait_ge(s["w1chi_done"], 1)
            eng.tensor_tensor(w1c_lo[:, :], w1c_raw[0:DE, :], w1c_hi[0:DE, :].bitcast(f32), ALU.subtract).then_inc(s["w1clo_done"], 1)
            for t in range(NT):
                eng.wait_ge(s["w2hi_done"], t + 1)
                eng.tensor_tensor(w2_lo[:, t, :], slot(2)[:, t, :], w2_hi[:, t, :].bitcast(f32), ALU.subtract).then_inc(s["w2lo_done"], 1)
            eng.wait_ge(s["b2_in"], 32)
            eng.tensor_copy(b2_rows[0:1, :], b2_raw[0:1, :]).then_inc(s["b2_done"], 1)
            eng.tensor_copy(b2_rows[32:33, :], b2_raw[32:33, :]).then_inc(s["b2_done"], 1)
            eng.wait_ge(s["b2_done"], 2)
            eng.tensor_tensor(b2_rows[32:33, :], b2_raw[32:33, :], b2_rows[32:33, :].bitcast(f32), ALU.subtract).then_inc(s["b2_done"], 1)

            eng.wait_ge(s["hb2_done"], NT)
            for t in range(NT):
                eng.wait_ge(s["ff2_ready"], t + 1)
                eng.tensor_tensor(y[:, t, :], bank[4 + t][:, :], h[:, t, :], ALU.add).then_inc(s["y2_ready"], 1)
                eng.wait_ge(s["y2_ready"], t + 1)
                statistics(LN_B, y, t, NT * LN_B)
            for t in range(NT):
                normalize(LN_B, t, 1, G2, BE2, y, s["y_shifted"])
                eng.wait_ge(s["y_shifted"], t + 1)
                eng.wait_ge(s["h_ready"], t + 1)
                eng.tensor_tensor(xres[:, t, :], xres[:, t, :], y[:, t, :], ALU.add).then_inc(s["x1_ready"], 1)
                eng.wait_ge(s["x1_ready"], t + 1)
                statistics(LN_IN1, xres, t, NT * LN_IN1)
            shifts(LN_IN1, 1)
            eng.wait_ge(s["rows1_in"], 16 * 5)
            for t in range(NT):
                eng.wait_ge(s["tab_ready"], t + 1)
                eng.tensor_tensor(y[:, t, :], bank[t][:, :], brow[:, B1, :], ALU.add).then_inc(s["ptab_taken"], 1)
            plus_row(B4, s["hb4_done"])

            def step(n, q, first=True, second=True, finish=True):
                p = q % 2
                if first:
                    eng.wait_ge(s["expA"], n + 1)
                    eng.tensor_scalar(eA[:, p, :], eA[:, p, :], TOP, None, ALU.min).then_inc(s["topA"], 1)
                    eng.wait_ge(s["topA"], n + 1)
                    need(eng, s["mishA"], n - 1)
                    eng.scalar_tensor_tensor(uA[:, p, :], eA[:, p, :], 2.0, eA[:, p, :], ALU.add, ALU.mult).then_inc(s["sqA"], 1)
                if finish:
                    k = 1 - p
                    eng.wait_ge(s["recB"], n - 2)
                    need(eng, s["scattered"], n - 4)
                    eng.scalar_tensor_tensor(mB[:, k, :], uB[:, 1 - p, :], 1.0, bank[3 - p][:, :], ALU.subtract, ALU.mult,
                                             reverse0=True).then_inc(s["mishB"], 1)
                    eng.tensor_scalar(oh[:, k, :], iota_n[:, :], dst_f[:, bass.ds(n - 3, 1)], None, ALU.is_equal
                                      ).then_inc(s["hotB"], 1)
                if first:
                    eng.wait_ge(s["recA"], n + 1)
                    need(eng, s["hiA"], n - 1)
                    need(eng, s["loA"], n - 1)
                    eng.scalar_tensor_tensor(mA[:, p, :], uA[:, p, :], 1.0, bank[p][:, :], ALU.subtract, ALU.mult,
                                             reverse0=True).then_inc(s["mishA"], 1)
                if second:
                    eng.wait_ge(s["expB"], n - 1)
                    eng.tensor_scalar(eB[:, p, :], eB[:, p, :], TOP, None, ALU.min).then_inc(s["topB"], 1)
                    eng.wait_ge(s["topB"], n - 1)
                    need(eng, s["mishB"], n - 3)
                    eng.scalar_tensor_tensor(uB[:, p, :], eB[:, p, :], 2.0, eB[:, p, :], ALU.add, ALU.mult).then_inc(s["sqB"], 1)
                if first:
                    hi = h_hi[:, q // 2, 2 * p:2 * p + 2, :]
                    eng.wait_ge(s["hiA"], n + 1)
                    eng.wait_ge(s["mishA"], n + 1)
                    need(eng, s["preB"], n - p - 2)
                    eng.tensor_tensor(h_lo[:, q // 2, 2 * p:2 * p + 2, :], mA[:, p, :].rearrange("p (c e) -> p c e", c=2),
                                      hi.bitcast(f32), ALU.subtract).then_inc(s["loA"], 1)

            for n in range(8):
                step(n, n % 4, second=n >= 2, finish=n >= 3)
            with eng.Fori(2, QUADS) as i:
                for q in range(4):
                    step(4 * i + q, q)
            for n in range(T, T + 3):
                step(n, n % 4, first=False, second=n < T + 2)

            def finish_u(f):
                eng.wait_ge(s["u_rec"], f + 1)
                eng.wait_ge(s["u_x"], f + 1)
                eng.scalar_tensor_tensor(qT[:, f, :], v[:, f, :], 1.0, kT[:, f, :], ALU.subtract, ALU.mult,
                                         reverse0=True).then_inc(s["u_mish"], 1)

            for f in range(NT):
                eng.wait_ge(s["u_ready"], f + 1)
                eng.wait_ge(s["u_exp"], f + 1)
                eng.tensor_scalar(kT[:, f, :], bank[f][:, :], bcol[:, 16 + f:17 + f], None, ALU.add).then_inc(s["u_x"], 1)
                eng.tensor_scalar(v[:, f, :], v[:, f, :], TOP, None, ALU.min).then_inc(s["u_top"], 1)
                eng.wait_ge(s["u_top"], f + 1)
                eng.scalar_tensor_tensor(v[:, f, :], v[:, f, :], 2.0, v[:, f, :], ALU.add, ALU.mult).then_inc(s["u_sq"], 1)
                if f:
                    finish_u(f - 1)
            finish_u(NT - 1)
            eng.wait_ge(s["hb4_done"], NT)
            for t in range(NT):
                eng.wait_ge(s["w4_ready"], t + 1)
                eng.tensor_tensor(y[:, t, :], bank[4 + t][:, :], h[:, t, :], ALU.add).then_inc(s["y4_ready"], 1)
                eng.wait_ge(s["y4_ready"], t + 1)
                statistics(LN_C, y, t, NT * LN_C)
            for t in range(NT):
                normalize(LN_C, t, 2, GAMMA, BETA, y, s["y_shifted"])
                eng.wait_ge(s["y_shifted"], NT + t + 1)
                eng.tensor_tensor(xres[:, t, :], xres[:, t, :], y[:, t, :], ALU.add).then_inc(s["x2_ready"], 1)
                eng.wait_ge(s["x2_ready"], t + 1)
                statistics(LN_IN2, xres, t, NT * LN_IN2)
            shifts(LN_IN2, 2)

            for t in range(NT):
                eng.wait_ge(s["h_ready"], 3 * NT + t + 1)
                eng.tensor_tensor(xres[:, t, :], xres[:, t, :], brow[:, L2B2, :], ALU.add).then_inc(s["xb2_done"], 1)
            eng.wait_ge(s["l2_in"], 48)
            eng.wait_ge(s["dinv_ready"], 1)
            eng.wait_ge(s["t1_ready"], 1)
            for t in range(NT):
                eng.tensor_scalar(t1[:, t, :], bank[6][:, t * DH:(t + 1) * DH], dinv[:, t:t + 1], None, ALU.mult).then_inc(s["t1_taken"], 1)
            eng.wait_ge(s["t1_taken"], NT)
            eng.wait_ge(s["a1_ready"], 1)
            for t in range(NT):
                eng.tensor_tensor(t2[:, t, :], bank[7][:, t * DH:(t + 1) * DH], t1[:, t, :], ALU.add).then_inc(s["a1_sum"], 1)
            for t in range(NT):
                eng.wait_ge(s["a1_sum"], t + 1)
                eng.scalar_tensor_tensor(t2[:, t, :], t2[:, t, :], dinv[:, t:t + 1], l2b1[:, :], ALU.mult, ALU.add).then_inc(s["a1_bias"], 1)
            for t in range(NT):
                eng.wait_ge(s["a1_bias"], t + 1)
                eng.tensor_scalar(t2[:, t, :], t2[:, t, :], 0.0, dinv[:, t:t + 1], ALU.max, ALU.mult).then_inc(s["t2_done"], 1)
            for t in range(NT):
                eng.wait_ge(s["o2_ready"], t + 1)
                eng.wait_ge(s["xb2_done"], t + 1)
                eng.scalar_tensor_tensor(xres[:, t, :], bank[4 + t][:, :], dinv[:, t:t + 1], xres[:, t, :],
                                         ALU.mult, ALU.add).then_inc(s["x3_ready"], 1)
                eng.wait_ge(s["x3_ready"], t + 1)
                statistics(LN_IN3, xres, t, NT * LN_IN3)
            shifts(LN_IN3, 3)

            eng.wait_ge(s["affine_in"], 32 * LAYERS)
            with eng.Fori(0, LAYERS) as l:
                for t in range(NT):
                    eng.wait_ge(s["m_h"], NT * l + t + 1)
                    eng.wait_ge(s["m_msg"], NT * l + t + 1)
                    eng.tensor_tensor(y[:, t, :], bank[4 + t][:, :], h[:, t, :], ALU.add).then_inc(s["m_y"], 1)
                    eng.wait_ge(s["m_y"], NT * l + t + 1)
                    statistics(LN_L3, y, t, NT * l + NT * LN_L3)
                for t in range(NT):
                    eng.wait_ge(s["ln_rstd"], NT * l + (NT * LN_L3 + t + 1))
                    eng.tensor_scalar(y[:, t, :], y[:, t, :], bn_mv[:, LN_L3, t, 0:1], rstd[:, LN_L3, t:t + 1],
                                      ALU.subtract, ALU.mult).then_inc(s["m_norm"], 1)
                    eng.wait_ge(s["m_norm"], NT * l + t + 1)
                    eng.tensor_tensor(y[:, t, :], y[:, t, :], WA[:, 0, bass.ds(l * D, D)], ALU.mult).then_inc(s["m_scaled"], 1)
                    eng.wait_ge(s["m_scaled"], NT * l + t + 1)
                    eng.tensor_tensor(y[:, t, :], y[:, t, :], WA[:, 1, bass.ds(l * D, D)], ALU.add).then_inc(s["m_shifted"], 1)
            for t in range(NT):
                eng.wait_ge(s["m_h"], NT * LAYERS + t + 1)
                eng.tensor_tensor(y[:, t, :], xres[:, t, :], h[:, t, :], ALU.add).then_inc(s["result"], 1)


_INS = """x src dst edge_attr_64 L0_gnn_Wq L0_gnn_bq L0_gnn_Wk L0_gnn_bk L0_gnn_Wv L0_gnn_bv L0_gnn_Wo L0_gnn_bo
L0_gnn_W1 L0_gnn_b1 L0_gnn_W2 L0_gnn_b2 L0_gnn_g1 L0_gnn_be1 L0_gnn_g2 L0_gnn_be2
L1_gnn_W1 L1_gnn_b1 L1_gnn_W2 L1_gnn_b2 L1_gnn_W3 L1_gnn_b3 L1_gnn_W4 L1_gnn_b4 L1_gnn_gamma L1_gnn_beta
L2_gnn_W1 L2_gnn_b1 L2_gnn_W2 L2_gnn_b2 L3_gnn_Ws L3_gnn_bs L3_gnn_gammas L3_gnn_betas""".split()


def kernel(**inputs):
    import numpy as np
    import concourse.bacc as bacc
    from concourse.bass_utils import run_bass_kernel_spmd

    nc = bacc.Bacc("TRN2", target_bir_lowering=False, num_devices=1)
    arrays, ins = {}, {}
    for name in _INS:
        a = np.ascontiguousarray(inputs[name])
        arrays[f"in_{name}"] = a
        ins[name] = nc.dram_tensor(f"in_{name}", a.shape, mybir.dt.from_np(a.dtype), kind="ExternalInput").ap()
    out = nc.dram_tensor("out_x", inputs["x"].shape, mybir.dt.float32, kind="ExternalOutput").ap()
    gnn_stack_kernel(nc, ins, out)
    return run_bass_kernel_spmd(nc, [arrays], core_ids=[0]).results[0]["out_x"]
```

```python
from contextlib import ExitStack

import concourse.bass as bass
from concourse import mybir


def gnn_stack_kernel(nc, ins, out):
    f32, f32r, bf16, i32 = mybir.dt.float32, mybir.dt.float32r, mybir.dt.bfloat16, mybir.dt.int32
    ALU, ACT, AX = mybir.AluOpType, mybir.ActivationFunctionType, mybir.AxisListType

    N, D = ins["x"].shape
    E, DE = ins["edge_attr_64"].shape
    P = 128
    NT = N // P
    T = E // P
    HEADS = 8
    HD = D // HEADS
    FT = ins["L0_gnn_W1"].shape[1] // P
    DH = ins["L2_gnn_W1"].shape[1]
    LAYERS = ins["L3_gnn_Ws"].shape[0]
    EPS = 1e-5
    SHIFT = 6
    WIN = 1 << SHIFT
    HALF = N // 2
    TOP = 1e8
    QUADS = T // 4
    assert N == D == 512 and T % 4 == 0 and 2 * DE == P and FT == 2 * NT

    ctx = ExitStack()
    with ctx:
        def sb(name, shape, dt=f32, to=ctx):
            return to.enter_context(nc.sbuf_tensor(name, shape, dt))

        src_table = nc.dram_tensor("src_table", (N, D), f32, kind="Internal").ap()
        dst_table = nc.dram_tensor("dst_table", (N, D), f32, kind="Internal").ap()
        eaT_dram = nc.dram_tensor("eaT_dram", (P, E), f32, kind="Internal").ap()

        ident = sb("ident", [P, P])
        iota_n = sb("iota_n", [P, N])
        ones = sb("ones", [P, 1])
        zrow = sb("zrow", [1, N], bf16)
        eps_c = sb("eps_c", [P, 1])
        dst_f = sb("dst_f", [P, T])
        src_f = sb("src_f", [P, T])
        dst_i = sb("dst_i", [P, T], i32)
        src_i = sb("src_i", [P, T], i32)
        idx_now = sb("idx_now", [P, 2, 4], i32)
        win_f = sb("win_f", [T, 2])
        win_v = sb("win_v", [T, 2], i32)
        win_i = sb("win_i", [T, 2], i32)
        win = sb("win", [1, 2 * T], i32)
        xres = sb("xres", [P, NT, D])
        h = sb("h", [P, NT, D])
        hT = sb("hT", [P, NT, N])
        CT = sb("CT", [P, NT, N])
        EAT = sb("EAT", [DE + 1, N])
        deg = sb("deg", [P, NT])
        dlog = sb("dlog", [P, NT])
        dinv = sb("dinv", [P, NT])
        bcol = sb("bcol", [P, 20])
        bn_st = sb("bn_st", [P, 8, NT, 6])
        bn_mv = sb("bn_mv", [P, 8, NT, 2])
        lnv = sb("lnv", [P, 8, NT])
        rstd = sb("rstd", [P, 8, NT])
        nbias = sb("nbias", [P, 8, NT])
        WA = sb("WA", [P, 8, NT * D])
        brow = sb("brow", [P, 7, D])
        w1c_hi = sb("w1c_hi", [P, D], f32r)
        w1c_lo = sb("w1c_lo", [DE, D], f32r)
        b2_rows = sb("b2_rows", [P, D], f32r)
        ones_r = sb("ones_r", [P, P], f32r)
        w2_hi = sb("w2_hi", [P, NT, D], f32r)
        w2_lo = sb("w2_lo", [P, NT, D], f32r)
        l2w1 = sb("l2w1", [P, NT, DH])
        l2w2 = sb("l2w2", [DH, D])
        l2b1 = sb("l2b1", [P, DH])
        t1 = sb("t1", [P, NT, DH])
        t2 = sb("t2", [P, NT, DH])
        a2 = sb("a2", [DH, N])

        wx_flat = WA[:, 5:8, :].rearrange("p l w -> p (l w)")
        we_flat = WA[0:DE + 1, 3, :]

        def slot(k):
            return WA[:, k, :].rearrange("p (t d) -> p t d", d=D)

        with ExitStack() as a:
            y = sb("y", [P, NT, D], to=a)
            mask = sb("mask", [P, NT, N], to=a)
            qT = sb("qT", [P, NT, N], to=a)
            kT = sb("kT", [P, NT, N], to=a)
            v = sb("v", [P, NT, D], to=a)
            S = sb("S", [P, 2, HEADS, HALF], to=a)
            smx = sb("smx", [P, HALF], to=a)
            ssm = sb("ssm", [P, 2, HALF], to=a)
        ea_sums = y[:, 0, :]
        w1c_raw = mask[:, 0, :]
        b2_raw = mask[0:33, 1, :]
        with ExitStack() as a:
            sb("unused_by_counting", [P, 5, NT * D], to=a)
            idx_i = sb("idx_i", [T, 2, P], i32, to=a)
            idx_f = sb("idx_f", [T, 2, P], to=a)
            e_raw = sb("e_raw", [P, 4, DE], to=a)
            e_split = sb("e_split", [P, 4, P], f32r, to=a)
            oh_src = sb("oh_src", [P, 2, N], f32r, to=a)
            oh_cnt = sb("oh_cnt", [P, 2, N], f32r, to=a)
            eaT_out = sb("eaT_out", [P, 4 * P], to=a)
        with ExitStack() as a:
            G = sb("G", [P, 4, D], to=a)
            h_hi = sb("h_hi", [P, 2, NT, 2 * P], f32r, to=a)
            h_lo = sb("h_lo", [P, 2, NT, 2 * P], f32r, to=a)
            eaT = sb("eaT", [P, 2, 2 * P], f32r, to=a)
            eA = sb("eA", [P, 2, D], to=a)
            uA = sb("uA", [P, 2, D], to=a)
            mA = sb("mA", [P, 2, D], to=a)
            eB = sb("eB", [P, 2, D], to=a)
            uB = sb("uB", [P, 2, D], to=a)
            mB = sb("mB", [P, 2, D], to=a)
            oh = sb("oh", [P, 2, N], to=a)

        bank = [ctx.enter_context(nc.psum_tensor(f"bank{i}", [P, 512], f32)) for i in range(8)]

        s = {name: ctx.enter_context(nc.semaphore(name)) for name in """
            consts ident_done idx_in idx_float idx_T idx_taken win_range win_value win_shift win_row
            x_in wq_in wk_in wv_in wo_in f1_in f2_in bcol_in
            rows_in
            w1a_in w1b_in w2_in w3_in w4_in wx_in affine_in we_in l2_in b2_in w1c_in
            rows1_in
            ea_in0 ea_in1 ea_hi ea_lo src_hot dst_hot counted ea_evac ea_out
            counts ct_taken cT_ready mask_ready deg_ready deg_taken dlog_done dinv_ready
            ln_stats ln_mv ln_log ln_rstd ln_nb h_ready hT_ready hT_taken
            qkv_ready qkv_taken w2hi_done w2lo_done w1chi_done w1clo_done b2_done
            s_ready s_masked s_max s_sub s_exp s_sum s_log s_rec att_ready av_done av_taken
            eat_ready eat_taken hb_done wo_ready y1_ready y_scaled hb2_done ff1_ready ff1_taken ff2_ready y2_ready
            x1_ready
            tab_ready ptab_taken qtab_taken src_stored dst_stored idx_now_set gath0 gath1 eaT0 eaT1
            preA expA topA sqA logA recA mishA hiA loA
            preB expB topB sqB logB recB mishB hotB scattered
            agg_ready agg_taken hb4_done u_ready u_x u_exp u_top u_sq u_log u_rec u_mish
            w4_ready y4_ready x2_ready
            t1_ready t1_taken a1_ready a1_sum a1_bias t2_done a2_ready a2_taken xb_done
            o2_ready x3_ready
            m_agg m_taken m_msg m_y m_shifted m_h result stored
            """.split()}

        block = ctx.enter_context(nc.Block())

        def need(eng, semaphore, value):
            if not isinstance(value, int) or value > 0:
                eng.wait_ge(semaphore, value)

        def rows(ap):
            return ap.rearrange("(t p) d -> p t d", p=P)

        def spread(name):
            return ins[name].rearrange("(a d) -> a d", a=1).to_broadcast([P, D])

        def ws(w):
            return bass.ds(w * WIN, WIN)

        BV, BO, G1, BE1, B2, G2, BE2 = range(7)
        B1, B4, GAMMA, BETA, L2B2 = range(5)
        LN_IN0, LN_A, LN_B, LN_IN1, LN_C, LN_IN2, LN_IN3, LN_L3 = range(8)

        ORDER = [(k, t) for k in (LN_IN0, LN_A) for t in range(NT)]
        for k, after in ((LN_B, LN_IN1), (LN_C, LN_IN2)):
            for t in range(NT + 1):
                ORDER += [(k, t)] * (t < NT) + [(after, t - 1)] * (t > 0)
        ORDER += [(k, t) for k in (LN_IN3, LN_L3) for t in range(NT)]

        def nth(k, t):
            return ORDER.index((k, t)) + 1

        @block.sync
        def _(eng):
            eng.dma_start(idx_i[:, 0, :], ins["dst"].rearrange("(t p) -> t p", p=P)).then_inc(s["idx_in"], 16)
            eng.dma_start(idx_i[:, 1, :], ins["src"].rearrange("(t p) -> t p", p=P)).then_inc(s["idx_in"], 16)
            eng.dma_start(xres[:, :, :], rows(ins["x"])).then_inc(s["x_in"], 16)

            pairs = ins["edge_attr_64"].rearrange("(g j p) d -> g p j d", j=2, p=P)

            def load_pair(pair, k, loaded):
                eng.dma_start(e_raw[:, 2 * k:2 * k + 2, :], pairs[bass.ds(pair, 1), :, :, :]
                              .rearrange("g p j d -> (g p) j d")).then_inc(loaded, 16)

            def store_quad(i):
                eng.wait_ge(s["ea_evac"], i + 1)
                eng.dma_start(eaT_dram[:, bass.ds(i * (4 * P), 4 * P)], eaT_out[:, :]).then_inc(s["ea_out"], 16)

            load_pair(0, 0, s["ea_in0"])
            load_pair(1, 1, s["ea_in1"])
            eng.wait_ge(s["win_shift"], 1)
            eng.dma_start(win[0:1, :], win_i[:, :]).then_inc(s["win_row"], 16)
            with eng.Fori(0, QUADS - 1) as i:
                eng.wait_ge(s["counted"], 4 * i + 2)
                load_pair(2 * i + 2, 0, s["ea_in0"])
                eng.wait_ge(s["counted"], 4 * i + 4)
                load_pair(2 * i + 3, 1, s["ea_in1"])
                store_quad(i)
            store_quad(QUADS - 1)

            w1 = ins["L1_gnn_W1"]
            eng.wait_ge(s["qkv_ready"], NT)
            eng.dma_start(slot(0), rows(w1[0:D, :])).then_inc(s["w1a_in"], 16)
            eng.wait_ge(s["qkv_ready"], 2 * NT)
            eng.dma_start(slot(1), rows(w1[D:2 * D, :])).then_inc(s["w1b_in"], 16)
            eng.wait_ge(s["qkv_ready"], 3 * NT)
            eng.dma_start(slot(2), rows(ins["L1_gnn_W2"])).then_inc(s["w2_in"], 16)
            eng.wait_ge(s["qkv_taken"], 3 * NT)
            eng.dma_start(brow[:, B1, :], spread("L1_gnn_b1")).then_inc(s["rows1_in"], 16)
            eng.wait_ge(s["hb_done"], NT)
            eng.dma_start(brow[:, B4, :], spread("L1_gnn_b4")).then_inc(s["rows1_in"], 16)
            eng.wait_ge(s["h_ready"], 2 * NT)
            eng.dma_start(brow[:, GAMMA, :], spread("L1_gnn_gamma")).then_inc(s["rows1_in"], 16)
            eng.dma_start(brow[:, BETA, :], spread("L1_gnn_beta")).then_inc(s["rows1_in"], 16)
            eng.wait_ge(s["ff1_ready"], FT)
            for c in range(2):
                eng.dma_start(slot(3 + c), rows(ins["L1_gnn_W3"][c * D:(c + 1) * D, :])).then_inc(s["w3_in"], 16)
            eng.wait_ge(s["hb2_done"], NT)
            eng.dma_start(brow[:, L2B2, :], spread("L2_gnn_b2")).then_inc(s["rows1_in"], 16)
            eng.wait_ge(s["w2lo_done"], NT)
            eng.dma_start(slot(2), rows(ins["L1_gnn_W4"])).then_inc(s["w4_in"], 16)
            eng.wait_ge(s["ff2_ready"], NT)
            for l in range(LAYERS):
                eng.dma_start(slot(5 + l), rows(ins["L3_gnn_Ws"][l, 0:D, :])).then_inc(s["wx_in"], 16)

            for t in range(NT):
                eng.wait_ge(s["ptab_taken"], t + 1)
                eng.dma_start(src_table[t * P:(t + 1) * P, :], y[:, t, :]).then_inc(s["src_stored"], 16)
            for t in range(NT):
                eng.wait_ge(s["qtab_taken"], t + 1)
                eng.dma_start(dst_table[t * P:(t + 1) * P, :], v[:, t, :]).then_inc(s["dst_stored"], 16)
            for l in range(LAYERS):
                eng.dma_start(WA[:, 0, l * D:(l + 1) * D], ins["L3_gnn_gammas"][l:l + 1, :].to_broadcast([P, D])).then_inc(s["affine_in"], 16)
                eng.dma_start(WA[:, 1, l * D:(l + 1) * D], ins["L3_gnn_betas"][l:l + 1, :].to_broadcast([P, D])).then_inc(s["affine_in"], 16)

            def load_group(g, k, loaded):
                eng.dma_start(eaT[:, k, :].bitcast(f32), eaT_dram[:, bass.ds(g * (2 * P), 2 * P)]).then_inc(loaded, 16)

            eng.wait_ge(s["src_stored"], 16 * NT)
            eng.wait_ge(s["dst_stored"], 16 * NT)
            eng.wait_ge(s["ea_out"], 16 * QUADS)
            load_group(0, 0, s["eaT0"])
            load_group(1, 1, s["eaT1"])
            with eng.Fori(0, QUADS - 1) as i:
                eng.wait_ge(s["preA"], 4 * i + 2)
                load_group(2 * i + 2, 0, s["eaT0"])
                eng.wait_ge(s["preA"], 4 * i + 4)
                load_group(2 * i + 3, 1, s["eaT1"])

            eng.wait_ge(s["u_ready"], NT)
            for l in range(LAYERS):
                eng.dma_start(we_flat[0:DE, l * D:(l + 1) * D], ins["L3_gnn_Ws"][l, D:D + DE, :]).then_inc(s["we_in"], 16)
                eng.dma_start(we_flat[DE:DE + 1, l * D:(l + 1) * D], ins["L3_gnn_bs"][l:l + 1, :]).then_inc(s["we_in"], 16)
            for t in range(NT):
                eng.wait_ge(s["result"], t + 1)
                eng.dma_start(out[t * P:(t + 1) * P, :], y[:, t, :]).then_inc(s["stored"], 16)
            eng.wait_ge(s["stored"], 16 * NT)

        @block.gpsimd
        def _(eng):
            eng.memset(ident[:, :], 0.0).then_inc(s["consts"], 1)
            eng.iota(iota_n[:, :], pattern=[[1, N]], base=0, channel_multiplier=0,
                     allow_small_or_imprecise_dtypes=True).then_inc(s["consts"], 1)
            eng.memset(ones[:, :], 1.0).then_inc(s["consts"], 1)
            eng.memset(zrow[:, :], 0.0).then_inc(s["consts"], 1)
            eng.memset(eps_c[:, :], EPS).then_inc(s["consts"], 1)
            eng.memset(ones_r[:, :].bitcast(f32), 1.0).then_inc(s["consts"], 1)
            eng.memset(b2_rows[:, :].bitcast(f32), 0.0).then_inc(s["consts"], 1)
            eng.wait_ge(s["consts"], 7)
            eng.affine_select(out=ident[:, :], in_=ident[:, :], compare_op=ALU.not_equal, fill=1.0, base=0,
                              pattern=[[-1, P]], channel_multiplier=1).then_inc(s["ident_done"], 1)
            eng.wait_ge(s["counted"], 8)
            eng.dma_start(slot(3), rows(ins["L0_gnn_Wo"])).then_inc(s["wo_in"], 16)
            for c in range(2):
                eng.dma_start(slot(4 + c), rows(ins["L0_gnn_W1"][:, c * D:(c + 1) * D])).then_inc(s["f1_in"], 16)
            for c in range(2):
                eng.dma_start(slot(6 + c), rows(ins["L0_gnn_W2"][c * D:(c + 1) * D, :])).then_inc(s["f2_in"], 16)
            eng.dma_start(l2w1[:, :, :], rows(ins["L2_gnn_W1"])).then_inc(s["l2_in"], 16)
            eng.dma_start(l2w2[:, :], ins["L2_gnn_W2"]).then_inc(s["l2_in"], 16)
            eng.dma_start(l2b1[:, :], ins["L2_gnn_b1"].rearrange("(a d) -> a d", a=1).to_broadcast([P, DH])).then_inc(s["l2_in"], 16)

            eng.wait_ge(s["s_masked"], 2 * NT * 4)
            for half in range(2):
                eng.dma_start(w1c_raw[half * DE:(half + 1) * DE, :], ins["L1_gnn_W1"][2 * D:2 * D + DE, :]).then_inc(s["w1c_in"], 16)
                eng.dma_start(b2_raw[32 * half:32 * half + 1, :], ins["L1_gnn_b2"].rearrange("(a d) -> a d", a=1)).then_inc(s["b2_in"], 16)

            eng.wait_ge(s["src_stored"], 16 * NT)
            eng.wait_ge(s["dst_stored"], 16 * NT)
            eng.wait_ge(s["idx_taken"], 4)

            def gather(g, k, gathered, before):
                eng.tensor_copy(idx_now[:, k, 0:2], src_i[:, bass.ds(2 * g, 2)]).then_inc(s["idx_now_set"], 1)
                eng.tensor_copy(idx_now[:, k, 2:4], dst_i[:, bass.ds(2 * g, 2)]).then_inc(s["idx_now_set"], 1)
                eng.wait_ge(s["idx_now_set"], 2 * g + 2)
                eng.nop(nofuse=True)
                for j in range(2):
                    eng.indirect_dma_start(out=G[:, 2 * k + j, :], out_offset=None, in_=src_table,
                                           in_offset=bass.IndirectOffsetOnAxis(ap=idx_now[:, k, j:j + 1], axis=0)
                                           ).then_inc(gathered, 16)
                eng.wait_ge(gathered, 64 * before + 32)
                eng.nop(nofuse=True)
                for j in range(2):
                    eng.indirect_dma_start(out=G[:, 2 * k + j, :], out_offset=None, in_=dst_table,
                                           in_offset=bass.IndirectOffsetOnAxis(ap=idx_now[:, k, 2 + j:3 + j], axis=0),
                                           compute_op=ALU.add).then_inc(gathered, 16)

            gather(0, 0, s["gath0"], 0)
            gather(1, 1, s["gath1"], 0)
            with eng.Fori(0, QUADS - 1) as i:
                eng.wait_ge(s["preA"], 4 * i + 2)
                gather(2 * i + 2, 0, s["gath0"], i + 1)
                eng.wait_ge(s["preA"], 4 * i + 4)
                gather(2 * i + 3, 1, s["gath1"], i + 1)

        @block.scalar
        def _(eng):
            eng.preload_act_table_set("natural_log_exp_and_others")
            eng.dma_start(slot(0), rows(ins["L0_gnn_Wq"])).then_inc(s["wq_in"], 16)
            eng.dma_start(slot(1), rows(ins["L0_gnn_Wk"])).then_inc(s["wk_in"], 16)
            eng.dma_start(slot(2), rows(ins["L0_gnn_Wv"])).then_inc(s["wv_in"], 16)
            for name, lo, n in (("L0_gnn_bq", 0, 4), ("L0_gnn_bk", 4, 4), ("L0_gnn_b1", 8, 8), ("L1_gnn_b3", 16, 4)):
                eng.dma_start(bcol[:, lo:lo + n], ins[name].rearrange("(c p) -> p c", p=P),
                              allow_slow_non_contiguous=True).then_inc(s["bcol_in"], 16)
            for name, k in (("bv", BV), ("bo", BO), ("g1", G1), ("be1", BE1), ("b2", B2), ("g2", G2), ("be2", BE2)):
                eng.dma_start(brow[:, k, :], spread("L0_gnn_" + name)).then_inc(s["rows_in"], 16)
            eng.wait_ge(s["consts"], 7)

            def inverse_deviation(k, t, later=0):
                eng.wait_ge(s["ln_mv"], later + nth(k, t))
                eng.activation(lnv[:, k, t:t + 1], bn_mv[:, k, t, 1:2], ACT.Ln, bias=eps_c[:, 0:1]).then_inc(s["ln_log"], 1)
                eng.wait_ge(s["ln_log"], later + nth(k, t))
                eng.activation(rstd[:, k, t:t + 1], lnv[:, k, t:t + 1], ACT.Exp, scale=-0.5).then_inc(s["ln_rstd"], 1)

            def relu_norm(k, t, before, done):
                eng.wait_ge(s["ln_nb"], NT * before + t + 1)
                eng.activation(h[:, t, :], xres[:, t, :], ACT.Relu, bias=nbias[:, k, t:t + 1],
                               scale=rstd[:, k, t:t + 1]).then_inc(done, 1)

            def take_hT(before, t, banks):
                eng.wait_ge(s["hT_ready"], before + t + 1)
                eng.activation(hT[:, :, t * P:(t + 1) * P], banks[t % 2][:, :].rearrange("p (c n) -> p c n", n=P),
                               ACT.Copy).then_inc(s["hT_taken"], 1)

            def end_block(k, after, before):
                for t in range(NT + 3):
                    if t < NT:
                        inverse_deviation(k, t)
                    if 1 <= t < NT + 1:
                        inverse_deviation(after, t - 1)
                    if 2 <= t < NT + 2:
                        relu_norm(after, t - 2, before, s["h_ready"])
                    if t >= 3:
                        take_hT(NT * (before + 1), t - 3, bank[0:2])

            for t in range(NT):
                inverse_deviation(LN_IN0, t)
            for t in range(NT):
                relu_norm(LN_IN0, t, 0, s["h_ready"])

            def quad(i):
                for q in range(4):
                    if q % 2 == 0:
                        eng.wait_ge((s["ea_in0"], s["ea_in1"])[q // 2], 16 * i + 16)
                    need(eng, s["counted"], 4 * i + q - 3)
                    eng.activation(e_split[:, q, 0:DE], e_raw[:, q, :], ACT.Copy).then_inc(s["ea_hi"], 1)
                eng.wait_ge(s["counted"], 4 * i + 4)
                need(eng, s["ea_out"], 16 * i)
                eng.activation(eaT_out[:, :], bank[5][:, :], ACT.Copy).then_inc(s["ea_evac"], 1)

            quad(0)
            with eng.Fori(1, QUADS) as i:
                quad(i)

            for t in range(NT):
                take_hT(0, t, bank[6:8])
            eng.wait_ge(s["counts"], 1)
            for t in range(NT):
                eng.activation(CT[:, t, :], bank[t][:, :], ACT.Copy).then_inc(s["ct_taken"], 1)
            eng.activation(ea_sums, bank[4][:, :], ACT.Copy).then_inc(s["ct_taken"], 1)
            eng.wait_ge(s["deg_taken"], 1)
            eng.activation(dlog[:, :], deg[:, :], ACT.Ln).then_inc(s["dlog_done"], 1)
            eng.wait_ge(s["dlog_done"], 1)
            eng.activation(dinv[:, :], dlog[:, :], ACT.Exp, scale=-0.5).then_inc(s["dinv_ready"], 1)

            for u in range(2 * NT):
                k = u % 2
                eng.wait_ge(s["s_sub"], u + 1)
                eng.activation(S[:, k, :, :], S[:, k, :, :], ACT.Exp).then_inc(s["s_exp"], 1)
                eng.wait_ge(s["s_sum"], u + 1)
                eng.activation(ssm[:, k, :], ssm[:, k, :], ACT.Ln).then_inc(s["s_log"], 1)
                eng.wait_ge(s["s_log"], u + 1)
                eng.activation(ssm[:, k, :], ssm[:, k, :], ACT.Exp, scale=-1.0).then_inc(s["s_rec"], 1)
                if u == NT:
                    eng.wait_ge(s["w2_in"], 16)
                    for t in range(NT):
                        eng.activation(w2_hi[:, t, :], slot(2)[:, t, :], ACT.Copy).then_inc(s["w2hi_done"], 1)
            eng.wait_ge(s["av_done"], 2 * NT)
            for t in range(NT):
                eng.activation(hT[:, t, :], bank[4 + t][:, :], ACT.Copy).then_inc(s["av_taken"], 1)
            for t in range(NT + 1):
                if t < NT:
                    inverse_deviation(LN_A, t)
                if t == 1:
                    eng.wait_ge(s["eat_ready"], 1)
                    eng.activation(EAT[:, :], bank[6][0:DE + 1, :], ACT.Copy).then_inc(s["eat_taken"], 1)
                if t:
                    eng.wait_ge(s["wo_ready"], NT)
                    take_hT(NT, t - 1, bank[4:6])
            eng.wait_ge(s["w1c_in"], 32)
            eng.activation(w1c_hi[:, :], w1c_raw[:, :], ACT.Copy).then_inc(s["w1chi_done"], 1)
            eng.wait_ge(s["bcol_in"], 64)
            for f in range(FT):
                eng.wait_ge(s["ff1_ready"], f + 1)
                eng.activation((qT, kT)[f // NT][:, f % NT, :], bank[f % 4][:, :], ACT.Relu,
                               bias=bcol[:, 8 + f:9 + f]).then_inc(s["ff1_taken"], 1)
            end_block(LN_B, LN_IN1, 1)
            for t in range(NT):
                eng.wait_ge(s["tab_ready"], 2 * t + 2)
                eng.activation(v[:, t, :], bank[6 + t % 2][:, :], ACT.Copy).then_inc(s["qtab_taken"], 1)

            def step(n, q, first=True, second=True, finish=True):
                p = q % 2
                if first:
                    eng.wait_ge(s["preA"], n + 1)
                    need(eng, s["sqA"], n - 1)
                    eng.activation(eA[:, p, :], bank[p][:, :], ACT.Exp).then_inc(s["expA"], 1)
                if finish:
                    eng.wait_ge(s["sqB"], n - 2)
                    eng.activation(uB[:, 1 - p, :], uB[:, 1 - p, :], ACT.Ln, bias=1.0, scale=0.5).then_inc(s["logB"], 1)
                    eng.wait_ge(s["logB"], n - 2)
                    eng.activation(uB[:, 1 - p, :], uB[:, 1 - p, :], ACT.Exp, scale=-1.0).then_inc(s["recB"], 1)
                if first:
                    eng.wait_ge(s["sqA"], n + 1)
                    eng.activation(uA[:, p, :], uA[:, p, :], ACT.Ln, bias=1.0, scale=0.5).then_inc(s["logA"], 1)
                    eng.wait_ge(s["logA"], n + 1)
                    eng.activation(uA[:, p, :], uA[:, p, :], ACT.Exp, scale=-1.0).then_inc(s["recA"], 1)
                if second:
                    eng.wait_ge(s["preB"], n - 1)
                    need(eng, s["sqB"], n - 3)
                    eng.activation(eB[:, p, :], bank[2 + p][:, :], ACT.Exp).then_inc(s["expB"], 1)
                if first:
                    eng.wait_ge(s["mishA"], n + 1)
                    need(eng, s["preB"], n - p - 2)
                    eng.activation(h_hi[:, q // 2, 2 * p:2 * p + 2, :], mA[:, p, :].rearrange("p (c e) -> p c e", c=2),
                                   ACT.Copy).then_inc(s["hiA"], 1)

            for n in range(4):
                step(n, n, second=n >= 2, finish=n >= 3)
            with eng.Fori(1, QUADS) as i:
                for q in range(4):
                    step(4 * i + q, q)
            for n in range(T, T + 3):
                step(n, n % 4, first=False, second=n < T + 2)

            eng.wait_ge(s["agg_ready"], 1)
            for t in range(NT):
                eng.activation(mask[:, t, :], bank[4 + t][:, :], ACT.Copy).then_inc(s["agg_taken"], 1)
            for f in range(NT):
                eng.wait_ge(s["u_ready"], f + 1)
                eng.activation(v[:, f, :], bank[f][:, :], ACT.Exp, bias=bcol[:, 16 + f:17 + f]).then_inc(s["u_exp"], 1)
                if f:
                    finish_u = f - 1
                    eng.wait_ge(s["u_sq"], finish_u + 1)
                    eng.activation(v[:, finish_u, :], v[:, finish_u, :], ACT.Ln, bias=1.0, scale=0.5).then_inc(s["u_log"], 1)
                    eng.wait_ge(s["u_log"], finish_u + 1)
                    eng.activation(v[:, finish_u, :], v[:, finish_u, :], ACT.Exp, scale=-1.0).then_inc(s["u_rec"], 1)
            eng.wait_ge(s["u_sq"], NT)
            eng.activation(v[:, NT - 1, :], v[:, NT - 1, :], ACT.Ln, bias=1.0, scale=0.5).then_inc(s["u_log"], 1)
            eng.wait_ge(s["u_log"], NT)
            eng.activation(v[:, NT - 1, :], v[:, NT - 1, :], ACT.Exp, scale=-1.0).then_inc(s["u_rec"], 1)
            end_block(LN_C, LN_IN2, 2)
            eng.wait_ge(s["a2_ready"], 1)
            eng.activation(a2[:, :], bank[3][0:DH, :], ACT.Copy).then_inc(s["a2_taken"], 1)
            for t in range(NT + 1):
                if t < NT:
                    inverse_deviation(LN_IN3, t)
                if t:
                    relu_norm(LN_IN3, t - 1, 3, s["m_h"])

            with eng.Fori(0, LAYERS) as l:
                for f in range(NT):
                    eng.wait_ge(s["m_agg"], NT * l + f + 1)
                    eng.activation(hT[:, f, :], bank[f][:, :], ACT.Copy).then_inc(s["m_taken"], 1)
                for t in range(NT + 1):
                    if t < NT:
                        inverse_deviation(LN_L3, t, NT * l)
                    if t:
                        eng.wait_ge(s["m_shifted"], NT * l + t)
                        eng.activation(h[:, t - 1, :], y[:, t - 1, :], ACT.Relu).then_inc(s["m_h"], 1)

        @block.tensor
        def _(eng):
            def transposes(src, t, to):
                for c in range(NT):
                    mm = eng.transpose(to[:, c * P:(c + 1) * P], src[:, t, c * P:(c + 1) * P], ident[:, :])
                return mm

            def product(to, lhs, rhs):
                for j, (a, b) in enumerate(zip(lhs, rhs)):
                    mm = eng.matmul(to, a, b, start=(j == 0), stop=(j == len(lhs) - 1))
                return mm

            def clear(to):
                eng.matmul(to, zrow[:, 0:to.shape[0]], zrow[:, :], start=True, stop=False, skip_group_check=True)

            def close(to):
                return eng.matmul(to, zrow[:, 0:to.shape[0]], zrow[:, :], start=False, stop=True, skip_group_check=True)

            eng.wait_ge(s["ident_done"], 1)
            eng.wait_ge(s["idx_float"], 1)
            eng.transpose(bank[6][:, 0:T], idx_f[:, 0, :], ident[0:T, 0:T])
            eng.transpose(bank[6][:, P:P + T], idx_f[:, 1, :], ident[0:T, 0:T]).then_inc(s["idx_T"], 1)

            def count(n, q, first=False):
                eng.wait_ge(s["src_hot"], n + 1)
                eng.wait_ge(s["dst_hot"], n + 1)
                for t in range(NT):
                    eng.matmul(bank[t][:, :], oh_src[:, q % 2, t * P:(t + 1) * P], oh_cnt[:, q % 2, :],
                               start=first, stop=False, skip_group_check=True)
                eng.wait_ge(s["ea_lo"], n + 1)
                eng.matmul(bank[4][:, :], e_split[:, q, :], oh_cnt[:, q % 2, :], start=first, stop=False, skip_group_check=True)
                eng.transpose(bank[5][:, q * P:(q + 1) * P], e_split[:, q, :].bitcast(f32), ident[:, :]).then_inc(s["counted"], 1)

            for q in range(4):
                count(q, q, first=(q == 0))
            with eng.Fori(1, QUADS) as i:
                for q in range(4):
                    if q == 0:
                        eng.wait_ge(s["ea_evac"], i)
                    count(4 * i + q, q)
            for t in range(NT + 1):
                mm = close(bank[t][:, :])
            mm.then_inc(s["counts"], 1)

            def transpose_h(before, t, banks):
                eng.wait_ge(s["h_ready"], before + t + 1)
                if t >= 2:
                    eng.wait_ge(s["hT_taken"], before + t - 1)
                transposes(h, t, banks[t % 2]).then_inc(s["hT_ready"], 1)

            eng.wait_ge(s["idx_taken"], 4)
            for t in range(NT):
                transpose_h(0, t, bank[6:8])

            eng.wait_ge(s["hT_taken"], NT)
            for j, (k, loaded) in enumerate(((0, s["wq_in"]), (1, s["wk_in"]), (2, s["wv_in"]))):
                eng.wait_ge(loaded, 16)
                for t in range(NT):
                    n = NT * j + t
                    if n >= 2:
                        eng.wait_ge(s["qkv_taken"], n - 1)
                    weight = [slot(k)[:, c, t * P:(t + 1) * P] for c in range(NT)]
                    nodes = [hT[:, c, t * P:(t + 1) * P] for c in range(NT)]
                    if j < 2:
                        mm = product(bank[6 + n % 2][:, :], weight, [hT[:, c, :] for c in range(NT)])
                    else:
                        mm = product(bank[6 + n % 2][:, :], nodes, [slot(k)[:, c, :] for c in range(NT)])
                    mm.then_inc(s["qkv_ready"], 1)

            eng.wait_ge(s["ct_taken"], NT + 1)
            eng.wait_ge(s["ea_evac"], QUADS)
            for t in range(NT):
                for c in range(NT):
                    mm = eng.matmul(bank[5][:, t:t + 1], CT[:, c, t * P:(t + 1) * P], ones[:, 0:1],
                                    start=(c == 0), stop=(c == NT - 1))
            mm.then_inc(s["deg_ready"], 1)
            for t in range(NT):
                for c in range(NT):
                    mm = eng.transpose(bank[t][:, c * P:(c + 1) * P], CT[:, c, t * P:(t + 1) * P], ident[:, :])
                mm.then_inc(s["cT_ready"], 1)

            def scores(u):
                half, m = u // NT, u % NT
                for j in range(4):
                    n = 4 * u + j
                    if n >= 4:
                        eng.wait_ge(s["s_masked"], n - 3)
                    for i in range(2):
                        c, lo = 2 * (j // 2) + i, HD * (j % 2)
                        mm = eng.matmul(bank[j][:, i * HALF:(i + 1) * HALF],
                                        kT[lo:lo + HD, c, m * P:(m + 1) * P],
                                        qT[lo:lo + HD, c, half * HALF:(half + 1) * HALF], start=True, stop=True)
                    mm.then_inc(s["s_ready"], 1)

            def attend(u):
                half, m, k = u // NT, u % NT, u % 2
                eng.wait_ge(s["att_ready"], u + 1)
                for hd in range(HEADS):
                    lo = HD * (hd % 2)
                    mm = eng.matmul(bank[4 + hd // 2][lo:lo + HD, half * HALF:(half + 1) * HALF],
                                    v[:, m, hd * HD:(hd + 1) * HD], S[:, k, hd, :],
                                    start=(m == 0), stop=(m == NT - 1))
                mm.then_inc(s["av_done"], 1)

            eng.wait_ge(s["mask_ready"], NT)
            eng.wait_ge(s["qkv_taken"], 3 * NT)
            eng.wait_ge(s["deg_taken"], 1)
            for u in range(2 * NT + 2):
                if u < 2 * NT:
                    scores(u)
                if u >= 2:
                    attend(u - 2)

            eng.wait_ge(s["av_taken"], NT)
            eng.wait_ge(s["wo_in"], 16)
            for t in range(NT):
                product(bank[t][:, :], [hT[:, c, t * P:(t + 1) * P] for c in range(NT)],
                        [slot(3)[:, c, :] for c in range(NT)]).then_inc(s["wo_ready"], 1)
            eng.matmul(bank[6][0:DE, :], ident[:, 0:DE], ea_sums, start=True, stop=False)
            eng.matmul(bank[6][0:DE, :], ident[:, DE:P], ea_sums, start=False, stop=True)
            for c in range(NT):
                mm = eng.matmul(bank[6][DE:DE + 1, :], ones[:, 0:1], CT[:, c, :], start=(c == 0), stop=(c == NT - 1))
            mm.then_inc(s["eat_ready"], 1)

            for t in range(NT):
                transpose_h(NT, t, bank[4:6])
            eng.wait_ge(s["hT_taken"], 2 * NT)
            eng.wait_ge(s["y1_ready"], NT)
            eng.wait_ge(s["f1_in"], 32)
            for f in range(FT):
                if f >= 4:
                    eng.wait_ge(s["ff1_taken"], f - 3)
                product(bank[f % 4][:, :], [slot(4 + f // NT)[:, c, (f % NT) * P:(f % NT + 1) * P] for c in range(NT)],
                        [hT[:, c, :] for c in range(NT)]).then_inc(s["ff1_ready"], 1)
            eng.wait_ge(s["ff1_taken"], FT)
            eng.wait_ge(s["eat_taken"], 1)
            eng.wait_ge(s["f2_in"], 32)
            for t in range(NT):
                product(bank[4 + t][:, :], [(qT, kT)[c // NT][:, c % NT, t * P:(t + 1) * P] for c in range(FT)],
                        [slot(6 + c // NT)[:, c % NT, :] for c in range(FT)]).then_inc(s["ff2_ready"], 1)

            eng.wait_ge(s["w1a_in"], 16)
            eng.wait_ge(s["w1b_in"], 16)
            for t in range(NT + 1):
                if t < NT:
                    transpose_h(2 * NT, t, bank[0:2])
                if t:
                    i = t - 1
                    eng.wait_ge(s["hT_taken"], 2 * NT + i + 1)
                    if i < 2:
                        eng.wait_ge(s["y2_ready"], NT)
                    else:
                        eng.wait_ge(s["ptab_taken"], i - 1)
                        eng.wait_ge(s["qtab_taken"], i - 1)
                    for to, k in ((4 + i % 2, 0), (6 + i % 2, 1)):
                        product(bank[to][:, :], [hT[:, c, i * P:(i + 1) * P] for c in range(NT)],
                                [slot(k)[:, c, :] for c in range(NT)]).then_inc(s["tab_ready"], 1)

            def first_layer(n, q, k_use):
                p, k = q % 2, q // 2
                if p == 0:
                    eng.wait_ge((s["gath0"], s["gath1"])[k], 64 * k_use + 64)
                    eng.wait_ge((s["eaT0"], s["eaT1"])[k], 16 * k_use + 16)
                need(eng, s["mishA"], n - 1)
                for c in range(2):
                    f = slice((2 * p + c) * P, (2 * p + c + 1) * P)
                    for j in range(2):
                        eng.matmul(bank[p][:, (2 * c + j) * P:(2 * c + j + 1) * P], G[:, 2 * k + j, f], ident[:, :],
                                   is_transpose=True, start=(c == 0 and j == 0), stop=False, skip_group_check=True)
                for c in range(2):
                    f = slice((2 * p + c) * P, (2 * p + c + 1) * P)
                    to = bank[p][:, 2 * c * P:2 * (c + 1) * P]
                    eng.matmul(to, w1c_hi[:, f], eaT[:, k, :], start=False, stop=False, skip_group_check=True)
                    mm = eng.matmul(to, w1c_lo[:, f], eaT[0:DE, k, :], start=False, stop=True, skip_group_check=True)
                mm.then_inc(s["preA"], 1)

            def second_layer(n, q, units_before, scattering=True):
                p, k = q % 2, q // 2
                if p == 0:
                    eng.wait_ge(s["hiA"], units_before)
                    eng.wait_ge(s["loA"], units_before)
                need(eng, s["mishB"], n - 1)
                to = bank[2 + p][:, :]
                mm = eng.matmul(to, ones_r[:, :], b2_rows[:, :], start=True, stop=False)
                if scattering:
                    mm.then_inc(s["scattered"], 1)
                for c in range(NT):
                    hi, lo = h_hi[:, k, c, p * P:(p + 1) * P], h_lo[:, k, c, p * P:(p + 1) * P]
                    eng.matmul(to, hi, w2_hi[:, c, :], start=False, stop=False)
                    eng.matmul(to, hi, w2_lo[:, c, :], start=False, stop=False)
                    mm = eng.matmul(to, lo, w2_hi[:, c, :], start=False, stop=(c == NT - 1))
                mm.then_inc(s["preB"], 1)

            def scatter(n, q):
                eng.wait_ge(s["mishB"], n + 1)
                eng.wait_ge(s["hotB"], n + 1)
                first = eng.value_load(win[0:1, bass.ds(2 * n, 1)], min_val=0, max_val=N // WIN - 1)
                end = eng.value_load(win[0:1, bass.ds(2 * n + 1, 1)], min_val=1, max_val=N // WIN)
                with eng.Fori(first, end) as w:
                    for t in range(NT):
                        eng.matmul(bank[4 + t][:, ws(w)], mB[:, q % 2, t * P:(t + 1) * P], oh[:, q % 2, ws(w)],
                                   start=False, stop=False, skip_group_check=True)

            eng.wait_ge(s["ptab_taken"], NT)
            eng.wait_ge(s["qtab_taken"], NT)
            eng.wait_ge(s["w1chi_done"], 1)
            eng.wait_ge(s["w1clo_done"], 1)
            eng.wait_ge(s["w2hi_done"], NT)
            eng.wait_ge(s["w2lo_done"], NT)
            eng.wait_ge(s["b2_done"], 3)
            eng.wait_ge(s["win_row"], 16)
            for t in range(NT):
                clear(bank[4 + t][:, :])
            for n in range(4):
                first_layer(n, n, 0)
                if n >= 2:
                    second_layer(n - 2, n - 2, 2, scattering=False)
            with eng.Fori(1, QUADS) as i:
                for q in range(4):
                    n = 4 * i + q
                    first_layer(n, q, i)
                    scatter(n - 4, q)
                    second_layer(n - 2, (q + 2) % 4, 4 * i + (0, 2)[q // 2])
            for n in range(T, T + 4):
                scatter(n - 4, n % 4)
                if n < T + 2:
                    second_layer(n - 2, (n + 2) % 4, T)
            for t in range(NT):
                mm = close(bank[4 + t][:, :])
            mm.then_inc(s["agg_ready"], 1)

            eng.wait_ge(s["w3_in"], 32)
            eng.wait_ge(s["mishB"], T)
            for k, operand in ((3, hT), (4, mask)):
                for f in range(NT):
                    if k == 4:
                        eng.wait_ge(s["agg_taken"], NT)
                    for c in range(NT):
                        mm = eng.matmul(bank[f][:, :], slot(k)[:, c, f * P:(f + 1) * P], operand[:, c, :],
                                        start=(k == 3 and c == 0), stop=(k == 4 and c == NT - 1))
                    if k == 4:
                        mm.then_inc(s["u_ready"], 1)
            eng.wait_ge(s["w4_in"], 16)
            eng.wait_ge(s["u_mish"], NT)
            for t in range(NT):
                product(bank[4 + t][:, :], [qT[:, c, t * P:(t + 1) * P] for c in range(NT)],
                        [slot(2)[:, c, :] for c in range(NT)]).then_inc(s["w4_ready"], 1)

            eng.wait_ge(s["l2_in"], 48)
            for t in range(NT + 1):
                if t < NT:
                    transpose_h(3 * NT, t, bank[0:2])
                if t:
                    i = t - 1
                    eng.wait_ge(s["hT_taken"], 3 * NT + i + 1)
                    if i == 0:
                        eng.wait_ge(s["y4_ready"], NT)
                    mm = product(bank[6][:, i * DH:(i + 1) * DH], [hT[:, c, i * P:(i + 1) * P] for c in range(NT)],
                                 [l2w1[:, c, :] for c in range(NT)])
            mm.then_inc(s["t1_ready"], 1)
            eng.wait_ge(s["t1_taken"], NT)
            for t in range(NT):
                mm = product(bank[7][:, t * DH:(t + 1) * DH], [CT[:, c, t * P:(t + 1) * P] for c in range(NT)],
                             [t1[:, c, :] for c in range(NT)])
            mm.then_inc(s["a1_ready"], 1)
            eng.wait_ge(s["t2_done"], NT)
            for c in range(NT):
                eng.matmul(bank[3][0:DH, c * P:(c + 1) * P], t2[:, c, :], ident[:, :],
                           start=(c == 0), stop=False, skip_group_check=True)
            for c in range(NT):
                mm = eng.matmul(bank[3][0:DH, :], t2[:, c, :], CT[:, c, :], start=False, stop=(c == NT - 1),
                                skip_group_check=True)
            mm.then_inc(s["a2_ready"], 1)
            eng.wait_ge(s["a2_taken"], 1)
            for t in range(NT):
                if t == 2:
                    eng.wait_ge(s["a1_sum"], NT)
                eng.matmul(bank[4 + t][:, :], a2[:, t * P:(t + 1) * P], l2w2[:, :], start=True, stop=True).then_inc(s["o2_ready"], 1)

            eng.wait_ge(s["wx_in"], 16 * LAYERS)
            eng.wait_ge(s["we_in"], 32 * LAYERS)
            eng.wait_ge(s["x3_ready"], NT)
            with eng.Fori(0, LAYERS) as l:
                for c in range(NT):
                    eng.wait_ge(s["m_h"], NT * l + c + 1)
                    for f in range(NT):
                        mm = eng.matmul(bank[f][:, :], h[:, c, f * P:(f + 1) * P], CT[:, c, :],
                                        start=(c == 0), stop=(c == NT - 1))
                        if c == NT - 1:
                            mm.then_inc(s["m_agg"], 1)
                eng.wait_ge(s["m_taken"], NT * l + NT)
                for t in range(NT):
                    product(bank[4 + t][:, :],
                            [hT[:, c, t * P:(t + 1) * P] for c in range(NT)] + [EAT[:, t * P:(t + 1) * P]],
                            [wx_flat[:, bass.ds(l * (NT * D) + c * D, D)] for c in range(NT)]
                            + [we_flat[:, bass.ds(l * D, D)]]).then_inc(s["m_msg"], 1)

        @block.vector
        def _(eng):
            eng.wait_ge(s["idx_in"], 32)
            eng.tensor_copy(idx_f[:, :, :], idx_i[:, :, :]).then_inc(s["idx_float"], 1)
            eng.wait_ge(s["idx_float"], 1)
            eng.tensor_reduce(win_f[:, 0:1], idx_f[:, 0, :], AX.X, ALU.min).then_inc(s["win_range"], 1)
            eng.tensor_reduce(win_f[:, 1:2], idx_f[:, 0, :], AX.X, ALU.max).then_inc(s["win_range"], 1)
            eng.wait_ge(s["win_range"], 2)
            eng.tensor_scalar(win_f[:, 1:2], win_f[:, 1:2], float(WIN), None, ALU.add).then_inc(s["win_range"], 1)
            eng.wait_ge(s["win_range"], 3)
            eng.tensor_copy(win_v[:, :], win_f[:, :]).then_inc(s["win_value"], 1)
            eng.wait_ge(s["win_value"], 1)
            eng.tensor_scalar(win_i[:, :], win_v[:, :], SHIFT, None, ALU.arith_shift_right).then_inc(s["win_shift"], 1)

            def statistics(k, src, t, later=0):
                eng.bn_stats(bn_st[:, k, t, :], src[:, t, :]).then_inc(s["ln_stats"], 1)
                eng.wait_ge(s["ln_stats"], later + nth(k, t))
                eng.nop(nofuse=True)
                eng.bn_aggr(bn_mv[:, k, t, :], bn_st[:, k, t, :]).then_inc(s["ln_mv"], 1)

            def shift(k, t):
                eng.wait_ge(s["ln_rstd"], nth(k, t))
                eng.wait_ge(s["ln_mv"], nth(k, t))
                eng.scalar_tensor_tensor(nbias[:, k, t:t + 1], bn_mv[:, k, t, 0:1], -1.0, rstd[:, k, t:t + 1],
                                         ALU.mult, ALU.mult).then_inc(s["ln_nb"], 1)

            eng.wait_ge(s["x_in"], 16)
            for t in range(NT):
                statistics(LN_IN0, xres, t)
            eng.wait_ge(s["idx_T"], 1)
            for to, lo in ((dst_f, 0), (src_f, P), (dst_i, 0), (src_i, P)):
                eng.tensor_copy(to[:, :], bank[6][:, lo:lo + T]).then_inc(s["idx_taken"], 1)
            for t in range(NT):
                shift(LN_IN0, t)

            eng.wait_ge(s["consts"], 7)
            eng.wait_ge(s["idx_taken"], 4)

            def count(n, q):
                need(eng, s["counted"], n - 1)
                eng.tensor_scalar(oh_src[:, q % 2, :], iota_n[:, :], src_f[:, bass.ds(n, 1)], None, ALU.is_equal
                                  ).then_inc(s["src_hot"], 1)
                eng.tensor_scalar(oh_cnt[:, q % 2, :], iota_n[:, :], dst_f[:, bass.ds(n, 1)], None, ALU.is_equal
                                  ).then_inc(s["dst_hot"], 1)
                eng.wait_ge(s["ea_hi"], n + 1)
                eng.tensor_tensor(e_split[:, q, DE:2 * DE], e_raw[:, q, :], e_split[:, q, 0:DE].bitcast(f32),
                                  ALU.subtract).then_inc(s["ea_lo"], 1)

            for q in range(4):
                count(q, q)
            with eng.Fori(1, QUADS) as i:
                for q in range(4):
                    count(4 * i + q, q)

            eng.wait_ge(s["bcol_in"], 64)
            eng.wait_ge(s["rows_in"], 16 * 7)
            for n in range(3 * NT):
                eng.wait_ge(s["qkv_ready"], n + 1)
                t, got = n % NT, bank[6 + n % 2][:, :]
                if n < NT:
                    eng.tensor_scalar(qT[:, t, :], got, bcol[:, t:t + 1], HD ** -0.5, ALU.add, ALU.mult).then_inc(s["qkv_taken"], 1)
                elif n < 2 * NT:
                    eng.tensor_scalar(kT[:, t, :], got, bcol[:, NT + t:NT + t + 1], None, ALU.add).then_inc(s["qkv_taken"], 1)
                else:
                    eng.tensor_tensor(v[:, t, :], got, brow[:, BV, :], ALU.add).then_inc(s["qkv_taken"], 1)
            eng.wait_ge(s["deg_ready"], 1)
            eng.tensor_scalar(deg[:, :], bank[5][:, 0:NT], 1.0, None, ALU.add).then_inc(s["deg_taken"], 1)
            for t in range(NT):
                eng.wait_ge(s["cT_ready"], t + 1)
                eng.tensor_scalar(mask[:, t, :], bank[t][:, :], 1.0, None, ALU.min).then_inc(s["mask_ready"], 1)

            def masked(u):
                half, m, k = u // NT, u % NT, u % 2
                need(eng, s["av_done"], u - 1)
                for j in range(4):
                    eng.wait_ge(s["s_ready"], 4 * u + j + 1)
                    hd = 4 * (j // 2) + j % 2
                    eng.tensor_tensor(S[:, k, hd:hd + 3:2, :], bank[j][:, :].rearrange("p (i n) -> p i n", i=2),
                                      mask[:, m, half * HALF:(half + 1) * HALF].unsqueeze(1).to_broadcast([P, 2, HALF]),
                                      ALU.mult).then_inc(s["s_masked"], 1)
                eng.wait_ge(s["s_masked"], 4 * u + 4)
                need(eng, s["s_sub"], u)
                eng.tensor_reduce(smx[:, :], S[:, k, :, :].rearrange("p h n -> p n h"), AX.X, ALU.max).then_inc(s["s_max"], 1)
                eng.wait_ge(s["s_max"], u + 1)
                eng.tensor_tensor(S[:, k, :, :], S[:, k, :, :], smx[:, :].unsqueeze(1).to_broadcast([P, HEADS, HALF]),
                                  ALU.subtract).then_inc(s["s_sub"], 1)

            def weights(u):
                k = u % 2
                eng.wait_ge(s["s_rec"], u + 1)
                eng.tensor_tensor(S[:, k, :, :], S[:, k, :, :], ssm[:, k, :].unsqueeze(1).to_broadcast([P, HEADS, HALF]),
                                  ALU.mult).then_inc(s["att_ready"], 1)

            eng.wait_ge(s["mask_ready"], NT)
            eng.wait_ge(s["ea_out"], 16 * QUADS)
            for u in range(2 * NT):
                k = u % 2
                masked(u)
                if u:
                    weights(u - 1)
                eng.wait_ge(s["s_exp"], u + 1)
                need(eng, s["att_ready"], u - 1)
                eng.tensor_reduce(ssm[:, k, :], S[:, k, :, :].rearrange("p h n -> p n h"), AX.X, ALU.add).then_inc(s["s_sum"], 1)
            weights(2 * NT - 1)

            def plus_row(k, done):
                for t in range(NT):
                    eng.tensor_tensor(h[:, t, :], h[:, t, :], brow[:, k, :], ALU.add).then_inc(done, 1)

            def plus_be2():
                for t in range(NT):
                    eng.tensor_tensor(xres[:, t, :], xres[:, t, :], brow[:, BE2, :], ALU.add).then_inc(s["xb_done"], 1)

            def end_block(k, after, before, bias_sem, product_ready, summed, gain, done):
                eng.wait_ge(bias_sem, NT)
                for t in range(NT + 2):
                    if t < NT:
                        eng.wait_ge(product_ready, t + 1)
                        eng.tensor_tensor(y[:, t, :], bank[4 + t][:, :], h[:, t, :], ALU.add).then_inc(summed, 1)
                        eng.wait_ge(summed, t + 1)
                        statistics(k, y, t)
                    if 1 <= t < NT + 1:
                        eng.wait_ge(s["xb_done"], NT * before + t - NT)
                        affine(k, t - 1, before, brow[:, gain, :], xres[:, t - 1, :], xres).then_inc(done, 1)
                        eng.wait_ge(done, t)
                        statistics(after, xres, t - 1)
                    if t >= 2:
                        shift(after, t - 2)

            eng.wait_ge(s["hT_ready"], NT)
            plus_row(BO, s["hb_done"])
            eng.wait_ge(s["hb_done"], NT)
            def affine(k, t, before, gain, plus, to, later=0):
                eng.wait_ge(s["ln_mv"], later + nth(k, t))
                eng.scalar_tensor_tensor(y[:, t, :], y[:, t, :], bn_mv[:, k, t, 0:1], gain,
                                         ALU.subtract, ALU.mult).then_inc(s["y_scaled"], 1)
                eng.wait_ge(s["y_scaled"], later + (NT * before + t + 1))
                eng.wait_ge(s["ln_rstd"], later + nth(k, t))
                return eng.scalar_tensor_tensor(to[:, t, :], y[:, t, :], rstd[:, k, t:t + 1], plus, ALU.mult, ALU.add)

            for t in range(NT + 1):
                if t < NT:
                    eng.wait_ge(s["wo_ready"], t + 1)
                    if t == 0:
                        eng.wait_ge(s["eat_ready"], 1)
                    eng.tensor_tensor(y[:, t, :], bank[t][:, :], h[:, t, :], ALU.add).then_inc(s["y1_ready"], 1)
                    eng.wait_ge(s["y1_ready"], t + 1)
                    statistics(LN_A, y, t)
                if t:
                    affine(LN_A, t - 1, 0, brow[:, G1, :], brow[:, BE1, :], h).then_inc(s["h_ready"], 1)
            plus_be2()
            eng.wait_ge(s["hT_ready"], 2 * NT)
            eng.wait_ge(s["h_ready"], 2 * NT)
            plus_row(B2, s["hb2_done"])

            eng.wait_ge(s["w1chi_done"], 1)
            eng.tensor_tensor(w1c_lo[:, :], w1c_raw[0:DE, :], w1c_hi[0:DE, :].bitcast(f32), ALU.subtract).then_inc(s["w1clo_done"], 1)
            for t in range(NT):
                eng.wait_ge(s["w2hi_done"], t + 1)
                eng.tensor_tensor(w2_lo[:, t, :], slot(2)[:, t, :], w2_hi[:, t, :].bitcast(f32), ALU.subtract).then_inc(s["w2lo_done"], 1)
            eng.wait_ge(s["b2_in"], 32)
            eng.tensor_copy(b2_rows[0:1, :], b2_raw[0:1, :]).then_inc(s["b2_done"], 1)
            eng.tensor_copy(b2_rows[32:33, :], b2_raw[32:33, :]).then_inc(s["b2_done"], 1)
            eng.wait_ge(s["b2_done"], 2)
            eng.tensor_tensor(b2_rows[32:33, :], b2_raw[32:33, :], b2_rows[32:33, :].bitcast(f32), ALU.subtract).then_inc(s["b2_done"], 1)

            end_block(LN_B, LN_IN1, 1, s["hb2_done"], s["ff2_ready"], s["y2_ready"], G2, s["x1_ready"])
            eng.wait_ge(s["rows1_in"], 16 * 5)
            for t in range(NT):
                eng.wait_ge(s["tab_ready"], 2 * t + 1)
                eng.tensor_tensor(y[:, t, :], bank[4 + t % 2][:, :], brow[:, B1, :], ALU.add).then_inc(s["ptab_taken"], 1)
            for t in range(NT):
                eng.wait_ge(s["h_ready"], 2 * NT + t + 1)
                eng.tensor_tensor(xres[:, t, :], xres[:, t, :], brow[:, BETA, :], ALU.add).then_inc(s["xb_done"], 1)
            eng.wait_ge(s["hT_ready"], 3 * NT)
            plus_row(B4, s["hb4_done"])

            def step(n, q, first=True, second=True, finish=True):
                p = q % 2
                if first:
                    eng.wait_ge(s["expA"], n + 1)
                    eng.tensor_scalar(eA[:, p, :], eA[:, p, :], TOP, None, ALU.min).then_inc(s["topA"], 1)
                    eng.wait_ge(s["topA"], n + 1)
                    need(eng, s["mishA"], n - 1)
                    eng.scalar_tensor_tensor(uA[:, p, :], eA[:, p, :], 2.0, eA[:, p, :], ALU.add, ALU.mult).then_inc(s["sqA"], 1)
                if finish:
                    k = 1 - p
                    eng.wait_ge(s["recB"], n - 2)
                    need(eng, s["scattered"], n - 4)
                    eng.scalar_tensor_tensor(mB[:, k, :], uB[:, 1 - p, :], 1.0, bank[3 - p][:, :], ALU.subtract, ALU.mult,
                                             reverse0=True).then_inc(s["mishB"], 1)
                    eng.tensor_scalar(oh[:, k, :], iota_n[:, :], dst_f[:, bass.ds(n - 3, 1)], None, ALU.is_equal
                                      ).then_inc(s["hotB"], 1)
                if first:
                    eng.wait_ge(s["recA"], n + 1)
                    need(eng, s["hiA"], n - 1)
                    need(eng, s["loA"], n - 1)
                    eng.scalar_tensor_tensor(mA[:, p, :], uA[:, p, :], 1.0, bank[p][:, :], ALU.subtract, ALU.mult,
                                             reverse0=True).then_inc(s["mishA"], 1)
                if second:
                    eng.wait_ge(s["expB"], n - 1)
                    eng.tensor_scalar(eB[:, p, :], eB[:, p, :], TOP, None, ALU.min).then_inc(s["topB"], 1)
                    eng.wait_ge(s["topB"], n - 1)
                    need(eng, s["mishB"], n - 3)
                    eng.scalar_tensor_tensor(uB[:, p, :], eB[:, p, :], 2.0, eB[:, p, :], ALU.add, ALU.mult).then_inc(s["sqB"], 1)
                if first:
                    hi = h_hi[:, q // 2, 2 * p:2 * p + 2, :]
                    eng.wait_ge(s["hiA"], n + 1)
                    eng.wait_ge(s["mishA"], n + 1)
                    need(eng, s["preB"], n - p - 2)
                    eng.tensor_tensor(h_lo[:, q // 2, 2 * p:2 * p + 2, :], mA[:, p, :].rearrange("p (c e) -> p c e", c=2),
                                      hi.bitcast(f32), ALU.subtract).then_inc(s["loA"], 1)

            for n in range(8):
                step(n, n % 4, second=n >= 2, finish=n >= 3)
            with eng.Fori(2, QUADS) as i:
                for q in range(4):
                    step(4 * i + q, q)
            for n in range(T, T + 3):
                step(n, n % 4, first=False, second=n < T + 2)

            def finish_u(f):
                eng.wait_ge(s["u_rec"], f + 1)
                eng.wait_ge(s["u_x"], f + 1)
                eng.scalar_tensor_tensor(qT[:, f, :], v[:, f, :], 1.0, kT[:, f, :], ALU.subtract, ALU.mult,
                                         reverse0=True).then_inc(s["u_mish"], 1)

            for f in range(NT):
                eng.wait_ge(s["u_ready"], f + 1)
                eng.wait_ge(s["u_exp"], f + 1)
                eng.tensor_scalar(kT[:, f, :], bank[f][:, :], bcol[:, 16 + f:17 + f], None, ALU.add).then_inc(s["u_x"], 1)
                eng.tensor_scalar(v[:, f, :], v[:, f, :], TOP, None, ALU.min).then_inc(s["u_top"], 1)
                eng.wait_ge(s["u_top"], f + 1)
                eng.scalar_tensor_tensor(v[:, f, :], v[:, f, :], 2.0, v[:, f, :], ALU.add, ALU.mult).then_inc(s["u_sq"], 1)
                if f:
                    finish_u(f - 1)
            finish_u(NT - 1)
            end_block(LN_C, LN_IN2, 2, s["hb4_done"], s["w4_ready"], s["y4_ready"], GAMMA, s["x2_ready"])

            for t in range(NT):
                eng.wait_ge(s["h_ready"], 3 * NT + t + 1)
                eng.tensor_tensor(xres[:, t, :], xres[:, t, :], brow[:, L2B2, :], ALU.add).then_inc(s["xb_done"], 1)
            eng.wait_ge(s["l2_in"], 48)
            eng.wait_ge(s["dinv_ready"], 1)
            eng.wait_ge(s["t1_ready"], 1)
            for t in range(NT):
                eng.tensor_scalar(t1[:, t, :], bank[6][:, t * DH:(t + 1) * DH], dinv[:, t:t + 1], None, ALU.mult).then_inc(s["t1_taken"], 1)
            eng.wait_ge(s["t1_taken"], NT)
            eng.wait_ge(s["a1_ready"], 1)
            for t in range(NT):
                eng.tensor_tensor(t2[:, t, :], bank[7][:, t * DH:(t + 1) * DH], t1[:, t, :], ALU.add).then_inc(s["a1_sum"], 1)
            for t in range(NT):
                eng.wait_ge(s["a1_sum"], t + 1)
                eng.scalar_tensor_tensor(t2[:, t, :], t2[:, t, :], dinv[:, t:t + 1], l2b1[:, :], ALU.mult, ALU.add).then_inc(s["a1_bias"], 1)
            for t in range(NT):
                eng.wait_ge(s["a1_bias"], t + 1)
                eng.tensor_scalar(t2[:, t, :], t2[:, t, :], 0.0, dinv[:, t:t + 1], ALU.max, ALU.mult).then_inc(s["t2_done"], 1)
            for t in range(NT + 1):
                if t < NT:
                    eng.wait_ge(s["o2_ready"], t + 1)
                    eng.wait_ge(s["xb_done"], 2 * NT + t + 1)
                    eng.scalar_tensor_tensor(xres[:, t, :], bank[4 + t][:, :], dinv[:, t:t + 1], xres[:, t, :],
                                             ALU.mult, ALU.add).then_inc(s["x3_ready"], 1)
                    eng.wait_ge(s["x3_ready"], t + 1)
                    statistics(LN_IN3, xres, t)
                if t:
                    shift(LN_IN3, t - 1)

            eng.wait_ge(s["affine_in"], 32 * LAYERS)
            with eng.Fori(0, LAYERS) as l:
                for t in range(NT + 1):
                    if t < NT:
                        eng.wait_ge(s["m_h"], NT * l + t + 1)
                        eng.wait_ge(s["m_msg"], NT * l + t + 1)
                        eng.tensor_tensor(y[:, t, :], bank[4 + t][:, :], h[:, t, :], ALU.add).then_inc(s["m_y"], 1)
                        eng.wait_ge(s["m_y"], NT * l + t + 1)
                        statistics(LN_L3, y, t, NT * l)
                    if t:
                        affine(LN_L3, t - 1, 3, WA[:, 0, bass.ds(l * D, D)], WA[:, 1, bass.ds(l * D, D)], y,
                               NT * l).then_inc(s["m_shifted"], 1)
            for t in range(NT):
                eng.wait_ge(s["m_h"], NT * LAYERS + t + 1)
                eng.tensor_tensor(y[:, t, :], xres[:, t, :], h[:, t, :], ALU.add).then_inc(s["result"], 1)


_INS = """x src dst edge_attr_64 L0_gnn_Wq L0_gnn_bq L0_gnn_Wk L0_gnn_bk L0_gnn_Wv L0_gnn_bv L0_gnn_Wo L0_gnn_bo
L0_gnn_W1 L0_gnn_b1 L0_gnn_W2 L0_gnn_b2 L0_gnn_g1 L0_gnn_be1 L0_gnn_g2 L0_gnn_be2
L1_gnn_W1 L1_gnn_b1 L1_gnn_W2 L1_gnn_b2 L1_gnn_W3 L1_gnn_b3 L1_gnn_W4 L1_gnn_b4 L1_gnn_gamma L1_gnn_beta
L2_gnn_W1 L2_gnn_b1 L2_gnn_W2 L2_gnn_b2 L3_gnn_Ws L3_gnn_bs L3_gnn_gammas L3_gnn_betas""".split()


def kernel(**inputs):
    import numpy as np
    import concourse.bacc as bacc
    from concourse.bass_utils import run_bass_kernel_spmd

    nc = bacc.Bacc("TRN2", target_bir_lowering=False, num_devices=1)
    arrays, ins = {}, {}
    for name in _INS:
        a = np.ascontiguousarray(inputs[name])
        arrays[f"in_{name}"] = a
        ins[name] = nc.dram_tensor(f"in_{name}", a.shape, mybir.dt.from_np(a.dtype), kind="ExternalInput").ap()
    out = nc.dram_tensor("out_x", inputs["x"].shape, mybir.dt.float32, kind="ExternalOutput").ap()
    gnn_stack_kernel(nc, ins, out)
    return run_bass_kernel_spmd(nc, [arrays], core_ids=[0]).results[0]["out_x"]
```

```python
from contextlib import ExitStack

import concourse.bass as bass
from concourse import mybir


def gnn_stack_kernel(nc, ins, out):
    f32, f32r, bf16, i32 = mybir.dt.float32, mybir.dt.float32r, mybir.dt.bfloat16, mybir.dt.int32
    ALU, ACT, AX = mybir.AluOpType, mybir.ActivationFunctionType, mybir.AxisListType

    N, D = ins["x"].shape
    E, DE = ins["edge_attr_64"].shape
    P = 128
    NT = N // P
    T = E // P
    HEADS = 8
    HD = D // HEADS
    FT = ins["L0_gnn_W1"].shape[1] // P
    DH = ins["L2_gnn_W1"].shape[1]
    LAYERS = ins["L3_gnn_Ws"].shape[0]
    EPS = 1e-5
    SHIFT = 6
    WIN = 1 << SHIFT
    HALF = N // 2
    TOP = 1e8
    TOP_X = 18.42
    QUADS = T // 4
    assert N == D == 512 and T % 8 == 4 and 2 * DE == P and FT == 2 * NT

    ctx = ExitStack()
    with ctx:
        def sb(name, shape, dt=f32, to=ctx):
            return to.enter_context(nc.sbuf_tensor(name, shape, dt))

        src_table = nc.dram_tensor("src_table", (N, D), f32, kind="Internal").ap()
        dst_table = nc.dram_tensor("dst_table", (N, D), f32, kind="Internal").ap()
        eaT_dram = nc.dram_tensor("eaT_dram", (P, E), f32, kind="Internal").ap()

        ident = sb("ident", [P, P])
        ident_r = sb("ident_r", [P, P], f32r)
        iota_n = sb("iota_n", [P, N])
        ones = sb("ones", [P, 1])
        zrow = sb("zrow", [1, N], bf16)
        eps_c = sb("eps_c", [P, 1])
        dst_f = sb("dst_f", [P, T])
        src_f = sb("src_f", [P, T])
        dst_i = sb("dst_i", [P, T], i32)
        src_i = sb("src_i", [P, T], i32)
        idx_now = sb("idx_now", [P, 4, 4], i32)
        win_f = sb("win_f", [T, 2])
        win_v = sb("win_v", [T, 2], i32)
        win_i = sb("win_i", [T, 2], i32)
        win = sb("win", [1, 2 * T], i32)
        xres = sb("xres", [P, NT, D])
        h = sb("h", [P, NT, D])
        with ExitStack() as a:
            hT = sb("hT", [P, NT, N], to=a)
        hT_hi = sb("hT_hi", [P, NT, N], f32r)
        CT = sb("CT", [P, NT, N])
        ea_sums = sb("ea_sums", [P, N])
        EAT = ea_sums[0:DE + 1, :]
        deg = sb("deg", [P, NT])
        dlog = sb("dlog", [P, NT])
        dinv = sb("dinv", [P, NT])
        bcol = sb("bcol", [P, 20])
        bn_st = sb("bn_st", [P, 8, NT, 6])
        bn_mv = sb("bn_mv", [P, 8, NT, 2])
        lnv = sb("lnv", [P, 8, NT])
        rstd = sb("rstd", [P, 8, NT])
        nbias = sb("nbias", [P, 8, NT])
        with ExitStack() as a:
            WA = sb("WA", [P, 8, NT * D], to=a)
        WA_r = sb("WA_r", [P, 8, NT * D], f32r)
        brow = sb("brow", [P, 7, D])
        w1c_hi = sb("w1c_hi", [P, D], f32r)
        w1c_lo = sb("w1c_lo", [DE, D], f32r)
        b2_rows = sb("b2_rows", [P, D], f32r)
        ones_r = sb("ones_r", [P, P], f32r)
        w2_hi = sb("w2_hi", [P, NT, D], f32r)
        w2_lo = sb("w2_lo", [P, NT, D], f32r)
        l2w1 = sb("l2w1", [P, NT, DH])
        l2w2 = sb("l2w2", [DH, D])
        l2b1 = sb("l2b1", [P, DH])
        t1 = sb("t1", [P, NT, DH])
        t2 = sb("t2", [P, NT, DH])
        a2 = sb("a2", [DH, N])

        e_raw = WA[:, 5:8, :].rearrange("p l w -> p (l w)")[:, 0:T * DE].rearrange("p (t d) -> p t d", d=DE)
        G = WA[:, 0:2, :].rearrange("p s (j d) -> p (s j) d", d=D)
        we_flat = WA[0:DE + 1, 3, :]

        def slot(k):
            return WA[:, k, :].rearrange("p (t d) -> p t d", d=D)

        with ExitStack() as a:
            y = sb("y", [P, NT, D], to=a)
            mask = sb("mask", [P, NT, N], to=a)
            qT = sb("qT", [P, NT, N], to=a)
            kT = sb("kT", [P, NT, N], to=a)
            v = sb("v", [P, NT, D], to=a)
            S = sb("S", [P, 2, HEADS, HALF], to=a)
            smx = sb("smx", [P, HALF], to=a)
            ssm = sb("ssm", [P, 2, HALF], to=a)
        S3 = [WA[:, k, :].rearrange("p (h n) -> p h n", n=HALF) for k in (0, 1)] + [S[:, 0]]
        unmask = hT
        w1c_raw = mask[:, 0, :]
        b2_raw = mask[0:33, 1, :]
        with ExitStack() as a:
            eaT_out = sb("eaT_out", [P, T * P], to=a)
            idx_i = sb("idx_i", [T, 2, P], i32, to=a)
            idx_f = sb("idx_f", [T, 2, P], to=a)
            e_split = sb("e_split", [P, 4, P], f32r, to=a)
            oh_src = sb("oh_src", [P, 4, N], f32r, to=a)
            oh_cnt = sb("oh_cnt", [P, 4, N], f32r, to=a)
        with ExitStack() as a:
            sb("y_mask_below", [P, 2 * NT * D], to=a)
            ff_hi = sb("ff_hi", [P, FT, N], f32r, to=a)
            f2_hi_v = sb("f2_hi_v", [P, NT, D], f32r, to=a)
            ff_lo = sb("ff_lo", [P, FT, N], f32r, to=a)
        with ExitStack() as a:
            sb("S0_below", [P, 6 * NT * D], to=a)
            hT0_lo = sb("hT0_lo", [P, NT, N], f32r, to=a)
        ff_now = mask[:, 2:4, :]
        with ExitStack() as a:
            h_hi = sb("h_hi", [P, 2, NT, 2 * P], f32r, to=a)
            h_lo = sb("h_lo", [P, 2, NT, 2 * P], f32r, to=a)
            eaT = sb("eaT", [P, 2, 2 * P], f32r, to=a)
            eA = sb("eA", [P, 2, D], to=a)
            uA = sb("uA", [P, 2, D], to=a)
            mA = sb("mA", [P, 2, D], to=a)
            eB = sb("eB", [P, 2, D], to=a)
            uB = sb("uB", [P, 2, D], to=a)
            mB = sb("mB", [P, 4, D], to=a)
            oh = sb("oh", [P, 4, N], to=a)
        with ExitStack() as a:
            sb("y_below", [P, NT * D], to=a)
            h3_lo = sb("h3_lo", [P, NT, D], f32r, to=a)
            hT_lo = sb("hT_lo", [P, NT, N], f32r, to=a)
            wx_hi = sb("wx_hi", [P, LAYERS * NT * D], f32r, to=a)
            h3_hi = sb("h3_hi", [P, NT, D], f32r, to=a)
        qkv_hi, qkv_lo = ([WA_r[:, k, :].rearrange("p (t d) -> p t d", d=D) for k in ks] for ks in ((3, 4, 5), (0, 1, 2)))
        f2_hi = (WA_r[:, 3, :].rearrange("p (t d) -> p t d", d=D), f2_hi_v)
        f2_lo = [WA_r[:, k, :].rearrange("p (t d) -> p t d", d=D) for k in (6, 7)]
        wx_raw = WA[:, 5:8, :].rearrange("p l w -> p (l w)")
        wx_lo = WA_r[:, 5:8, :].rearrange("p l w -> p (l w)")
        CT_lo, CT_hi = (WA_r[:, k, :].rearrange("p (t d) -> p t d", d=D) for k in (2, 4))

        banks = ctx.enter_context(nc.psum_tensor("banks", [P, 8, 512], f32))
        bank = [banks[:, i, :] for i in range(8)]

        s = {name: ctx.enter_context(nc.semaphore(name)) for name in """
            consts ident_done idx_in idx_float idx_T idx_taken win_range win_shift win_row
            x_in wq_in wk_in wv_in wo_in f1_in f2_in bcol_in
            rows_in
            w1a_in w1b_in w2_in w3_in w4_in wx_in affine_in we_in l2_in b2_in w1c_in
            rows1_in
            ea_in0 ea_in1 ea_in2 ea_in3 ea_hi ea_lo src_hot dst_hot counted ea_evac ea_out
            counts ct_taken cT_ready mask_ready unmask_ready deg_ready dlog_done dinv_ready
            ln_stats ln_mv ln_log ln_rstd ln_nb h_ready hT_ready hT_taken hT_low
            qkv_ready qkv_taken w2hi_done w2lo_done w1chi_done w1clo_done b2_done
            s_ready s_masked s_max s_sub s_exp s_sum s_log s_rec att_ready att_rest av_done av_taken
            eat_ready eat_taken hb_done wo_ready y1_ready y_scaled ff_hi ff_lo ff1_ready ff1_taken ff2_ready y2_ready
            x1_ready
            tab_ready ptab_taken qtab_taken src_stored dst_stored idx_now_set gath0 gath1 gath2 gath3 eaT0 eaT1
            preA expA topA sqA logA recA mishA hiA loA
            preB expB topB sqB logB recB mishB hotB scattered
            agg_ready agg_taken u_ready u_x u_exp u_top u_sq u_log u_rec u_mish
            w4_ready x2_ready
            t1_ready t1_taken a1_ready a1_sum a1_bias t2_done a2_ready a2_taken xb_done
            o2_ready x3_ready
            m_agg m_taken m_tlo m_hi m_lo hi_done lo_done m_msg m_y m_shifted m_h result stored
            """.split()}

        block = ctx.enter_context(nc.Block())

        def need(eng, semaphore, value):
            if not isinstance(value, int) or value > 0:
                eng.wait_ge(semaphore, value)

        def rows(ap):
            return ap.rearrange("(t p) d -> p t d", p=P)

        def spread(name):
            return ins[name].rearrange("(a d) -> a d", a=1).to_broadcast([P, D])

        def ws(w):
            return bass.ds(w * WIN, WIN)

        EA_PARTS = ((0, 1), (1, 5), (5, 11), (11, QUADS))
        EAT_PARTS = ((0, 5), (5, 10), (10, 15), (15, QUADS))
        SHARE = HEADS // 2
        BV, BO, G1, BE1, B2, G2, BE2 = range(7)
        B1, B4, GAMMA, BETA, L2B2 = range(5)
        LN_IN0, LN_A, LN_B, LN_IN1, LN_C, LN_IN2, LN_IN3, LN_L3 = range(8)

        APART = {LN_B: 0, LN_C: 1}
        ORDER = [(k, t) for k in (LN_IN0, LN_A) for t in range(NT)]
        for k, after in ((LN_B, LN_IN1), (LN_C, LN_IN2)):
            for t in range(NT + APART[k]):
                ORDER += [(k, t)] * (t < NT) + [(after, t - APART[k])] * (t >= APART[k])
        ORDER += [(k, t) for k in (LN_IN3, LN_L3) for t in range(NT)]

        def nth(k, t):
            return ORDER.index((k, t)) + 1

        @block.sync
        def _(eng):
            eng.dma_start(idx_i[:, 0, :], ins["dst"].rearrange("(t p) -> t p", p=P)).then_inc(s["idx_in"], 16)
            eng.dma_start(idx_i[:, 1, :], ins["src"].rearrange("(t p) -> t p", p=P)).then_inc(s["idx_in"], 16)
            attributes = ins["edge_attr_64"].rearrange("(t p) d -> p t d", p=P)
            for (a, b), loaded in zip(EA_PARTS, (s["ea_in0"], s["ea_in1"], s["ea_in2"], s["ea_in3"])):
                eng.dma_start(e_raw[:, 4 * a:4 * b, :], attributes[:, 4 * a:4 * b, :]).then_inc(loaded, 16)
                if a == 0:
                    eng.dma_start(xres[:, :, :], rows(ins["x"])).then_inc(s["x_in"], 16)

            eng.wait_ge(s["win_shift"], 1)
            eng.dma_start(win[0:1, :], win_i[:, :]).then_inc(s["win_row"], 16)
            for a, b in EAT_PARTS:
                eng.wait_ge(s["ea_evac"], 2 * b)
                eng.dma_start(eaT_dram[:, a * 4 * P:b * 4 * P], eaT_out[:, a * 4 * P:b * 4 * P]).then_inc(s["ea_out"], 16)

            w1 = ins["L1_gnn_W1"]
            eng.wait_ge(s["qkv_ready"], 3 * NT)
            eng.dma_start(slot(2), rows(ins["L1_gnn_W2"])).then_inc(s["w2_in"], 16)
            eng.wait_ge(s["av_done"], 2 * NT)
            eng.dma_start(slot(0), rows(w1[0:D, :])).then_inc(s["w1a_in"], 16)
            eng.dma_start(slot(1), rows(w1[D:2 * D, :])).then_inc(s["w1b_in"], 16)
            eng.wait_ge(s["qkv_taken"], 3 * NT)
            eng.dma_start(brow[:, B1, :], spread("L1_gnn_b1")).then_inc(s["rows1_in"], 16)
            eng.wait_ge(s["hb_done"], NT)
            eng.dma_start(brow[:, B4, :], spread("L1_gnn_b4")).then_inc(s["rows1_in"], 16)
            eng.wait_ge(s["h_ready"], 2 * NT)
            eng.dma_start(brow[:, GAMMA, :], spread("L1_gnn_gamma")).then_inc(s["rows1_in"], 16)
            eng.dma_start(brow[:, BETA, :], spread("L1_gnn_beta")).then_inc(s["rows1_in"], 16)
            eng.wait_ge(s["ff2_ready"], NT)
            for c in range(2):
                eng.dma_start(slot(3 + c), rows(ins["L1_gnn_W3"][c * D:(c + 1) * D, :])).then_inc(s["w3_in"], 16)
            eng.wait_ge(s["hb_done"], 2 * NT)
            eng.dma_start(brow[:, L2B2, :], spread("L2_gnn_b2")).then_inc(s["rows1_in"], 16)
            eng.wait_ge(s["w2lo_done"], NT)
            eng.dma_start(slot(2), rows(ins["L1_gnn_W4"])).then_inc(s["w4_in"], 16)
            eng.wait_ge(s["ff2_ready"], NT)
            for l in range(LAYERS):
                eng.dma_start(slot(5 + l), rows(ins["L3_gnn_Ws"][l, 0:D, :])).then_inc(s["wx_in"], 16)

            for t in range(NT):
                eng.wait_ge(s["ptab_taken"], t + 1)
                eng.dma_start(src_table[t * P:(t + 1) * P, :], y[:, t, :]).then_inc(s["src_stored"], 16)
            for t in range(NT):
                eng.wait_ge(s["qtab_taken"], t + 1)
                eng.dma_start(dst_table[t * P:(t + 1) * P, :], v[:, t, :]).then_inc(s["dst_stored"], 16)
            def load_group(g, k, loaded):
                eng.dma_start(eaT[:, k, :].bitcast(f32), eaT_dram[:, bass.ds(g * (2 * P), 2 * P)]).then_inc(loaded, 16)

            eng.wait_ge(s["src_stored"], 16 * NT)
            eng.wait_ge(s["dst_stored"], 16 * NT)
            eng.wait_ge(s["ea_out"], 16 * len(EAT_PARTS))
            load_group(0, 0, s["eaT0"])
            load_group(1, 1, s["eaT1"])
            with eng.Fori(0, QUADS - 1) as i:
                eng.wait_ge(s["preA"], 4 * i + 2)
                load_group(2 * i + 2, 0, s["eaT0"])
                eng.wait_ge(s["preA"], 4 * i + 4)
                load_group(2 * i + 3, 1, s["eaT1"])

            eng.wait_ge(s["preA"], T)
            for l in range(LAYERS):
                eng.dma_start(WA[:, 0, l * D:(l + 1) * D], ins["L3_gnn_gammas"][l:l + 1, :].to_broadcast([P, D])).then_inc(s["affine_in"], 16)
                eng.dma_start(WA[:, 1, l * D:(l + 1) * D], ins["L3_gnn_betas"][l:l + 1, :].to_broadcast([P, D])).then_inc(s["affine_in"], 16)
            eng.wait_ge(s["u_ready"], NT)
            for l in range(LAYERS):
                eng.dma_start(we_flat[0:DE, l * D:(l + 1) * D], ins["L3_gnn_Ws"][l, D:D + DE, :]).then_inc(s["we_in"], 16)
                eng.dma_start(we_flat[DE:DE + 1, l * D:(l + 1) * D], ins["L3_gnn_bs"][l:l + 1, :]).then_inc(s["we_in"], 16)
            for t in range(NT):
                eng.wait_ge(s["result"], t + 1)
                eng.dma_start(out[t * P:(t + 1) * P, :], y[:, t, :]).then_inc(s["stored"], 16)
            eng.wait_ge(s["stored"], 16 * NT)

        @block.gpsimd
        def _(eng):
            eng.memset(ident[:, :], 0.0).then_inc(s["consts"], 1)
            eng.iota(iota_n[:, :], pattern=[[1, N]], base=0, channel_multiplier=0,
                     allow_small_or_imprecise_dtypes=True).then_inc(s["consts"], 1)
            eng.memset(ones[:, :], 1.0).then_inc(s["consts"], 1)
            eng.memset(zrow[:, :], 0.0).then_inc(s["consts"], 1)
            eng.memset(eps_c[:, :], EPS).then_inc(s["consts"], 1)
            eng.memset(ones_r[:, :].bitcast(f32), 1.0).then_inc(s["consts"], 1)
            eng.memset(b2_rows[:, :].bitcast(f32), 0.0).then_inc(s["consts"], 1)
            eng.wait_ge(s["consts"], 7)
            eng.affine_select(out=ident[:, :], in_=ident[:, :], compare_op=ALU.not_equal, fill=1.0, base=0,
                              pattern=[[-1, P]], channel_multiplier=1).then_inc(s["ident_done"], 1)
            eng.wait_ge(s["counted"], 4)
            eng.dma_start(slot(0), rows(ins["L0_gnn_Wq"])).then_inc(s["wq_in"], 16)
            eng.dma_start(slot(1), rows(ins["L0_gnn_Wk"])).then_inc(s["wk_in"], 16)
            eng.dma_start(slot(2), rows(ins["L0_gnn_Wv"])).then_inc(s["wv_in"], 16)
            eng.wait_ge(s["counted"], 16)
            for name, lo, n in (("L0_gnn_bq", 0, 4), ("L0_gnn_bk", 4, 4), ("L0_gnn_b1", 8, 8), ("L1_gnn_b3", 16, 4)):
                eng.dma_start(bcol[:, lo:lo + n], ins[name].rearrange("(c p) -> p c", p=P),
                              allow_slow_non_contiguous=True).then_inc(s["bcol_in"], 16)
            eng.wait_ge(s["counted"], 24)
            for name, k in (("bv", BV), ("bo", BO), ("g1", G1), ("be1", BE1), ("b2", B2), ("g2", G2), ("be2", BE2)):
                eng.dma_start(brow[:, k, :], spread("L0_gnn_" + name)).then_inc(s["rows_in"], 16)

            def split_qkv(j):
                eng.wait_ge((s["wq_in"], s["wk_in"], s["wv_in"])[j], 16)
                for c in range(NT):
                    eng.tensor_copy(qkv_hi[j][:, c, :], slot(j)[:, c, :]).then_inc(s["hi_done"], 1)
                for c in range(NT):
                    eng.wait_ge(s["hi_done"], NT * j + c + 1)
                    eng.tensor_tensor(qkv_lo[j][:, c, :], slot(j)[:, c, :], qkv_hi[j][:, c, :].bitcast(f32), ALU.subtract
                                      ).then_inc(s["lo_done"], 1)

            split_qkv(0)
            split_qkv(1)
            eng.wait_ge(s["counted"], T)
            split_qkv(2)
            for c in range(2):
                eng.dma_start(slot(6 + c), rows(ins["L0_gnn_W2"][c * D:(c + 1) * D, :])).then_inc(s["f2_in"], 16)
            eng.dma_start(l2w1[:, :, :], rows(ins["L2_gnn_W1"])).then_inc(s["l2_in"], 16)
            eng.dma_start(l2w2[:, :], ins["L2_gnn_W2"]).then_inc(s["l2_in"], 16)
            eng.dma_start(l2b1[:, :], ins["L2_gnn_b1"].rearrange("(a d) -> a d", a=1).to_broadcast([P, DH])).then_inc(s["l2_in"], 16)

            eng.wait_ge(s["qkv_ready"], 3 * NT)
            eng.dma_start(slot(3), rows(ins["L0_gnn_Wo"])).then_inc(s["wo_in"], 16)
            for c in range(2):
                eng.dma_start(slot(4 + c), rows(ins["L0_gnn_W1"][:, c * D:(c + 1) * D])).then_inc(s["f1_in"], 16)

            for u in range(2 * NT):
                rest = S3[u % 3][:, SHARE:HEADS, :]
                eng.wait_ge(s["s_masked"], u + 1)
                eng.tensor_tensor(rest, rest, ssm[:, u % 2, :].unsqueeze(1).to_broadcast([P, HEADS - SHARE, HALF]),
                                  ALU.mult).then_inc(s["att_rest"], 1)
            for half in range(2):
                eng.dma_start(w1c_raw[half * DE:(half + 1) * DE, :], ins["L1_gnn_W1"][2 * D:2 * D + DE, :]).then_inc(s["w1c_in"], 16)
                eng.dma_start(b2_raw[32 * half:32 * half + 1, :], ins["L1_gnn_b2"].rearrange("(a d) -> a d", a=1)).then_inc(s["b2_in"], 16)

            for c in range(FT):
                eng.wait_ge(s["hi_done"], 3 * NT + c + 1)
                eng.tensor_tensor(f2_lo[c // NT][:, c % NT, :], slot(6 + c // NT)[:, c % NT, :],
                                  f2_hi[c // NT][:, c % NT, :].bitcast(f32), ALU.subtract).then_inc(s["lo_done"], 1)

            gathered = (s["gath0"], s["gath1"], s["gath2"], s["gath3"])

            def gather_src(g, k):
                eng.tensor_copy(idx_now[:, k, 0:2], src_i[:, bass.ds(2 * g, 2)]).then_inc(s["idx_now_set"], 1)
                eng.tensor_copy(idx_now[:, k, 2:4], dst_i[:, bass.ds(2 * g, 2)]).then_inc(s["idx_now_set"], 1)
                eng.wait_ge(s["idx_now_set"], 2 * g + 2)
                eng.nop(nofuse=True)
                for j in range(2):
                    eng.indirect_dma_start(out=G[:, 2 * k + j, :], out_offset=None, in_=src_table,
                                           in_offset=bass.IndirectOffsetOnAxis(ap=idx_now[:, k, j:j + 1], axis=0)
                                           ).then_inc(gathered[k], 16)

            def gather_dst(k, before):
                eng.wait_ge(gathered[k], 64 * before + 32)
                eng.nop(nofuse=True)
                for j in range(2):
                    eng.indirect_dma_start(out=G[:, 2 * k + j, :], out_offset=None, in_=dst_table,
                                           in_offset=bass.IndirectOffsetOnAxis(ap=idx_now[:, k, 2 + j:3 + j], axis=0),
                                           compute_op=ALU.add).then_inc(gathered[k], 16)

            eng.wait_ge(s["idx_taken"], 4)
            eng.wait_ge(s["src_stored"], 16 * NT)
            for g in range(6):
                if g == 2:
                    eng.wait_ge(s["tab_ready"], 2 * NT)
                if g >= 4:
                    eng.wait_ge(s["preA"], 2 * (g - 4) + 2)
                gather_src(g, g % 4)
                if g == 1:
                    eng.wait_ge(s["dst_stored"], 16 * NT)
                if g:
                    gather_dst((g - 1) % 4, (g - 1) // 4)
            with eng.Fori(0, (2 * QUADS - 6) // 4) as i:
                for j in range(4):
                    eng.wait_ge(s["preA"], 8 * i + (2 * j + 6))
                    gather_src(4 * i + (6 + j), (2 + j) % 4)
                    gather_dst((1 + j) % 4, i + (5 + j) // 4)
            gather_dst((2 * QUADS - 1) % 4, (2 * QUADS - 1) // 4)

            for c in range(LAYERS * NT):
                at = slice(c * D, (c + 1) * D)
                eng.wait_ge(s["hi_done"], 3 * NT + FT + c + 1)
                eng.tensor_tensor(wx_lo[:, at], wx_raw[:, at], wx_hi[:, at].bitcast(f32), ALU.subtract
                                  ).then_inc(s["lo_done"], 1)
            eng.wait_ge(s["w4_ready"], NT)
            for c in range(NT):
                eng.wait_ge(s["hi_done"], 3 * NT + FT + LAYERS * NT + c + 1)
                eng.tensor_tensor(CT_lo[:, c, :], CT[:, c, :], CT_hi[:, c, :].bitcast(f32), ALU.subtract
                                  ).then_inc(s["lo_done"], 1)

            def low_h(t, later=0):
                eng.wait_ge(s["m_hi"], later + (t + 1))
                eng.wait_ge(s["m_h"], later + (t + 1))
                eng.tensor_tensor(h3_lo[:, t, :], h[:, t, :], h3_hi[:, t, :].bitcast(f32), ALU.subtract).then_inc(s["m_lo"], 1)

            for t in range(NT):
                low_h(t)
            with eng.Fori(0, LAYERS) as l:
                for t in range(NT):
                    low_h(t, NT * l + NT)

        @block.scalar
        def _(eng):
            eng.preload_act_table_set("natural_log_exp_and_others")
            eng.wait_ge(s["consts"], 7)

            def inverse_deviation(k, t, later=0):
                eng.wait_ge(s["ln_mv"], later + nth(k, t))
                eng.activation(lnv[:, k, t:t + 1], bn_mv[:, k, t, 1:2], ACT.Ln, bias=eps_c[:, 0:1]).then_inc(s["ln_log"], 1)
                eng.wait_ge(s["ln_log"], later + nth(k, t))
                eng.activation(rstd[:, k, t:t + 1], lnv[:, k, t:t + 1], ACT.Exp, scale=-0.5).then_inc(s["ln_rstd"], 1)

            def relu_norm(k, t, before, done):
                eng.wait_ge(s["ln_nb"], NT * before + t + 1)
                eng.activation(h[:, t, :], xres[:, t, :], ACT.Relu, bias=nbias[:, k, t:t + 1],
                               scale=rstd[:, k, t:t + 1]).then_inc(done, 1)

            def take_hT(before, t, pair, to=hT):
                eng.wait_ge(s["hT_ready"], before + t + 1)
                eng.activation(to[:, :, t * P:(t + 1) * P], pair[t % 2][:, :].rearrange("p (c n) -> p c n", n=P),
                               ACT.Copy).then_inc(s["hT_taken"], 1)

            def end_block(k, after, before):
                d = APART[k]
                for t in range(NT + 2 * d + 1):
                    if t < NT:
                        inverse_deviation(k, t)
                    if d <= t < NT + d:
                        inverse_deviation(after, t - d)
                    if 2 * d <= t < NT + 2 * d:
                        relu_norm(after, t - 2 * d, before, s["h_ready"])
                    if t > 2 * d:
                        take_hT(NT * (before + 1), t - 2 * d - 1, bank[0:2])

            def high_parts(i, half):
                for q in (2 * half, 2 * half + 1):
                    need(eng, s["counted"], 4 * i + q - 3)
                    eng.activation(e_split[:, q, 0:DE], e_raw[:, bass.ds(4 * i + q, 1), :].rearrange("p a d -> p (a d)"),
                                   ACT.Copy).then_inc(s["ea_hi"], 1)

            def take_pair(i, half):
                eng.wait_ge(s["counted"], 4 * i + 2 * half + 2)
                eng.activation(eaT_out[:, bass.ds(i * (4 * P) + 2 * half * P, 2 * P)], bank[(5, 7)[half]][:, 0:2 * P], ACT.Copy
                               ).then_inc(s["ea_evac"], 1)

            eng.wait_ge(s["ident_done"], 1)
            eng.activation(ident_r[:, :], ident[:, :], ACT.Copy).then_inc(s["ident_done"], 1)
            eng.wait_ge(s["ea_in0"], 16)
            high_parts(0, 0)
            high_parts(0, 1)
            take_pair(0, 0)
            for (a, b), loaded in zip(EA_PARTS[1:], (s["ea_in1"], s["ea_in2"], s["ea_in3"])):
                eng.wait_ge(loaded, 16)
                with eng.Fori(a, b) as i:
                    high_parts(i, 0)
                    take_pair(i - 1, 1)
                    high_parts(i, 1)
                    take_pair(i, 0)
                for t in range(NT):
                    if a == 1:
                        inverse_deviation(LN_IN0, t)
                    if a == 5:
                        relu_norm(LN_IN0, t, 0, s["h_ready"])
            take_pair(QUADS - 1, 1)

            for t in range(NT):
                take_hT(0, t, bank[6:8], hT_hi)
            eng.wait_ge(s["counts"], 1)
            for t in range(NT):
                eng.activation(CT[:, t, :], bank[t][:, :], ACT.Copy).then_inc(s["ct_taken"], 1)
            eng.activation(ea_sums[:, :], bank[4][:, :], ACT.Copy).then_inc(s["ct_taken"], 1)
            eng.wait_ge(s["deg_ready"], NT)
            eng.activation(dlog[:, :], deg[:, :], ACT.Ln, bias=1.0).then_inc(s["dlog_done"], 1)
            eng.wait_ge(s["dlog_done"], 1)
            eng.activation(dinv[:, :], dlog[:, :], ACT.Exp, scale=-0.5).then_inc(s["dinv_ready"], 1)

            def take_half(half):
                eng.wait_ge(s["av_done"], NT * (half + 1))
                for t in range(NT):
                    at = slice(half * HALF, (half + 1) * HALF)
                    eng.activation(hT[:, t, at], bank[4 + t][:, at], ACT.Copy).then_inc(s["av_taken"], 1)

            for u in range(2 * NT):
                k = u % 2
                eng.wait_ge(s["s_sub"], 2 * u + 2)
                eng.activation(S3[u % 3], S3[u % 3], ACT.Exp).then_inc(s["s_exp"], 1)
                if u == NT + 1:
                    take_half(0)
                eng.wait_ge(s["s_sum"], u + 1)
                eng.activation(ssm[:, k, :], ssm[:, k, :], ACT.Ln).then_inc(s["s_log"], 1)
                eng.wait_ge(s["s_log"], u + 1)
                eng.activation(ssm[:, k, :], ssm[:, k, :], ACT.Exp, scale=-1.0).then_inc(s["s_rec"], 1)
                if u >= NT:
                    t = u - NT
                    eng.wait_ge(s["w2_in"], 16)
                    eng.activation(w2_hi[:, t, :], slot(2)[:, t, :], ACT.Copy).then_inc(s["w2hi_done"], 1)
            take_half(1)
            for t in range(NT + 1):
                if t < NT:
                    inverse_deviation(LN_A, t)
                if t == 1:
                    eng.wait_ge(s["eat_ready"], 1)
                    eng.activation(EAT[:, :], bank[6][0:DE + 1, :], ACT.Copy).then_inc(s["eat_taken"], 1)
                if t:
                    eng.wait_ge(s["wo_ready"], NT)
                    take_hT(NT, t - 1, bank[4:6])
            eng.wait_ge(s["w1c_in"], 32)
            eng.activation(w1c_hi[:, :], w1c_raw[:, :], ACT.Copy).then_inc(s["w1chi_done"], 1)
            eng.wait_ge(s["bcol_in"], 64)
            for f in range(FT):
                eng.wait_ge(s["ff1_ready"], f + 1)
                need(eng, s["ff_lo"], f - 1)
                eng.activation(ff_now[:, f % 2, :], bank[f % 4][:, :], ACT.Relu,
                               bias=bcol[:, 8 + f:9 + f]).then_inc(s["ff1_taken"], 1)
                eng.wait_ge(s["ff1_taken"], f + 1)
                eng.activation(ff_hi[:, f, :], ff_now[:, f % 2, :], ACT.Copy).then_inc(s["ff_hi"], 1)
                for c in range(2 * f, 2 * f + 2) if f < NT else ():
                    eng.wait_ge(s["f2_in"], 32)
                    eng.activation(f2_hi[c // NT][:, c % NT, :], slot(6 + c // NT)[:, c % NT, :], ACT.Copy
                                   ).then_inc(s["hi_done"], 1)
            end_block(LN_B, LN_IN1, 1)
            for t in range(NT):
                eng.wait_ge(s["tab_ready"], NT + t + 1)
                eng.activation(v[:, t, :], bank[t][:, :], ACT.Copy).then_inc(s["qtab_taken"], 1)

            def step(n, q, first=True, split=True, second=True, finish=True):
                p = q % 2
                if first:
                    eng.wait_ge(s["preA"], n + 1)
                    need(eng, s["sqA"], n - 1)
                    eng.activation(eA[:, p, :], bank[p][:, :], ACT.Exp).then_inc(s["expA"], 1)
                if finish:
                    eng.wait_ge(s["sqB"], n - 3)
                    eng.activation(uB[:, p, :], uB[:, p, :], ACT.Ln, bias=1.0, scale=0.5).then_inc(s["logB"], 1)
                    eng.wait_ge(s["logB"], n - 3)
                    eng.activation(uB[:, p, :], uB[:, p, :], ACT.Exp, scale=-1.0).then_inc(s["recB"], 1)
                if split:
                    m, k = (q - 1) % 2, (q - 1) % 4 // 2
                    eng.wait_ge(s["mishA"], n)
                    need(eng, s["preB"], n - 3 - m)
                    eng.activation(h_hi[:, k, 2 * m:2 * m + 2, :], mA[:, m, :].rearrange("p (c e) -> p c e", c=2),
                                   ACT.Copy).then_inc(s["hiA"], 1)
                if first:
                    eng.wait_ge(s["sqA"], n + 1)
                    eng.activation(uA[:, p, :], uA[:, p, :], ACT.Ln, bias=1.0, scale=0.5).then_inc(s["logA"], 1)
                    eng.wait_ge(s["logA"], n + 1)
                    eng.activation(uA[:, p, :], uA[:, p, :], ACT.Exp, scale=-1.0).then_inc(s["recA"], 1)
                if second:
                    eng.wait_ge(s["preB"], n - 2)
                    need(eng, s["sqB"], n - 4)
                    eng.activation(eB[:, 1 - p, :], bank[3 - p][:, :], ACT.Exp).then_inc(s["expB"], 1)

            for n in range(8):
                step(n, n % 4, split=n >= 1, second=n >= 3, finish=n >= 4)
            with eng.Fori(2, QUADS) as i:
                for q in range(4):
                    step(4 * i + q, q)
            for n in range(T, T + 4):
                step(n, n % 4, first=False, split=n == T, second=n < T + 3)

            eng.wait_ge(s["agg_ready"], 1)
            for t in range(NT):
                eng.activation(mask[:, t, :], bank[4 + t][:, :], ACT.Copy).then_inc(s["agg_taken"], 1)
            for f in range(NT):
                eng.wait_ge(s["u_top"], f + 1)
                eng.activation(v[:, f, :], v[:, f, :], ACT.Exp).then_inc(s["u_exp"], 1)
                if f:
                    finish_u = f - 1
                    eng.wait_ge(s["u_sq"], finish_u + 1)
                    eng.activation(v[:, finish_u, :], v[:, finish_u, :], ACT.Ln, bias=1.0, scale=0.5).then_inc(s["u_log"], 1)
                    eng.wait_ge(s["u_log"], finish_u + 1)
                    eng.activation(v[:, finish_u, :], v[:, finish_u, :], ACT.Exp, scale=-1.0).then_inc(s["u_rec"], 1)
            eng.wait_ge(s["u_sq"], NT)
            eng.activation(v[:, NT - 1, :], v[:, NT - 1, :], ACT.Ln, bias=1.0, scale=0.5).then_inc(s["u_log"], 1)
            eng.wait_ge(s["u_log"], NT)
            eng.activation(v[:, NT - 1, :], v[:, NT - 1, :], ACT.Exp, scale=-1.0).then_inc(s["u_rec"], 1)
            def high_weights(layers):
                for c in range(NT * layers[0], NT * (layers[-1] + 1)):
                    at = slice(c * D, (c + 1) * D)
                    eng.activation(wx_hi[:, at], wx_raw[:, at], ACT.Copy).then_inc(s["hi_done"], 1)

            eng.wait_ge(s["wx_in"], 16 * LAYERS)
            eng.wait_ge(s["u_mish"], NT)
            high_weights((0, 1))
            end_block(LN_C, LN_IN2, 2)
            high_weights((2,))
            for c in range(NT):
                eng.activation(CT_hi[:, c, :], CT[:, c, :], ACT.Copy).then_inc(s["hi_done"], 1)
            eng.wait_ge(s["a2_ready"], 1)
            eng.activation(a2[:, :], bank[3][0:DH, :], ACT.Copy).then_inc(s["a2_taken"], 1)
            for t in range(NT + 1):
                if t < NT:
                    inverse_deviation(LN_IN3, t)
                if t:
                    relu_norm(LN_IN3, t - 1, 3, s["m_h"])
                    eng.wait_ge(s["m_h"], t)
                    eng.activation(h3_hi[:, t - 1, :], h[:, t - 1, :], ACT.Copy).then_inc(s["m_hi"], 1)

            with eng.Fori(0, LAYERS) as l:
                for f in range(NT):
                    eng.wait_ge(s["m_agg"], NT * l + f + 1)
                    eng.activation(hT_hi[:, f, :], bank[f][:, :], ACT.Copy).then_inc(s["m_taken"], 1)
                for t in range(NT + 1):
                    if t < NT:
                        inverse_deviation(LN_L3, t, NT * l)
                    if t:
                        eng.wait_ge(s["m_shifted"], NT * l + t)
                        eng.activation(h3_hi[:, t - 1, :], y[:, t - 1, :], ACT.Relu).then_inc(s["m_hi"], 1)
                        eng.activation(h[:, t - 1, :], y[:, t - 1, :], ACT.Relu).then_inc(s["m_h"], 1)

        @block.tensor
        def _(eng):
            def transposes(src, t, to):
                for c in range(NT):
                    mm = eng.transpose(to[:, c * P:(c + 1) * P], src[:, t, c * P:(c + 1) * P], ident[:, :])
                return mm

            def product(to, lhs, rhs):
                for j, (a, b) in enumerate(zip(lhs, rhs)):
                    mm = eng.matmul(to, a, b, start=(j == 0), stop=(j == len(lhs) - 1))
                return mm

            def split_product(to, a, b, first, last):
                (a_hi, a_lo), (b_hi, b_lo) = a, b
                eng.matmul(to, a_hi, b_hi, start=first, stop=False)
                eng.matmul(to, a_hi, b_lo, start=False, stop=False)
                return eng.matmul(to, a_lo, b_hi, start=False, stop=last)

            def clear(to):
                eng.matmul(to, zrow[:, 0:to.shape[0]], zrow[:, :], start=True, stop=False, skip_group_check=True)

            def close(to):
                return eng.matmul(to, zrow[:, 0:to.shape[0]], zrow[:, :], start=False, stop=True, skip_group_check=True)

            eng.wait_ge(s["ident_done"], 1)
            eng.wait_ge(s["idx_float"], 1)
            eng.transpose(bank[6][:, 0:T], idx_f[:, 0, :], ident[0:T, 0:T])
            eng.transpose(bank[6][:, P:P + T], idx_f[:, 1, :], ident[0:T, 0:T]).then_inc(s["idx_T"], 1)

            eng.wait_ge(s["ident_done"], 2)

            def count(n, q, first=False):
                eng.wait_ge(s["src_hot"], n + 1)
                eng.wait_ge(s["dst_hot"], n + 1)
                for t in range(NT):
                    eng.matmul(bank[t][:, :], oh_src[:, q, t * P:(t + 1) * P], oh_cnt[:, q, :],
                               start=first, stop=False, skip_group_check=True)
                eng.wait_ge(s["ea_lo"], n + 1)
                eng.matmul(bank[4][:, :], e_split[:, q, :], oh_cnt[:, q, :], start=first, stop=False, skip_group_check=True)
                eng.matmul(bank[(5, 7)[q // 2]][:, (q % 2) * P:(q % 2 + 1) * P], e_split[:, q, :], ident_r[:, :],
                           start=True, stop=True).then_inc(s["counted"], 1)

            for q in range(4):
                count(q, q, first=(q == 0))
            with eng.Fori(1, QUADS) as i:
                for q in range(4):
                    if q % 2 == 0:
                        eng.wait_ge(s["ea_evac"], 2 * i - 1 + q // 2)
                    count(4 * i + q, q)
            for t in range(NT + 1):
                mm = close(bank[t][:, :])
            mm.then_inc(s["counts"], 1)

            def transpose_h(before, t, pair):
                eng.wait_ge(s["h_ready"], before + t + 1)
                if t >= 2:
                    eng.wait_ge(s["hT_taken"], before + t - 1)
                transposes(h, t, pair[t % 2]).then_inc(s["hT_ready"], 1)

            eng.wait_ge(s["idx_taken"], 4)
            eng.wait_ge(s["ea_evac"], 2 * QUADS)
            for t in range(NT):
                if t >= 2:
                    eng.wait_ge(s["hT_low"], t - 1)
                transpose_h(0, t, bank[6:8])

            def project_in(n):
                j, t = n // NT, n % NT
                eng.wait_ge(s["lo_done"], NT * (j + 1))
                if n >= 2:
                    eng.wait_ge(s["qkv_taken"], n - 1)
                at = slice(t * P, (t + 1) * P)
                for c in range(NT):
                    w, x = (qkv_hi[j][:, c, :], qkv_lo[j][:, c, :]), (hT_hi[:, c, :], hT0_lo[:, c, :])
                    a, b = (w, x) if j < 2 else (x, w)
                    mm = split_product(bank[6 + n % 2], (a[0][:, at], a[1][:, at]), b, c == 0, c == NT - 1)
                mm.then_inc(s["qkv_ready"], 1)

            eng.wait_ge(s["hT_low"], NT)
            for n in range(NT):
                project_in(n)
            eng.wait_ge(s["ct_taken"], NT)
            for t in range(NT):
                for c in range(NT):
                    mm = eng.transpose(bank[t][:, c * P:(c + 1) * P], CT[:, c, t * P:(t + 1) * P], ident[:, :])
                mm.then_inc(s["cT_ready"], 1)
            for n in range(NT, 2 * NT):
                project_in(n)

            def place(hd):
                return 4 * (hd // 4) + 2 * (hd % 2) + hd % 4 // 2

            def scores(u):
                half, m = u // NT, u % NT
                for hd in range(HEADS):
                    if hd % 4 == 0:
                        need(eng, s["s_sub"], 2 * u - 1 + hd // 4 if u else 0)
                    at, lo = place(hd), HD * (hd % 2)
                    mm = eng.matmul(bank[at // 2][:, at % 2 * HALF:(at % 2 + 1) * HALF],
                                    kT[lo:lo + HD, hd // 2, m * P:(m + 1) * P],
                                    qT[lo:lo + HD, hd // 2, half * HALF:(half + 1) * HALF], start=True, stop=True)
                mm.then_inc(s["s_ready"], 1)

            def uniform(u):
                half, m = u // NT, u % NT
                eng.wait_ge(s["unmask_ready"], m + 1)
                if m == 0:
                    need(eng, s["av_taken"], NT * half)
                for c in range(NT):
                    eng.matmul(bank[4 + c][:, half * HALF:(half + 1) * HALF], v[:, m, c * P:(c + 1) * P],
                               unmask[:, m, half * HALF:(half + 1) * HALF], start=(m == 0), stop=False, skip_group_check=True)

            def attend(u):
                half, m = u // NT, u % NT
                eng.wait_ge(s["att_ready"], u + 1)
                eng.wait_ge(s["att_rest"], u + 1)
                for hd in range(HEADS):
                    lo = HD * (hd % 2)
                    mm = eng.matmul(bank[4 + hd // 2][lo:lo + HD, half * HALF:(half + 1) * HALF],
                                    v[:, m, hd * HD:(hd + 1) * HD], S3[u % 3][:, place(hd), :],
                                    start=False, stop=(m == NT - 1), skip_group_check=True)
                mm.then_inc(s["av_done"], 1)

            def project(t):
                product(bank[t][:, :], [hT[:, c, t * P:(t + 1) * P] for c in range(NT)],
                        [slot(3)[:, c, :] for c in range(NT)]).then_inc(s["wo_ready"], 1)

            eng.wait_ge(s["mask_ready"], NT)
            eng.wait_ge(s["deg_ready"], NT)
            eng.wait_ge(s["qkv_taken"], 2 * NT)
            scores(0)
            project_in(2 * NT)
            project_in(2 * NT + 1)
            scores(1)
            project_in(2 * NT + 2)
            project_in(2 * NT + 3)
            eng.wait_ge(s["qkv_taken"], 3 * NT)
            eng.wait_ge(s["ct_taken"], NT + 1)
            for u in range(2, 2 * NT + 2):
                if u < 2 * NT:
                    scores(u)
                for w in {2: [0], 3: [1], 4: [2], 5: [3], 6: [4], 7: [5, 6], 8: [7]}.get(u, []):
                    uniform(w)
                if u == 2 * NT + 1:
                    eng.wait_ge(s["wo_in"], 16)
                    eng.wait_ge(s["av_taken"], NT)
                    eng.wait_ge(s["s_sub"], 4 * NT)
                    project(0)
                attend(u - 2)
            project(1)
            eng.wait_ge(s["av_taken"], 2 * NT)
            project(2)
            project(3)
            eng.matmul(bank[6][0:DE, :], ident[:, 0:DE], ea_sums[:, :], start=True, stop=False)
            eng.matmul(bank[6][0:DE, :], ident[:, DE:P], ea_sums[:, :], start=False, stop=True)
            for c in range(NT):
                mm = eng.matmul(bank[6][DE:DE + 1, :], ones[:, 0:1], CT[:, c, :], start=(c == 0), stop=(c == NT - 1))
            mm.then_inc(s["eat_ready"], 1)

            for t in range(NT):
                transpose_h(NT, t, bank[4:6])
            eng.wait_ge(s["hT_taken"], 2 * NT)
            eng.wait_ge(s["y1_ready"], NT)
            eng.wait_ge(s["f1_in"], 32)
            for f in range(FT):
                if f >= 4:
                    eng.wait_ge(s["ff1_taken"], f - 3)
                product(bank[f % 4][:, :], [slot(4 + f // NT)[:, c, (f % NT) * P:(f % NT + 1) * P] for c in range(NT)],
                        [hT[:, c, :] for c in range(NT)]).then_inc(s["ff1_ready"], 1)
            eng.wait_ge(s["eat_taken"], 1)
            for t in range(NT):
                at = slice(t * P, (t + 1) * P)
                for c in range(FT):
                    if t == 0:
                        eng.wait_ge(s["ff_lo"], c + 1)
                        eng.wait_ge(s["lo_done"], 3 * NT + c + 1)
                    mm = split_product(bank[4 + t], (ff_hi[:, c, at], ff_lo[:, c, at]),
                                       (f2_hi[c // NT][:, c % NT, :], f2_lo[c // NT][:, c % NT, :]), c == 0, c == FT - 1)
                mm.then_inc(s["ff2_ready"], 1)
                if t:
                    transpose_h(2 * NT, t - 1, bank[0:2])

            def table_by_src(i):
                eng.wait_ge(s["hT_taken"], 2 * NT + i + 1)
                eng.wait_ge(s["y2_ready"], i + 1)
                product(bank[4 + i][:, :], [hT[:, c, i * P:(i + 1) * P] for c in range(NT)],
                        [slot(0)[:, c, :] for c in range(NT)]).then_inc(s["tab_ready"], 1)

            eng.wait_ge(s["w1a_in"], 16)
            for i in range(NT - 1):
                table_by_src(i)
            transpose_h(2 * NT, NT - 1, bank[0:2])
            table_by_src(NT - 1)
            eng.wait_ge(s["w1b_in"], 16)
            for t in range(NT):
                product(bank[t][:, :], [hT[:, c, t * P:(t + 1) * P] for c in range(NT)],
                        [slot(1)[:, c, :] for c in range(NT)]).then_inc(s["tab_ready"], 1)

            def first_layer(n, q, quad, g, g_use):
                p, k = q % 2, q // 2
                if p == 0:
                    eng.wait_ge((s["gath0"], s["gath1"], s["gath2"], s["gath3"])[g], 64 * g_use + 64)
                    eng.wait_ge((s["eaT0"], s["eaT1"])[k], 16 * quad + 16)
                need(eng, s["mishA"], n - 1)
                for c in range(2):
                    f = slice((2 * p + c) * P, (2 * p + c + 1) * P)
                    for j in range(2):
                        eng.matmul(bank[p][:, (2 * c + j) * P:(2 * c + j + 1) * P], G[:, 2 * g + j, f], ident[:, :],
                                   is_transpose=True, start=(c == 0 and j == 0), stop=False, skip_group_check=True)
                for c in range(2):
                    f = slice((2 * p + c) * P, (2 * p + c + 1) * P)
                    to = bank[p][:, 2 * c * P:2 * (c + 1) * P]
                    eng.matmul(to, w1c_hi[:, f], eaT[:, k, :], start=False, stop=False, skip_group_check=True)
                    mm = eng.matmul(to, w1c_lo[:, f], eaT[0:DE, k, :], start=False, stop=True, skip_group_check=True)
                mm.then_inc(s["preA"], 1)

            def second_layer(n, q, scattering=True):
                p, k = q % 2, q // 2
                if p == 0:
                    eng.wait_ge(s["hiA"], n + 2)
                    eng.wait_ge(s["loA"], n + 2)
                need(eng, s["mishB"], n - 1)
                to = bank[2 + p][:, :]
                mm = eng.matmul(to, ones_r[:, :], b2_rows[:, :], start=True, stop=False)
                if scattering:
                    mm.then_inc(s["scattered"], 1)
                for c in range(NT):
                    hi, lo = h_hi[:, k, c, p * P:(p + 1) * P], h_lo[:, k, c, p * P:(p + 1) * P]
                    eng.matmul(to, hi, w2_hi[:, c, :], start=False, stop=False)
                    eng.matmul(to, hi, w2_lo[:, c, :], start=False, stop=False)
                    mm = eng.matmul(to, lo, w2_hi[:, c, :], start=False, stop=(c == NT - 1))
                mm.then_inc(s["preB"], 1)

            def scatter(n, q):
                eng.wait_ge(s["mishB"], n + 1)
                eng.wait_ge(s["hotB"], n + 1)
                first = eng.value_load(win[0:1, bass.ds(2 * n, 1)], min_val=0, max_val=N // WIN - 1)
                end = eng.value_load(win[0:1, bass.ds(2 * n + 1, 1)], min_val=1, max_val=N // WIN)
                with eng.Fori(first, end) as w:
                    for t in range(NT):
                        eng.matmul(bank[4 + t][:, ws(w)], mB[:, q, t * P:(t + 1) * P], oh[:, q, ws(w)],
                                   start=False, stop=False, skip_group_check=True)

            eng.wait_ge(s["ptab_taken"], NT)
            eng.wait_ge(s["qtab_taken"], NT)
            eng.wait_ge(s["w1chi_done"], 1)
            eng.wait_ge(s["w1clo_done"], 1)
            eng.wait_ge(s["w2hi_done"], NT)
            eng.wait_ge(s["w2lo_done"], NT)
            eng.wait_ge(s["b2_done"], 3)
            eng.wait_ge(s["win_row"], 16)
            for t in range(NT):
                clear(bank[4 + t][:, :])
            def node_share(f, k, operand):
                for c in range(NT):
                    mm = eng.matmul(bank[f], slot(k)[:, c, f * P:(f + 1) * P], operand[:, c, :],
                                    start=(k == 3 and c == 0), stop=(k == 4 and c == NT - 1))
                if k == 4:
                    mm.then_inc(s["u_ready"], 1)

            def step(n, q, quad, g, g_use, first=True, scatters=True, second=True):
                if first:
                    first_layer(n, q, quad, g, g_use)
                if scatters:
                    scatter(n - 6, (q - 6) % 4)
                if second:
                    second_layer(n - 3, (q - 3) % 4, scattering=scatters)

            for n in range(8):
                step(n, n % 4, n // 4, n // 2, 0, scatters=n >= 6, second=n >= 3)
            with eng.Fori(1, T // 8) as i:
                for j in range(8):
                    step(8 * i + j, j % 4, 2 * i + j // 4, j // 2, i)
            for n in range(T // 8 * 8, T + 6):
                if n in (T + 1, T + 3):
                    eng.wait_ge(s["w3_in"], 32)
                    eng.wait_ge(s["mishA"], min(n - 2, T))
                    node_share(n // 2 - T // 2, 3, hT)
                step(n, n % 4, n // 4, n % 8 // 2, n // 8, first=n < T, second=n < T + 3)
            for t in range(NT):
                mm = close(bank[4 + t][:, :])
            mm.then_inc(s["agg_ready"], 1)

            eng.wait_ge(s["mishB"], T)
            node_share(2, 3, hT)
            node_share(3, 3, hT)
            eng.wait_ge(s["agg_taken"], NT)
            for f in range(NT):
                node_share(f, 4, mask)
            eng.wait_ge(s["w4_in"], 16)
            eng.wait_ge(s["hb_done"], 3 * NT)
            for t in range(NT):
                eng.matmul(bank[4 + t][:, :], ident[:, :], h[:, t, :], start=True, stop=False)
            order = [(t, c) for t in (0, 1) for c in range(NT - 1)] + [(t, NT - 1) for t in (0, 1)]
            order += [(t, c) for t in range(2, NT) for c in range(NT)]
            for t, c in order:
                if t < 2:
                    eng.wait_ge(s["u_mish"], c + 1)
                mm = eng.matmul(bank[4 + t][:, :], qT[:, c, t * P:(t + 1) * P], slot(2)[:, c, :],
                                start=False, stop=(c == NT - 1))
                if c == NT - 1:
                    mm.then_inc(s["w4_ready"], 1)

            eng.wait_ge(s["l2_in"], 48)
            for t in range(NT + 1):
                if t < NT:
                    transpose_h(3 * NT, t, bank[0:2])
                if t:
                    i = t - 1
                    eng.wait_ge(s["hT_taken"], 3 * NT + i + 1)
                    mm = product(bank[2][:, i * DH:(i + 1) * DH], [hT[:, c, i * P:(i + 1) * P] for c in range(NT)],
                                 [l2w1[:, c, :] for c in range(NT)])
            mm.then_inc(s["t1_ready"], 1)
            eng.wait_ge(s["t1_taken"], NT)
            eng.wait_ge(s["x2_ready"], NT)
            for t in range(NT):
                mm = product(bank[7][:, t * DH:(t + 1) * DH], [CT[:, c, t * P:(t + 1) * P] for c in range(NT)],
                             [t1[:, c, :] for c in range(NT)])
            mm.then_inc(s["a1_ready"], 1)
            eng.wait_ge(s["t2_done"], NT)
            for c in range(NT):
                eng.matmul(bank[3][0:DH, c * P:(c + 1) * P], t2[:, c, :], ident[:, :],
                           start=(c == 0), stop=False, skip_group_check=True)
            for c in range(NT):
                mm = eng.matmul(bank[3][0:DH, :], t2[:, c, :], CT[:, c, :], start=False, stop=(c == NT - 1),
                                skip_group_check=True)
            mm.then_inc(s["a2_ready"], 1)
            eng.wait_ge(s["a2_taken"], 1)
            for t in range(NT):
                if t == 2:
                    eng.wait_ge(s["a1_sum"], NT)
                eng.matmul(bank[4 + t][:, :], a2[:, t * P:(t + 1) * P], l2w2[:, :], start=True, stop=True).then_inc(s["o2_ready"], 1)

            eng.wait_ge(s["lo_done"], 3 * NT + FT + LAYERS * NT + NT)
            eng.wait_ge(s["we_in"], 32 * LAYERS)
            with eng.Fori(0, LAYERS) as l:
                for c in range(NT):
                    eng.wait_ge(s["m_lo"], NT * l + c + 1)
                    for f in range(NT):
                        at = slice(f * P, (f + 1) * P)
                        mm = split_product(bank[f][:, :], (h3_hi[:, c, at], h3_lo[:, c, at]), (CT_hi[:, c, :], CT_lo[:, c, :]),
                                           c == 0, c == NT - 1)
                        if c == NT - 1:
                            mm.then_inc(s["m_agg"], 1)
                for t in range(NT):
                    at = slice(t * P, (t + 1) * P)
                    eng.matmul(bank[4 + t][:, :], EAT[:, at], we_flat[:, bass.ds(l * D, D)], start=True, stop=False)
                    for c in range(NT):
                        if t == 0:
                            eng.wait_ge(s["m_tlo"], NT * l + c + 1)
                        w = bass.ds(l * (NT * D) + c * D, D)
                        mm = split_product(bank[4 + t][:, :], (hT_hi[:, c, at], hT_lo[:, c, at]), (wx_hi[:, w], wx_lo[:, w]),
                                           False, c == NT - 1)
                    mm.then_inc(s["m_msg"], 1)

        @block.vector
        def _(eng):
            eng.wait_ge(s["idx_in"], 32)
            eng.tensor_copy(idx_f[:, :, :], idx_i[:, :, :]).then_inc(s["idx_float"], 1)
            eng.wait_ge(s["idx_float"], 1)
            eng.tensor_reduce(win_f[:, 0:1], idx_f[:, 0, :], AX.X, ALU.min).then_inc(s["win_range"], 1)
            eng.tensor_reduce(win_f[:, 1:2], idx_f[:, 0, :], AX.X, ALU.max).then_inc(s["win_range"], 1)
            eng.wait_ge(s["win_range"], 2)
            eng.tensor_scalar(win_f[:, 1:2], win_f[:, 1:2], float(WIN), None, ALU.add).then_inc(s["win_range"], 1)
            eng.wait_ge(s["win_range"], 3)
            eng.tensor_copy(win_v[:, :], win_f[:, :]).then_inc(s["win_range"], 1)
            eng.wait_ge(s["win_range"], 4)
            eng.tensor_scalar(win_i[:, :], win_v[:, :], SHIFT, None, ALU.arith_shift_right).then_inc(s["win_shift"], 1)

            def statistics(k, src, t, later=0):
                eng.bn_stats(bn_st[:, k, t, :], src[:, t, :]).then_inc(s["ln_stats"], 1)
                eng.wait_ge(s["ln_stats"], later + nth(k, t))
                eng.nop(nofuse=True)
                eng.bn_aggr(bn_mv[:, k, t, :], bn_st[:, k, t, :]).then_inc(s["ln_mv"], 1)

            def shift(k, t):
                eng.wait_ge(s["ln_rstd"], nth(k, t))
                eng.wait_ge(s["ln_mv"], nth(k, t))
                eng.scalar_tensor_tensor(nbias[:, k, t:t + 1], bn_mv[:, k, t, 0:1], -1.0, rstd[:, k, t:t + 1],
                                         ALU.mult, ALU.mult).then_inc(s["ln_nb"], 1)

            eng.wait_ge(s["idx_T"], 1)
            for to, lo in ((dst_f, 0), (src_f, P), (dst_i, 0), (src_i, P)):
                eng.tensor_copy(to[:, :], bank[6][:, lo:lo + T]).then_inc(s["idx_taken"], 1)
            eng.wait_ge(s["consts"], 7)
            eng.wait_ge(s["idx_taken"], 4)

            def count(n, q):
                need(eng, s["counted"], n - 3)
                eng.tensor_scalar(oh_src[:, q, :], iota_n[:, :], src_f[:, bass.ds(n, 1)], None, ALU.is_equal
                                  ).then_inc(s["src_hot"], 1)
                eng.tensor_scalar(oh_cnt[:, q, :], iota_n[:, :], dst_f[:, bass.ds(n, 1)], None, ALU.is_equal
                                  ).then_inc(s["dst_hot"], 1)
                eng.wait_ge(s["ea_hi"], n + 1)
                eng.tensor_tensor(e_split[:, q, DE:2 * DE], e_raw[:, bass.ds(n, 1), :].rearrange("p a d -> p (a d)"), e_split[:, q, 0:DE].bitcast(f32),
                                  ALU.subtract).then_inc(s["ea_lo"], 1)

            for q in range(4):
                count(q, q)
            for a, b in EA_PARTS[1:]:
                with eng.Fori(a, b) as i:
                    for q in range(4):
                        count(4 * i + q, q)
                for t in range(NT):
                    if a == 1:
                        eng.wait_ge(s["x_in"], 16)
                        statistics(LN_IN0, xres, t)
                    if a == 5:
                        shift(LN_IN0, t)

            def low_hT(t):
                at = slice(t * P, (t + 1) * P)
                eng.wait_ge(s["hT_taken"], t + 1)
                eng.tensor_tensor(hT0_lo[:, :, at], bank[6 + t % 2].rearrange("p (c n) -> p c n", n=P),
                                  hT_hi[:, :, at].bitcast(f32), ALU.subtract).then_inc(s["hT_low"], 1)

            for t in range(NT):
                low_hT(t)

            eng.wait_ge(s["bcol_in"], 64)
            eng.wait_ge(s["rows_in"], 16 * 7)
            def take(n):
                eng.wait_ge(s["qkv_ready"], n + 1)
                t, got = n % NT, bank[6 + n % 2]
                if n < NT:
                    eng.tensor_scalar(qT[:, t, :], got, bcol[:, t:t + 1], HD ** -0.5, ALU.add, ALU.mult).then_inc(s["qkv_taken"], 1)
                elif n < 2 * NT:
                    eng.tensor_scalar(kT[:, t, :], got, bcol[:, NT + t:NT + t + 1], None, ALU.add).then_inc(s["qkv_taken"], 1)
                else:
                    eng.tensor_tensor(v[:, t, :], got, brow[:, BV, :], ALU.add).then_inc(s["qkv_taken"], 1)

            eng.wait_ge(s["ea_out"], 16 * len(EAT_PARTS))
            for n in range(NT):
                take(n)
            for t in range(NT):
                eng.wait_ge(s["cT_ready"], t + 1)
                eng.tensor_scalar(mask[:, t, :], bank[t][:, :], 1.0, None, ALU.min).then_inc(s["mask_ready"], 1)
                eng.tensor_reduce(deg[:, t:t + 1], bank[t][:, :], AX.X, ALU.add).then_inc(s["deg_ready"], 1)
            for n in range(NT, 2 * NT):
                take(n)

            def weights(u):
                half, m, k = u // NT, u % NT, u % 2
                eng.wait_ge(s["s_rec"], u + 1)
                eng.tensor_tensor(ssm[:, k, :], ssm[:, k, :], mask[:, m, half * HALF:(half + 1) * HALF], ALU.mult
                                  ).then_inc(s["s_masked"], 1)
                eng.wait_ge(s["s_masked"], u + 1)
                eng.tensor_tensor(S3[u % 3][:, 0:SHARE, :], S3[u % 3][:, 0:SHARE, :],
                                  ssm[:, k, :].unsqueeze(1).to_broadcast([P, SHARE, HALF]), ALU.mult).then_inc(s["att_ready"], 1)

            raw = banks[:, 0:4, :].rearrange("p b (i n) -> p (b i) n", n=HALF)
            eng.wait_ge(s["mask_ready"], NT)

            def differences(u):
                eng.wait_ge(s["s_ready"], u + 1)
                need(eng, s["s_sub"], 2 * u)
                eng.tensor_reduce(smx[:, :], raw.rearrange("p h n -> p n h"), AX.X, ALU.max).then_inc(s["s_max"], 1)
                eng.wait_ge(s["s_max"], u + 1)
                need(eng, s["av_done"], u - 2)
                for part in range(2):
                    at = slice(part * HEADS // 2, (part + 1) * HEADS // 2)
                    eng.tensor_tensor(S3[u % 3][:, at, :], raw[:, at, :], smx[:, :].unsqueeze(1)
                                      .to_broadcast([P, HEADS // 2, HALF]), ALU.subtract).then_inc(s["s_sub"], 1)

            def sum_heads(u):
                eng.wait_ge(s["s_exp"], u + 1)
                need(eng, s["att_ready"], u - 1)
                need(eng, s["att_rest"], u - 1)
                eng.tensor_reduce(ssm[:, u % 2, :], S3[u % 3].rearrange("p h n -> p n h"), AX.X, ALU.add).then_inc(s["s_sum"], 1)

            for u in range(2 * NT):
                differences(u)
                if u < 2:
                    take(2 * NT + 2 * u)
                    take(2 * NT + 2 * u + 1)
                if u == 1:
                    for t in range(NT):
                        eng.tensor_scalar(unmask[:, t, :], mask[:, t, :], 1.0, -1.0 / HEADS, ALU.subtract, ALU.mult
                                          ).then_inc(s["unmask_ready"], 1)
                if u:
                    weights(u - 1)
                sum_heads(u)
            weights(2 * NT - 1)

            def plus_row(k):
                for t in range(NT):
                    eng.tensor_tensor(h[:, t, :], h[:, t, :], brow[:, k, :], ALU.add).then_inc(s["hb_done"], 1)

            def plus_be2():
                for t in range(NT):
                    eng.tensor_tensor(xres[:, t, :], xres[:, t, :], brow[:, BE2, :], ALU.add).then_inc(s["xb_done"], 1)

            def end_block(k, after, before, gain, summed, src, done):
                d = APART[k]
                for t in range(NT + 2 * d):
                    if t < NT:
                        summed(t)
                        statistics(k, src, t)
                    if d <= t < NT + d:
                        i = t - d
                        eng.wait_ge(s["xb_done"], NT * (before - 1) + i + 1)
                        affine(k, i, before, brow[:, gain, :], xres[:, i, :], xres, src=src).then_inc(done, 1)
                        eng.wait_ge(done, i + 1)
                        statistics(after, xres, i)
                    if t >= 2 * d:
                        shift(after, t - 2 * d)

            eng.wait_ge(s["hT_ready"], NT)
            plus_row(BO)
            eng.wait_ge(s["hb_done"], NT)
            def affine(k, t, before, gain, plus, to, later=0, src=y):
                eng.wait_ge(s["ln_mv"], later + nth(k, t))
                eng.scalar_tensor_tensor(y[:, t, :], src[:, t, :], bn_mv[:, k, t, 0:1], gain,
                                         ALU.subtract, ALU.mult).then_inc(s["y_scaled"], 1)
                eng.wait_ge(s["y_scaled"], later + (NT * before + t + 1))
                eng.wait_ge(s["ln_rstd"], later + nth(k, t))
                return eng.scalar_tensor_tensor(to[:, t, :], y[:, t, :], rstd[:, k, t:t + 1], plus, ALU.mult, ALU.add)

            for t in range(NT + 1):
                if t < NT:
                    eng.wait_ge(s["wo_ready"], t + 1)
                    eng.tensor_tensor(y[:, t, :], bank[t][:, :], h[:, t, :], ALU.add).then_inc(s["y1_ready"], 1)
                    eng.wait_ge(s["y1_ready"], t + 1)
                    statistics(LN_A, y, t)
                if t:
                    affine(LN_A, t - 1, 0, brow[:, G1, :], brow[:, BE1, :], h).then_inc(s["h_ready"], 1)
            plus_be2()
            eng.wait_ge(s["hT_ready"], 2 * NT)
            eng.wait_ge(s["h_ready"], 2 * NT)
            plus_row(B2)

            for f in range(FT):
                eng.wait_ge(s["ff_hi"], f + 1)
                eng.tensor_tensor(ff_lo[:, f, :], ff_now[:, f % 2, :], ff_hi[:, f, :].bitcast(f32), ALU.subtract
                                  ).then_inc(s["ff_lo"], 1)
                if f < NT:
                    eng.wait_ge(s["w2hi_done"], f + 1)
                    eng.tensor_tensor(w2_lo[:, f, :], slot(2)[:, f, :], w2_hi[:, f, :].bitcast(f32), ALU.subtract
                                      ).then_inc(s["w2lo_done"], 1)
            eng.wait_ge(s["w1chi_done"], 1)
            eng.tensor_tensor(w1c_lo[:, :], w1c_raw[0:DE, :], w1c_hi[0:DE, :].bitcast(f32), ALU.subtract).then_inc(s["w1clo_done"], 1)
            eng.wait_ge(s["b2_in"], 32)
            eng.tensor_copy(b2_rows[0:1, :], b2_raw[0:1, :]).then_inc(s["b2_done"], 1)
            eng.tensor_copy(b2_rows[32:33, :], b2_raw[32:33, :]).then_inc(s["b2_done"], 1)
            eng.wait_ge(s["b2_done"], 2)
            eng.tensor_tensor(b2_rows[32:33, :], b2_raw[32:33, :], b2_rows[32:33, :].bitcast(f32), ALU.subtract).then_inc(s["b2_done"], 1)

            def sum_ff(t):
                eng.wait_ge(s["ff2_ready"], t + 1)
                eng.tensor_tensor(y[:, t, :], bank[4 + t], h[:, t, :], ALU.add).then_inc(s["y2_ready"], 1)
                eng.wait_ge(s["y2_ready"], t + 1)

            eng.wait_ge(s["hb_done"], 2 * NT)
            end_block(LN_B, LN_IN1, 1, G2, sum_ff, y, s["x1_ready"])
            eng.wait_ge(s["rows1_in"], 16 * 5)
            for t in range(NT):
                eng.wait_ge(s["tab_ready"], t + 1)
                eng.tensor_tensor(y[:, t, :], bank[4 + t][:, :], brow[:, B1, :], ALU.add).then_inc(s["ptab_taken"], 1)
            for t in range(NT):
                eng.wait_ge(s["h_ready"], 2 * NT + t + 1)
                eng.tensor_tensor(xres[:, t, :], xres[:, t, :], brow[:, BETA, :], ALU.add).then_inc(s["xb_done"], 1)
            eng.wait_ge(s["hT_ready"], 3 * NT)
            plus_row(B4)

            def step(n, q, first=True, split=True, second=True, finish=True):
                p = q % 2
                if first:
                    eng.wait_ge(s["expA"], n + 1)
                    eng.tensor_scalar(eA[:, p, :], eA[:, p, :], TOP, None, ALU.min).then_inc(s["topA"], 1)
                    eng.wait_ge(s["topA"], n + 1)
                    need(eng, s["mishA"], n - 1)
                    eng.scalar_tensor_tensor(uA[:, p, :], eA[:, p, :], 2.0, eA[:, p, :], ALU.add, ALU.mult).then_inc(s["sqA"], 1)
                if finish:
                    eng.wait_ge(s["recB"], n - 3)
                    need(eng, s["scattered"], n - 7)
                    eng.scalar_tensor_tensor(mB[:, q, :], uB[:, p, :], 1.0, bank[2 + p][:, :], ALU.subtract, ALU.mult,
                                             reverse0=True).then_inc(s["mishB"], 1)
                    eng.tensor_scalar(oh[:, q, :], iota_n[:, :], dst_f[:, bass.ds(n - 4, 1)], None, ALU.is_equal
                                      ).then_inc(s["hotB"], 1)
                if split:
                    m, k = (q - 1) % 2, (q - 1) % 4 // 2
                    eng.wait_ge(s["hiA"], n)
                    eng.wait_ge(s["mishA"], n)
                    need(eng, s["preB"], n - 3 - m)
                    eng.tensor_tensor(h_lo[:, k, 2 * m:2 * m + 2, :], mA[:, m, :].rearrange("p (c e) -> p c e", c=2),
                                      h_hi[:, k, 2 * m:2 * m + 2, :].bitcast(f32), ALU.subtract).then_inc(s["loA"], 1)
                if first:
                    eng.wait_ge(s["recA"], n + 1)
                    need(eng, s["hiA"], n - 1)
                    need(eng, s["loA"], n - 1)
                    eng.scalar_tensor_tensor(mA[:, p, :], uA[:, p, :], 1.0, bank[p][:, :], ALU.subtract, ALU.mult,
                                             reverse0=True).then_inc(s["mishA"], 1)
                if second:
                    eng.wait_ge(s["expB"], n - 2)
                    eng.tensor_scalar(eB[:, 1 - p, :], eB[:, 1 - p, :], TOP, None, ALU.min).then_inc(s["topB"], 1)
                    eng.wait_ge(s["topB"], n - 2)
                    need(eng, s["mishB"], n - 4)
                    eng.scalar_tensor_tensor(uB[:, 1 - p, :], eB[:, 1 - p, :], 2.0, eB[:, 1 - p, :], ALU.add, ALU.mult).then_inc(s["sqB"], 1)

            for n in range(8):
                step(n, n % 4, split=n >= 1, second=n >= 3, finish=n >= 4)
            with eng.Fori(2, QUADS) as i:
                for q in range(4):
                    step(4 * i + q, q)
            for n in range(T, T + 4):
                step(n, n % 4, first=False, split=n == T, second=n < T + 3)

            def finish_u(f):
                eng.wait_ge(s["u_rec"], f + 1)
                eng.wait_ge(s["u_x"], f + 1)
                eng.scalar_tensor_tensor(qT[:, f, :], v[:, f, :], 1.0, kT[:, f, :], ALU.subtract, ALU.mult,
                                         reverse0=True).then_inc(s["u_mish"], 1)

            for f in range(NT):
                eng.wait_ge(s["u_ready"], f + 1)
                eng.tensor_scalar(kT[:, f, :], bank[f][:, :], bcol[:, 16 + f:17 + f], None, ALU.add).then_inc(s["u_x"], 1)
                eng.wait_ge(s["u_x"], f + 1)
                eng.tensor_scalar(v[:, f, :], kT[:, f, :], TOP_X, None, ALU.min).then_inc(s["u_top"], 1)
                eng.wait_ge(s["u_exp"], f + 1)
                eng.scalar_tensor_tensor(v[:, f, :], v[:, f, :], 2.0, v[:, f, :], ALU.add, ALU.mult).then_inc(s["u_sq"], 1)
                if f:
                    finish_u(f - 1)
            finish_u(NT - 1)
            end_block(LN_C, LN_IN2, 2, GAMMA, lambda t: eng.wait_ge(s["w4_ready"], t + 1), banks[:, 4:8, :], s["x2_ready"])

            for t in range(NT):
                eng.wait_ge(s["h_ready"], 3 * NT + t + 1)
                eng.tensor_tensor(xres[:, t, :], xres[:, t, :], brow[:, L2B2, :], ALU.add).then_inc(s["xb_done"], 1)
            eng.wait_ge(s["l2_in"], 48)
            eng.wait_ge(s["dinv_ready"], 1)
            eng.wait_ge(s["t1_ready"], 1)
            for t in range(NT):
                eng.tensor_scalar(t1[:, t, :], bank[2][:, t * DH:(t + 1) * DH], dinv[:, t:t + 1], None, ALU.mult).then_inc(s["t1_taken"], 1)
            eng.wait_ge(s["t1_taken"], NT)
            eng.wait_ge(s["a1_ready"], 1)
            for t in range(NT):
                eng.tensor_tensor(t2[:, t, :], bank[7][:, t * DH:(t + 1) * DH], t1[:, t, :], ALU.add).then_inc(s["a1_sum"], 1)
            for t in range(NT):
                eng.wait_ge(s["a1_sum"], t + 1)
                eng.scalar_tensor_tensor(t2[:, t, :], t2[:, t, :], dinv[:, t:t + 1], l2b1[:, :], ALU.mult, ALU.add).then_inc(s["a1_bias"], 1)
            for t in range(NT):
                eng.wait_ge(s["a1_bias"], t + 1)
                eng.tensor_scalar(t2[:, t, :], t2[:, t, :], 0.0, dinv[:, t:t + 1], ALU.max, ALU.mult).then_inc(s["t2_done"], 1)
            for t in range(NT + 1):
                if t < NT:
                    eng.wait_ge(s["o2_ready"], t + 1)
                    eng.wait_ge(s["xb_done"], 2 * NT + t + 1)
                    eng.scalar_tensor_tensor(xres[:, t, :], bank[4 + t][:, :], dinv[:, t:t + 1], xres[:, t, :],
                                             ALU.mult, ALU.add).then_inc(s["x3_ready"], 1)
                    eng.wait_ge(s["x3_ready"], t + 1)
                    statistics(LN_IN3, xres, t)
                if t:
                    shift(LN_IN3, t - 1)

            eng.wait_ge(s["affine_in"], 32 * LAYERS)
            with eng.Fori(0, LAYERS) as l:
                for f in range(NT):
                    eng.wait_ge(s["m_taken"], NT * l + f + 1)
                    eng.tensor_tensor(hT_lo[:, f, :], bank[f][:, :], hT_hi[:, f, :].bitcast(f32), ALU.subtract
                                      ).then_inc(s["m_tlo"], 1)
                for t in range(NT + 1):
                    if t < NT:
                        eng.wait_ge(s["m_h"], NT * l + t + 1)
                        eng.wait_ge(s["m_msg"], NT * l + t + 1)
                        eng.tensor_tensor(y[:, t, :], bank[4 + t][:, :], h[:, t, :], ALU.add).then_inc(s["m_y"], 1)
                        eng.wait_ge(s["m_y"], NT * l + t + 1)
                        statistics(LN_L3, y, t, NT * l)
                    if t:
                        affine(LN_L3, t - 1, 3, WA[:, 0, bass.ds(l * D, D)], WA[:, 1, bass.ds(l * D, D)], y,
                               NT * l).then_inc(s["m_shifted"], 1)
            for t in range(NT):
                eng.wait_ge(s["m_h"], NT * LAYERS + t + 1)
                eng.tensor_tensor(y[:, t, :], xres[:, t, :], h[:, t, :], ALU.add).then_inc(s["result"], 1)


_INS = """x src dst edge_attr_64 L0_gnn_Wq L0_gnn_bq L0_gnn_Wk L0_gnn_bk L0_gnn_Wv L0_gnn_bv L0_gnn_Wo L0_gnn_bo
L0_gnn_W1 L0_gnn_b1 L0_gnn_W2 L0_gnn_b2 L0_gnn_g1 L0_gnn_be1 L0_gnn_g2 L0_gnn_be2
L1_gnn_W1 L1_gnn_b1 L1_gnn_W2 L1_gnn_b2 L1_gnn_W3 L1_gnn_b3 L1_gnn_W4 L1_gnn_b4 L1_gnn_gamma L1_gnn_beta
L2_gnn_W1 L2_gnn_b1 L2_gnn_W2 L2_gnn_b2 L3_gnn_Ws L3_gnn_bs L3_gnn_gammas L3_gnn_betas""".split()


def kernel(**inputs):
    import numpy as np
    import concourse.bacc as bacc
    from concourse.bass_utils import run_bass_kernel_spmd

    nc = bacc.Bacc("TRN2", target_bir_lowering=False, num_devices=1)
    arrays, ins = {}, {}
    for name in _INS:
        a = np.ascontiguousarray(inputs[name])
        arrays[f"in_{name}"] = a
        ins[name] = nc.dram_tensor(f"in_{name}", a.shape, mybir.dt.from_np(a.dtype), kind="ExternalInput").ap()
    out = nc.dram_tensor("out_x", inputs["x"].shape, mybir.dt.float32, kind="ExternalOutput").ap()
    gnn_stack_kernel(nc, ins, out)
    return run_bass_kernel_spmd(nc, [arrays], core_ids=[0]).results[0]["out_x"]
```
